# Optimizing a Trainium2 kernel written in Bass

```python
import numpy as np
import jax
import jax.numpy as jnp

def _softmax(x, axis=-1):
    return jax.nn.softmax(x, axis=axis)

def _gelu(x):
    return jax.nn.gelu(x, approximate=True)

def _silu(x):
    return jax.nn.silu(x)

def _sigmoid(x):
    return jax.nn.sigmoid(x)

def _layernorm(x, axis=-1, eps=1e-05):
    m = jnp.mean(x, axis=axis, keepdims=True)
    v = jnp.var(x, axis=axis, keepdims=True)
    return (x - m) / jnp.sqrt(v + eps)

def _scatter_add(tgt, idx, src, axis=0):
    return tgt.at[idx].add(src)

def _segment_sum(src, seg, n):
    return jax.ops.segment_sum(src, seg, n)
kernel_name = 'mk_xattn_ffn_d4_seqx_r8_6a3fd1'

def setup_inputs(seed: int=0):
    np.random.seed(seed)
    _w = jnp.asarray

    def _rec_inputs():
        import jax
        import jax.numpy as jnp
        _rk = jax.random.key(seed)
        x = 0.0002417 + 0.9998 * jax.random.normal(jax.random.fold_in(_rk, 1), (32, 128, 128), jnp.float32)
        _lenS = 128 - jax.random.randint(jax.random.fold_in(_rk, 7), (32,), 0, max(1, 128 // 4) + 1, jnp.int32)
        _lenS2 = 120 - jax.random.randint(jax.random.fold_in(_rk, 8), (32,), 0, max(1, 120 // 4) + 1, jnp.int32)
        _ctx_1024P = jax.random.normal(jax.random.fold_in(_rk, 11), (32, 16, 128), jnp.float32)
        _ctx_1024c = jax.random.dirichlet(jax.random.fold_in(_rk, 511), 0.3 * jnp.ones((16,), jnp.float32), (32, 120))
        _ctx_1024t = jnp.einsum('bsk,bkd->bsd', _ctx_1024c, _ctx_1024P)
        _ctx_1024t = _ctx_1024t * jax.lax.rsqrt(jnp.mean(jnp.square(_ctx_1024t)) + 1e-12) * 0.953939
        ctx_1024 = 7.22013e-05 + 1.00017 * (_ctx_1024t + 0.3 * jax.random.normal(jax.random.fold_in(_rk, 611), (32, 120, 128), jnp.float32))
        _validS = jnp.arange(128)[None, :] < _lenS[:, None]
        _validS2 = jnp.arange(120)[None, :] < _lenS2[:, None]
        _causal = jnp.tril(jnp.ones((128, 128), dtype=bool))
        mask_BxSxS2_ff1 = jnp.where(jnp.ones((32, 128, 120), dtype=bool), 1.0, 0.0).astype(jnp.float32)
        mask_BxS2_ff1 = jnp.where(jnp.ones((32, 120), dtype=bool), 1.0, 0.0).astype(jnp.float32)
        mask_BxS2_ik0 = jnp.where(jnp.broadcast_to(_validS2[:, :], (32, 120)), 0, 1).astype(jnp.int32)
        mask_Bx1xSxS2_bk1 = jnp.broadcast_to(_validS2[:, None, None, :], (32, 1, 128, 120))
        return (x, ctx_1024, mask_BxSxS2_ff1, mask_BxS2_ff1, mask_BxS2_ik0, mask_Bx1xSxS2_bk1)
    x, ctx_1024, mask_BxSxS2_ff1, mask_BxS2_ff1, mask_BxS2_ik0, mask_Bx1xSxS2_bk1 = _rec_inputs()

    def _L0_xattn_setup():
        import jax, jax.numpy as jnp
        import numpy as np
        D_MODEL = 128
        B, S = (4, 256)
        key = jax.random.key(seed)
        ks = jax.random.split(key, 10)
        s = 1.0 / np.sqrt(D_MODEL)
        return {'k': jax.random.normal(ks[0], (B, S, D_MODEL), jnp.float32), 'v': jax.random.normal(ks[1], (B, S, D_MODEL), jnp.float32), 'q': jax.random.normal(ks[2], (B, S, D_MODEL), jnp.float32), 'Wk': jax.random.normal(ks[3], (D_MODEL, D_MODEL), jnp.float32) * s, 'Wv': jax.random.normal(ks[4], (D_MODEL, D_MODEL), jnp.float32) * s, 'bv': jnp.zeros((D_MODEL,), jnp.float32), 'Wq': jax.random.normal(ks[5], (D_MODEL, D_MODEL), jnp.float32) * s, 'bq': jnp.zeros((D_MODEL,), jnp.float32), 'Wo': jax.random.normal(ks[6], (D_MODEL, D_MODEL), jnp.float32) * s, 'bo': jnp.zeros((D_MODEL,), jnp.float32)}
    _L0_xattn_all = _L0_xattn_setup()
    _L0_xattn_in = {k: v for k, v in _L0_xattn_all.items() if k in ('Wk', 'Wv', 'bv', 'Wq', 'bq', 'Wo', 'bo')}
    del _L0_xattn_all

    def _L0_ffn_setup():
        import jax, jax.numpy as jnp
        import numpy as np
        B, S, H = (2, 128, 128)
        E, F = (8, 512)
        GATE_TEMP = 0.1
        key = jax.random.key(seed)
        ks = jax.random.split(key, 6)
        s_h = 1.0 / np.sqrt(H)
        s_f = 1.0 / np.sqrt(F)
        return {'hidden_states': jax.random.normal(ks[0], (B, S, H), dtype=jnp.float32), 'w_router': jax.random.normal(ks[1], (H, E), dtype=jnp.float32) * s_h, 'w_gating': jax.random.normal(ks[2], (H, E), dtype=jnp.float32) * s_h, 'w_gate': jax.random.normal(ks[3], (E, H, F), dtype=jnp.float32) * s_h, 'w_up': jax.random.normal(ks[4], (E, H, F), dtype=jnp.float32) * s_h, 'w_down': jax.random.normal(ks[5], (E, F, H), dtype=jnp.float32) * s_f}
    _L0_ffn_all = _L0_ffn_setup()
    _L0_ffn_in = {k: v for k, v in _L0_ffn_all.items() if k in ('w_router', 'w_gating', 'w_gate', 'w_up', 'w_down')}
    del _L0_ffn_all

    def _L1_xattn_setup():
        import jax, jax.numpy as jnp
        import numpy as np
        key = jax.random.key(seed)
        ks = jax.random.split(key, 5)
        B, S, D = (8, 256, 128)
        return {'query': jax.random.normal(ks[0], (B, S, D), dtype=jnp.float32), 'key': jax.random.normal(ks[1], (B, S, D), dtype=jnp.float32), 'value': jax.random.normal(ks[2], (B, S, D), dtype=jnp.float32), 'cell_mask': jnp.ones((B, S, S), dtype=jnp.float32), 'seq_mask': jnp.ones((B, S), dtype=jnp.float32), 'W_k': jax.random.normal(ks[3], (D, D), dtype=jnp.float32) * (1.0 / np.sqrt(D)), 'b_k': jnp.zeros((D,), dtype=jnp.float32), 'W_o': jax.random.normal(ks[4], (D, D), dtype=jnp.float32) * (1.0 / np.sqrt(D)), 'b_o': jnp.zeros((D,), dtype=jnp.float32)}
    _L1_xattn_all = _L1_xattn_setup()
    _L1_xattn_in = {k: v for k, v in _L1_xattn_all.items() if k in ('W_k', 'b_k', 'W_o', 'b_o')}
    del _L1_xattn_all

    def _L1_ffn_setup():
        import jax, jax.numpy as jnp
        import numpy as np
        BLOCK = 32
        W_BITS = 4
        ACT_BITS = 16

        def act_qdq(x):
            qmax = 2.0 ** (ACT_BITS - 1) - 1.0
            scale = jnp.maximum(jnp.max(jnp.abs(x)) / qmax, 1e-12)
            return jnp.clip(jnp.round(x / scale), -qmax - 1.0, qmax) * scale

        def fixed_qdq_u16(x):
            scale = 1.0 / 65536.0
            return jnp.clip(jnp.round(x / scale), 0.0, 65535.0) * scale

        def lpbq_dequant(w):
            O, I = w.shape
            qmax = 2.0 ** (W_BITS - 1) - 1.0
            wb = w.reshape(O, I // BLOCK, BLOCK)
            s = jnp.maximum(jnp.max(jnp.abs(wb), axis=-1, keepdims=True) / qmax, 1e-12)
            wq = jnp.clip(jnp.round(wb / s), -qmax - 1.0, qmax) * s
            return wq.reshape(O, I)
        key = jax.random.key(seed)
        k1, k2, k3, k4 = jax.random.split(key, 4)
        B, S, H, I = (2, 512, 128, 384)
        x = jax.random.normal(k1, (B, S, H), jnp.float32)
        w_gate = jax.random.normal(k2, (I, H), jnp.float32) * 0.02
        w_up = jax.random.normal(k3, (I, H), jnp.float32) * 0.02
        w_down = jax.random.normal(k4, (H, I), jnp.float32) * 0.02
        return {'x': x, 'w_gate': w_gate, 'w_up': w_up, 'w_down': w_down}
    _L1_ffn_all = _L1_ffn_setup()
    _L1_ffn_in = {k: v for k, v in _L1_ffn_all.items() if k in ('w_gate', 'w_up', 'w_down')}
    del _L1_ffn_all

    def _L2_xattn_setup():
        import jax, jax.numpy as jnp
        import numpy as np
        import math
        D_MODEL = 128
        N_HEADS = 16
        D_K = D_MODEL // N_HEADS
        key = jax.random.key(seed)
        ks = jax.random.split(key, 12)
        B, SQ, SK = (4, 128, 256)
        s = 1.0 / math.sqrt(D_MODEL)
        inp = {'query': jax.random.normal(ks[0], (B, SQ, D_MODEL), jnp.float32), 'key_value': jax.random.normal(ks[1], (B, SK, D_MODEL), jnp.float32), 'mask': jax.random.randint(ks[2], (B, SK), 0, 2, jnp.int32), 'Wq': jax.random.normal(ks[3], (D_MODEL, D_MODEL), jnp.float32) * s, 'bq': jnp.zeros((D_MODEL,), jnp.float32), 'Wk': jax.random.normal(ks[4], (D_MODEL, D_MODEL), jnp.float32) * s, 'bk': jnp.zeros((D_MODEL,), jnp.float32), 'Wv': jax.random.normal(ks[5], (D_MODEL, D_MODEL), jnp.float32) * s, 'bv': jnp.zeros((D_MODEL,), jnp.float32), 'Wo': jax.random.normal(ks[6], (D_MODEL, D_MODEL), jnp.float32) * s, 'bo': jnp.zeros((D_MODEL,), jnp.float32)}
        return inp
    _L2_xattn_all = _L2_xattn_setup()
    _L2_xattn_in = {k: v for k, v in _L2_xattn_all.items() if k in ('Wq', 'bq', 'Wk', 'bk', 'Wv', 'bv', 'Wo', 'bo')}
    del _L2_xattn_all

    def _L2_ffn_setup():
        import jax, jax.numpy as jnp
        import numpy as np
        from jax import lax
        N_HEADS = 16
        TOP_K = 2
        N_EXPERTS = 8

        def layer_norm(x, w, b, eps=1e-05):
            mu = jnp.mean(x, axis=-1, keepdims=True)
            var = jnp.mean(jnp.square(x - mu), axis=-1, keepdims=True)
            return (x - mu) * lax.rsqrt(var + eps) * w + b

        def attention(x, w_qkv, b_qkv, w_o, b_o):
            B, T, D = x.shape
            dh = D // N_HEADS
            qkv = x @ w_qkv + b_qkv
            q, k, v = jnp.split(qkv, 3, axis=-1)
            q = q.reshape(B, T, N_HEADS, dh)
            k = k.reshape(B, T, N_HEADS, dh)
            v = v.reshape(B, T, N_HEADS, dh)
            scores = jnp.einsum('bqhd,bkhd->bhqk', q, k) / jnp.sqrt(jnp.float32(dh)).astype(x.dtype)
            probs = jax.nn.softmax(scores, axis=-1)
            ctx = jnp.einsum('bhqk,bkhd->bqhd', probs, v).reshape(B, T, D)
            return ctx @ w_o + b_o

        def moe_ff(x, w_gate, w1, b1, w2, b2):
            B, T, D = x.shape
            t = x.reshape(B * T, D)
            probs = jax.nn.softmax(t @ w_gate, axis=-1)
            tw, ti = lax.top_k(probs, TOP_K)
            tw = tw / jnp.sum(tw, axis=-1, keepdims=True)
            out = jnp.zeros_like(t)
            for e in range(N_EXPERTS):
                we = jnp.sum(jnp.where(ti == e, tw, 0.0), axis=-1)
                h = jax.nn.gelu(t @ w1[e] + b1[e]) @ w2[e] + b2[e]
                out = out + we[:, None] * h
            return out.reshape(B, T, D)
        key = jax.random.key(seed)
        ks = jax.random.split(key, 8)
        B, T, D, H, E = (4, 64, 128, 512, 8)
        s = lambda d: 1.0 / np.sqrt(d)
        return {'x': jax.random.normal(ks[0], (B, T, D), jnp.float32), 'ln1_w': jnp.ones((D,), jnp.float32), 'ln1_b': jnp.zeros((D,), jnp.float32), 'ln2_w': jnp.ones((D,), jnp.float32), 'ln2_b': jnp.zeros((D,), jnp.float32), 'w_qkv': jax.random.normal(ks[1], (D, 3 * D), jnp.float32) * s(D), 'b_qkv': jnp.zeros((3 * D,), jnp.float32), 'w_o': jax.random.normal(ks[2], (D, D), jnp.float32) * s(D), 'b_o': jnp.zeros((D,), jnp.float32), 'w_gate': jax.random.normal(ks[3], (D, E), jnp.float32) * s(D), 'w1': jax.random.normal(ks[4], (E, D, H), jnp.float32) * s(D), 'b1': jnp.zeros((E, H), jnp.float32), 'w2': jax.random.normal(ks[5], (E, H, D), jnp.float32) * s(H), 'b2': jnp.zeros((E, D), jnp.float32)}
    _L2_ffn_all = _L2_ffn_setup()
    _L2_ffn_in = {k: v for k, v in _L2_ffn_all.items() if k in ('ln1_w', 'ln1_b', 'ln2_w', 'ln2_b', 'w_qkv', 'b_qkv', 'w_o', 'b_o', 'w_gate', 'w1', 'b1', 'w2', 'b2')}
    del _L2_ffn_all

    def _L3_xattn_setup():
        import jax, jax.numpy as jnp
        import numpy as np
        D_MODEL = 128
        HEAD_NUM = 16
        key = jax.random.key(seed)
        ks = jax.random.split(key, 12)
        B, S, D = (2, 256, D_MODEL)
        std = 0.02
        inp = {'q': jax.random.normal(ks[0], (B, S, D), dtype=jnp.float32), 'k': jax.random.normal(ks[1], (B, S, D), dtype=jnp.float32), 'v': jax.random.normal(ks[2], (B, S, D), dtype=jnp.float32), 'mask': jax.random.randint(ks[3], (B, 1, S, S), 0, 2).astype(bool), 'wq_w': jax.random.normal(ks[4], (D, D), dtype=jnp.float32) * std, 'wq_b': jnp.zeros((D,), dtype=jnp.float32), 'wk_w': jax.random.normal(ks[5], (D, D), dtype=jnp.float32) * std, 'wk_b': jnp.zeros((D,), dtype=jnp.float32), 'wv_w': jax.random.normal(ks[6], (D, D), dtype=jnp.float32) * std, 'wv_b': jnp.zeros((D,), dtype=jnp.float32), 'wo_w': jax.random.normal(ks[7], (D, D), dtype=jnp.float32) * std, 'wo_b': jnp.zeros((D,), dtype=jnp.float32)}
        return inp
    _L3_xattn_all = _L3_xattn_setup()
    _L3_xattn_in = {k: v for k, v in _L3_xattn_all.items() if k in ('wq_w', 'wq_b', 'wk_w', 'wk_b', 'wv_w', 'wv_b', 'wo_w', 'wo_b')}
    del _L3_xattn_all

    def _L3_ffn_setup():
        import jax, jax.numpy as jnp
        import numpy as np
        HIDDEN = 128
        INNER = 512

        def _weight_quant(w):
            scale = 1.0 / jnp.clip(jnp.mean(jnp.abs(w)), 1e-05)
            wq = jnp.clip(jnp.round(w * scale), -1.0, 1.0) / scale
            return w + jax.lax.stop_gradient(wq - w)

        def _act_quant(x):
            scale = 127.0 / jnp.clip(jnp.max(jnp.abs(x), axis=-1, keepdims=True), 1e-05)
            xq = jnp.clip(jnp.round(x * scale), -128.0, 127.0) / scale
            return x + jax.lax.stop_gradient(xq - x)

        def _bitlinear(x, w):
            return jnp.einsum('bsi,oi->bso', _act_quant(x), _weight_quant(w))
        key = jax.random.key(seed)
        k0, k1, k2, k3 = jax.random.split(key, 4)
        x = jax.random.normal(k0, (4, 256, HIDDEN), dtype=jnp.float32)
        w_gate = jax.random.normal(k1, (INNER, HIDDEN), dtype=jnp.float32) / np.sqrt(HIDDEN)
        w_up = jax.random.normal(k2, (INNER, HIDDEN), dtype=jnp.float32) / np.sqrt(HIDDEN)
        w_down = jax.random.normal(k3, (HIDDEN, INNER), dtype=jnp.float32) / np.sqrt(INNER)
        return {'x': x, 'w_gate': w_gate, 'w_up': w_up, 'w_down': w_down}
    _L3_ffn_all = _L3_ffn_setup()
    _L3_ffn_in = {k: v for k, v in _L3_ffn_all.items() if k in ('w_gate', 'w_up', 'w_down')}
    del _L3_ffn_all
    return {'x': x, 'ctx_1024': ctx_1024, 'mask_BxSxS2_ff1': mask_BxSxS2_ff1, 'mask_BxS2_ff1': mask_BxS2_ff1, 'mask_BxS2_ik0': mask_BxS2_ik0, 'mask_Bx1xSxS2_bk1': mask_Bx1xSxS2_bk1, 'L0_xattn_Wk': _L0_xattn_in['Wk'], 'L0_xattn_Wv': _L0_xattn_in['Wv'], 'L0_xattn_bv': _L0_xattn_in['bv'], 'L0_xattn_Wq': _L0_xattn_in['Wq'], 'L0_xattn_bq': _L0_xattn_in['bq'], 'L0_xattn_Wo': _L0_xattn_in['Wo'], 'L0_xattn_bo': _L0_xattn_in['bo'], 'L0_ffn_w_router': _L0_ffn_in['w_router'], 'L0_ffn_w_gating': _L0_ffn_in['w_gating'], 'L0_ffn_w_gate': _L0_ffn_in['w_gate'], 'L0_ffn_w_up': _L0_ffn_in['w_up'], 'L0_ffn_w_down': _L0_ffn_in['w_down'], 'L1_xattn_W_k': _L1_xattn_in['W_k'], 'L1_xattn_b_k': _L1_xattn_in['b_k'], 'L1_xattn_W_o': _L1_xattn_in['W_o'], 'L1_xattn_b_o': _L1_xattn_in['b_o'], 'L1_ffn_w_gate': _L1_ffn_in['w_gate'], 'L1_ffn_w_up': _L1_ffn_in['w_up'], 'L1_ffn_w_down': _L1_ffn_in['w_down'], 'L2_xattn_Wq': _L2_xattn_in['Wq'], 'L2_xattn_bq': _L2_xattn_in['bq'], 'L2_xattn_Wk': _L2_xattn_in['Wk'], 'L2_xattn_bk': _L2_xattn_in['bk'], 'L2_xattn_Wv': _L2_xattn_in['Wv'], 'L2_xattn_bv': _L2_xattn_in['bv'], 'L2_xattn_Wo': _L2_xattn_in['Wo'], 'L2_xattn_bo': _L2_xattn_in['bo'], 'L2_ffn_ln1_w': _L2_ffn_in['ln1_w'], 'L2_ffn_ln1_b': _L2_ffn_in['ln1_b'], 'L2_ffn_ln2_w': _L2_ffn_in['ln2_w'], 'L2_ffn_ln2_b': _L2_ffn_in['ln2_b'], 'L2_ffn_w_qkv': _L2_ffn_in['w_qkv'], 'L2_ffn_b_qkv': _L2_ffn_in['b_qkv'], 'L2_ffn_w_o': _L2_ffn_in['w_o'], 'L2_ffn_b_o': _L2_ffn_in['b_o'], 'L2_ffn_w_gate': _L2_ffn_in['w_gate'], 'L2_ffn_w1': _L2_ffn_in['w1'], 'L2_ffn_b1': _L2_ffn_in['b1'], 'L2_ffn_w2': _L2_ffn_in['w2'], 'L2_ffn_b2': _L2_ffn_in['b2'], 'L3_xattn_wq_w': _L3_xattn_in['wq_w'], 'L3_xattn_wq_b': _L3_xattn_in['wq_b'], 'L3_xattn_wk_w': _L3_xattn_in['wk_w'], 'L3_xattn_wk_b': _L3_xattn_in['wk_b'], 'L3_xattn_wv_w': _L3_xattn_in['wv_w'], 'L3_xattn_wv_b': _L3_xattn_in['wv_b'], 'L3_xattn_wo_w': _L3_xattn_in['wo_w'], 'L3_xattn_wo_b': _L3_xattn_in['wo_b'], 'L3_ffn_w_gate': _L3_ffn_in['w_gate'], 'L3_ffn_w_up': _L3_ffn_in['w_up'], 'L3_ffn_w_down': _L3_ffn_in['w_down']}

def reference(x, ctx_1024, mask_BxSxS2_ff1, mask_BxS2_ff1, mask_BxS2_ik0, mask_Bx1xSxS2_bk1, L0_xattn_Wk, L0_xattn_Wv, L0_xattn_bv, L0_xattn_Wq, L0_xattn_bq, L0_xattn_Wo, L0_xattn_bo, L0_ffn_w_router, L0_ffn_w_gating, L0_ffn_w_gate, L0_ffn_w_up, L0_ffn_w_down, L1_xattn_W_k, L1_xattn_b_k, L1_xattn_W_o, L1_xattn_b_o, L1_ffn_w_gate, L1_ffn_w_up, L1_ffn_w_down, L2_xattn_Wq, L2_xattn_bq, L2_xattn_Wk, L2_xattn_bk, L2_xattn_Wv, L2_xattn_bv, L2_xattn_Wo, L2_xattn_bo, L2_ffn_ln1_w, L2_ffn_ln1_b, L2_ffn_ln2_w, L2_ffn_ln2_b, L2_ffn_w_qkv, L2_ffn_b_qkv, L2_ffn_w_o, L2_ffn_b_o, L2_ffn_w_gate, L2_ffn_w1, L2_ffn_b1, L2_ffn_w2, L2_ffn_b2, L3_xattn_wq_w, L3_xattn_wq_b, L3_xattn_wk_w, L3_xattn_wk_b, L3_xattn_wv_w, L3_xattn_wv_b, L3_xattn_wo_w, L3_xattn_wo_b, L3_ffn_w_gate, L3_ffn_w_up, L3_ffn_w_down):
    import jax
    import jax.numpy as jnp

    def _L0_xattn_ref(k, v, q, Wk, Wv, bv, Wq, bq, Wo, bo):
        import jax, jax.numpy as jnp
        import numpy as np
        D_MODEL = 128
        B, S = (4, 256)
        kp = jnp.einsum('bsd,ed->bse', k, Wk)
        vp = jnp.einsum('bsd,ed->bse', v, Wv) + bv
        qp = jnp.einsum('bsd,ed->bse', q, Wq) + bq
        scale = 1.0 / jnp.sqrt(jnp.float32(kp.shape[-1]))
        scores = jnp.einsum('bqd,bkd->bqk', qp, kp) * scale
        probs = jax.nn.softmax(scores, axis=-1)
        ctx = jnp.einsum('bqk,bkd->bqd', probs, vp)
        return jnp.einsum('bqd,ed->bqe', ctx, Wo) + bo

    def _L0_ffn_ref(hidden_states, w_router, w_gating, w_gate, w_up, w_down):
        import jax, jax.numpy as jnp
        import numpy as np
        B, S, H = (2, 128, 128)
        E, F = (8, 512)
        GATE_TEMP = 0.1
        x = hidden_states
        router_probs = jax.nn.softmax(jnp.einsum('bsh,he->bse', x, w_router), axis=-1)
        gate_weights = jax.nn.softmax(jnp.einsum('bsh,he->bse', x, w_gating) / GATE_TEMP, axis=-1)
        g = jnp.einsum('bsh,ehf->ebsf', x, w_gate)
        u = jnp.einsum('bsh,ehf->ebsf', x, w_up)
        h = jax.nn.silu(g) * u
        expert_out = jnp.einsum('ebsf,efh->ebsh', h, w_down)
        cw = router_probs * gate_weights
        cw = cw / (jnp.sum(cw, axis=-1, keepdims=True) + 1e-09)
        out = jnp.einsum('ebsh,bse->bsh', expert_out, cw)
        return out

    def _L1_xattn_ref(query, key, value, cell_mask, seq_mask, W_k, b_k, W_o, b_o):
        import jax, jax.numpy as jnp
        import numpy as np
        k_proj = jnp.einsum('bkd,qd->bkq', key, W_k) + b_k
        scores = jnp.einsum('bqd,bkd->bqk', query, k_proj)
        scores = scores + jnp.log(cell_mask) + jnp.log(seq_mask)[:, None, :]
        p_attn = jax.nn.softmax(scores, axis=-1)
        x = jnp.einsum('bqk,bkd->bqd', p_attn, value)
        return jnp.einsum('bqd,od->bqo', x, W_o) + b_o

    def _L1_ffn_ref(x, w_gate, w_up, w_down):
        import jax, jax.numpy as jnp
        import numpy as np
        BLOCK = 32
        W_BITS = 4
        ACT_BITS = 16

        def act_qdq(x):
            qmax = 2.0 ** (ACT_BITS - 1) - 1.0
            scale = jnp.maximum(jnp.max(jnp.abs(x)) / qmax, 1e-12)
            return jnp.clip(jnp.round(x / scale), -qmax - 1.0, qmax) * scale

        def fixed_qdq_u16(x):
            scale = 1.0 / 65536.0
            return jnp.clip(jnp.round(x / scale), 0.0, 65535.0) * scale

        def lpbq_dequant(w):
            O, I = w.shape
            qmax = 2.0 ** (W_BITS - 1) - 1.0
            wb = w.reshape(O, I // BLOCK, BLOCK)
            s = jnp.maximum(jnp.max(jnp.abs(wb), axis=-1, keepdims=True) / qmax, 1e-12)
            wq = jnp.clip(jnp.round(wb / s), -qmax - 1.0, qmax) * s
            return wq.reshape(O, I)
        x = act_qdq(x)
        up = act_qdq(x @ lpbq_dequant(w_up).T)
        gate = act_qdq(x @ lpbq_dequant(w_gate).T)
        sig = fixed_qdq_u16(jax.nn.sigmoid(gate))
        gate = act_qdq(gate * sig)
        o = act_qdq(gate * up)
        return o @ lpbq_dequant(w_down).T

    def _L2_xattn_ref(query, key_value, mask, Wq, bq, Wk, bk, Wv, bv, Wo, bo):
        import jax, jax.numpy as jnp
        import numpy as np
        import math
        D_MODEL = 128
        N_HEADS = 16
        D_K = D_MODEL // N_HEADS
        B, SQ, _ = query.shape
        SK = key_value.shape[1]
        scale = math.sqrt(D_K)

        def proj(x, W, b):
            y = jnp.einsum('bsd,ed->bse', x, W) + b
            return y.reshape(x.shape[0], x.shape[1], N_HEADS, D_K).transpose(0, 2, 1, 3)
        Q = proj(query, Wq, bq)
        K = proj(key_value, Wk, bk)
        V = proj(key_value, Wv, bv)
        scores = jnp.einsum('bhqd,bhkd->bhqk', Q, K) / scale
        m = mask[:, None, None, :] == 0
        scores = jnp.where(m, jnp.float32(-1000000000.0), scores)
        attn = jax.nn.softmax(scores, axis=-1)
        ctx = jnp.einsum('bhqk,bhkd->bhqd', attn, V)
        ctx = ctx.transpose(0, 2, 1, 3).reshape(B, SQ, D_MODEL)
        out = jnp.einsum('bsd,ed->bse', ctx, Wo) + bo
        return out

    def _L2_ffn_ref(x, ln1_w, ln1_b, ln2_w, ln2_b, w_qkv, b_qkv, w_o, b_o, w_gate, w1, b1, w2, b2):
        import jax, jax.numpy as jnp
        import numpy as np
        from jax import lax
        N_HEADS = 16
        TOP_K = 2
        N_EXPERTS = 8

        def layer_norm(x, w, b, eps=1e-05):
            mu = jnp.mean(x, axis=-1, keepdims=True)
            var = jnp.mean(jnp.square(x - mu), axis=-1, keepdims=True)
            return (x - mu) * lax.rsqrt(var + eps) * w + b

        def attention(x, w_qkv, b_qkv, w_o, b_o):
            B, T, D = x.shape
            dh = D // N_HEADS
            qkv = x @ w_qkv + b_qkv
            q, k, v = jnp.split(qkv, 3, axis=-1)
            q = q.reshape(B, T, N_HEADS, dh)
            k = k.reshape(B, T, N_HEADS, dh)
            v = v.reshape(B, T, N_HEADS, dh)
            scores = jnp.einsum('bqhd,bkhd->bhqk', q, k) / jnp.sqrt(jnp.float32(dh)).astype(x.dtype)
            probs = jax.nn.softmax(scores, axis=-1)
            ctx = jnp.einsum('bhqk,bkhd->bqhd', probs, v).reshape(B, T, D)
            return ctx @ w_o + b_o

        def moe_ff(x, w_gate, w1, b1, w2, b2):
            B, T, D = x.shape
            t = x.reshape(B * T, D)
            probs = jax.nn.softmax(t @ w_gate, axis=-1)
            tw, ti = lax.top_k(probs, TOP_K)
            tw = tw / jnp.sum(tw, axis=-1, keepdims=True)
            out = jnp.zeros_like(t)
            for e in range(N_EXPERTS):
                we = jnp.sum(jnp.where(ti == e, tw, 0.0), axis=-1)
                h = jax.nn.gelu(t @ w1[e] + b1[e]) @ w2[e] + b2[e]
                out = out + we[:, None] * h
            return out.reshape(B, T, D)
        h = x + attention(layer_norm(x, ln1_w, ln1_b), w_qkv, b_qkv, w_o, b_o)
        return h + moe_ff(layer_norm(h, ln2_w, ln2_b), w_gate, w1, b1, w2, b2)

    def _L3_xattn_ref(q, k, v, mask, wq_w, wq_b, wk_w, wk_b, wv_w, wv_b, wo_w, wo_b):
        import jax, jax.numpy as jnp
        import numpy as np
        D_MODEL = 128
        HEAD_NUM = 16
        B, Sq, D = q.shape
        H = HEAD_NUM
        Dh = D // H
        qp = q @ wq_w.T + wq_b
        kp = k @ wk_w.T + wk_b
        vp = v @ wv_w.T + wv_b
        Sk = kp.shape[1]
        qh = qp.reshape(B, Sq, H, Dh).transpose(0, 2, 1, 3)
        kh = kp.reshape(B, Sk, H, Dh).transpose(0, 2, 1, 3)
        vh = vp.reshape(B, Sk, H, Dh).transpose(0, 2, 1, 3)
        alpha = jnp.einsum('bhqd,bhkd->bhqk', qh, kh)
        alpha = jnp.where(mask, jnp.float32(-100000.0), alpha)
        score = jax.nn.softmax(alpha, axis=-1)
        x = jnp.einsum('bhqk,bhkd->bhqd', score, vh)
        x = x.transpose(0, 2, 1, 3).reshape(B, Sq, D)
        return x @ wo_w.T + wo_b

    def _L3_ffn_ref(x, w_gate, w_up, w_down):
        import jax, jax.numpy as jnp
        import numpy as np
        HIDDEN = 128
        INNER = 512

        def _weight_quant(w):
            scale = 1.0 / jnp.clip(jnp.mean(jnp.abs(w)), 1e-05)
            wq = jnp.clip(jnp.round(w * scale), -1.0, 1.0) / scale
            return w + jax.lax.stop_gradient(wq - w)

        def _act_quant(x):
            scale = 127.0 / jnp.clip(jnp.max(jnp.abs(x), axis=-1, keepdims=True), 1e-05)
            xq = jnp.clip(jnp.round(x * scale), -128.0, 127.0) / scale
            return x + jax.lax.stop_gradient(xq - x)

        def _bitlinear(x, w):
            return jnp.einsum('bsi,oi->bso', _act_quant(x), _weight_quant(w))
        gate = jax.nn.silu(_bitlinear(x, w_gate))
        up = _bitlinear(x, w_up)
        return _bitlinear(gate * up, w_down)
    x = x + _L0_xattn_ref(ctx_1024, ctx_1024, _layernorm(x, axis=-1), L0_xattn_Wk, L0_xattn_Wv, L0_xattn_bv, L0_xattn_Wq, L0_xattn_bq, L0_xattn_Wo, L0_xattn_bo)
    x = x + _L0_ffn_ref(_layernorm(x, axis=-1), L0_ffn_w_router, L0_ffn_w_gating, L0_ffn_w_gate, L0_ffn_w_up, L0_ffn_w_down)
    x = x + _L1_xattn_ref(_layernorm(x, axis=-1), ctx_1024, ctx_1024, mask_BxSxS2_ff1, mask_BxS2_ff1, L1_xattn_W_k, L1_xattn_b_k, L1_xattn_W_o, L1_xattn_b_o)
    x = x + _L1_ffn_ref(_layernorm(x, axis=-1), L1_ffn_w_gate, L1_ffn_w_up, L1_ffn_w_down)
    x = x + _L2_xattn_ref(_layernorm(x, axis=-1), ctx_1024, mask_BxS2_ik0, L2_xattn_Wq, L2_xattn_bq, L2_xattn_Wk, L2_xattn_bk, L2_xattn_Wv, L2_xattn_bv, L2_xattn_Wo, L2_xattn_bo)
    x = x + _L2_ffn_ref(_layernorm(x, axis=-1), L2_ffn_ln1_w, L2_ffn_ln1_b, L2_ffn_ln2_w, L2_ffn_ln2_b, L2_ffn_w_qkv, L2_ffn_b_qkv, L2_ffn_w_o, L2_ffn_b_o, L2_ffn_w_gate, L2_ffn_w1, L2_ffn_b1, L2_ffn_w2, L2_ffn_b2)
    x = x + _L3_xattn_ref(_layernorm(x, axis=-1), ctx_1024, ctx_1024, mask_Bx1xSxS2_bk1, L3_xattn_wq_w, L3_xattn_wq_b, L3_xattn_wk_w, L3_xattn_wk_b, L3_xattn_wv_w, L3_xattn_wv_b, L3_xattn_wo_w, L3_xattn_wo_b)
    x = x + _L3_ffn_ref(_layernorm(x, axis=-1), L3_ffn_w_gate, L3_ffn_w_up, L3_ffn_w_down)
    return x

_drawn_inputs = setup_inputs


def setup_inputs(seed=0):
    import zlib

    import numpy as np

    out = dict(_drawn_inputs(seed))
    spreads = {'L0_xattn_bv': (0.0, 0.1),
     'L0_xattn_bq': (0.0, 0.1),
     'L0_xattn_bo': (0.0, 0.1),
     'L1_xattn_b_k': (0.0, 2.0),
     'L1_xattn_b_o': (0.0, 0.1),
     'L2_xattn_bq': (0.0, 0.309),
     'L2_xattn_bk': (0.0, 2.0),
     'L2_xattn_bv': (0.0, 0.1),
     'L2_xattn_bo': (0.0, 0.1),
     'L2_ffn_ln1_w': (1.0, 0.2),
     'L2_ffn_ln1_b': (0.0, 0.1),
     'L2_ffn_ln2_w': (1.0, 0.2),
     'L2_ffn_ln2_b': (0.0, 0.1),
     'L2_ffn_b_qkv': (0.0, 0.1),
     'L2_ffn_b_o': (0.0, 0.1),
     'L2_ffn_b1': (0.0, 0.462),
     'L2_ffn_b2': (0.0, 0.309),
     'L3_xattn_wq_b': (0.0, 0.8),
     'L3_xattn_wk_b': (0.0, 2.0),
     'L3_xattn_wv_b': (0.0, 0.8),
     'L3_xattn_wo_b': (0.0, 0.304)}
    factors = {'L1_ffn_w_gate': 5.509,
     'L1_ffn_w_up': 5.83,
     'L1_ffn_w_down': 5.662,
     'L3_xattn_wq_w': 8.0,
     'L3_xattn_wk_w': 8.0,
     'L3_xattn_wv_w': 5.728,
     'L3_xattn_wo_w': 4.55}
    for name, (base, spread) in spreads.items():
        noise = np.random.default_rng([zlib.crc32(name.encode()), seed]).standard_normal(out[name].shape)
        drawn = base * np.exp(spread * noise) if base else spread * noise
        out[name] = jnp.asarray(drawn.astype(out[name].dtype))
    for name, factor in factors.items():
        out[name] = (out[name] * factor).astype(out[name].dtype)
    return out
```

```python
import numpy as np
import concourse.bass as bass
from concourse import mybir
from contextlib import ExitStack

F32, BF16, F16, I32, U8 = (mybir.dt.float32, mybir.dt.bfloat16, mybir.dt.float16, mybir.dt.int32, mybir.dt.uint8)
ALU, ACT, AX = mybir.AluOpType, mybir.ActivationFunctionType, mybir.AxisListType

B, S, D, KEYS = 32, 128, 128, 120
QUAD = 4
TURNS = B // QUAD
TOK = QUAD * S
HEADS, DH = 16, 8
PER = 4
GROUPS = HEADS // PER
EPS = 1e-5
E, F0, F1 = 8, 512, 384
FC = F0 // 128
SHUT = -float(2 ** 44)
ROUND = 1.5 * 2 ** 23

SMALL = {}


def _column(name, width):
    SMALL[name] = (sum(w for _, w in SMALL.values()), width)


for _name, _width in (
    [("ident", 128), ("q_low", 1), ("k_low", 1), ("expert_rank", 8)]
    + [(f"L0_{x}", 128) for x in ("wq", "wk", "wv", "wo", "bo", "bv")] + [("L0_bq", 1)]
    + [(f"L1_{x}", 128) for x in ("wk", "wo", "bo")] + [("L1_bk", 1)]
    + [(f"{l}_{x}", w) for l in ("X2", "F2", "X3")
       for x, w in (("wq", 512), ("wk", 512), ("wv", 128), ("wo", 128), ("bo", 128), ("bv", 128), ("bq", 4), ("bk", 4))]
    + [("router", 16), ("gate2", 8), ("ln1_w", 1), ("ln1_b", 1), ("ln2_w", 1), ("ln2_b", 1), ("b1", E * FC), ("b2", 128)]
):
    _column(_name, _width)
SMALL_WIDTH = sum(w for _, w in SMALL.values())


class Tally:

    def __init__(self, sem, per, credit=0):
        self.sem, self.per, self.credit = sem, per, credit

    def at(self, turn, n):
        assert n + 1 + self.credit > 0
        return turn * self.per + (n + 1 + self.credit)


class Chain:

    def __init__(self, eng, sem, per=0):
        self.eng, self.sem, self.per, self.n, self.turn = eng, sem, per, 0, 0

    def link(self, instruction):
        self.n += 1
        instruction.then_inc(self.sem, 1)
        self.eng.wait_ge(self.sem, self.turn * self.per + self.n)

    def start(self, turn):
        self.turn, self.n = turn, 0


class Core:

    def __init__(self, nc, ctx, ins, outs):
        self.nc, self.ins, self.outs = nc, ins, outs

        def sb(name, shape, dt=F32):
            return ctx.enter_context(nc.sbuf_tensor(name, shape, dt))

        self.X = sb("X", [S, B, D])
        self.stat = sb("stat", [S, B, 2])
        self.stats6 = sb("stats6", [S, B, 6])
        self.norm_work = sb("norm_work", [S, 2, B])
        self.rstd = sb("rstd", [S, B])
        self.small = sb("small", [128, SMALL_WIDTH])
        self.arena = sb("arena", [128, 12288])
        self.ident16 = sb("ident16", [128, 128], BF16)
        self.neg_ident16 = sb("neg_ident16", [128, 128], BF16)
        self.ones_row = sb("ones_row", [1, 512])
        self.ones_row16 = sb("ones_row16", [1, 128], BF16)
        self.wide = sb("wide", [128, 12288])
        self.bank = [ctx.enter_context(nc.psum_tensor(f"bank{i}", [128, 512], F32)) for i in range(8)]
        self.apart = ctx.enter_context(nc.semaphore("apart"))
        self.arena_in = ctx.enter_context(nc.semaphore("arena_in"))
        self.wide_in = ctx.enter_context(nc.semaphore("wide_in"))
        self.w1_in = sb("w1_in", [128, 36, 32])
        self.w1_sem = ctx.enter_context(nc.semaphore("w1_in_sem"))
        self.arena2_in = ctx.enter_context(nc.semaphore("arena2_in"))
        self.inner = self.wide[:, 0:B * D].rearrange("p (b d) -> p b d", b=B)
        self.w3_in = sb("w3_in", [128, 3, F0])
        self.w3_sem = ctx.enter_context(nc.semaphore("w3_in_sem"))
        self.masks_made = ctx.enter_context(nc.semaphore("masks_made"))
        self.masks_logged = ctx.enter_context(nc.semaphore("masks_logged"))

    def w(self, name, rows=128):
        at, width = SMALL[name]
        return self.small[0:rows, at:at + width]


class PartSemaphores:

    def __init__(self, nc, ctx):
        self.nc, self.taken = nc, []
        ctx.callback(self.give_back)

    def __call__(self, name):
        self.taken.append(self.nc.alloc_semaphore(name=name))
        return self.taken[-1]

    def give_back(self):
        self.nc.clear_and_free_semaphores(self.taken)
        self.nc.all_engine_barrier()


def moe0_weights(c):
    n = E * F0
    gate = c.arena[:, 0:n].rearrange("p (e f) -> p e f", e=E)
    up = c.arena[:, n:2 * n].rearrange("p (e f) -> p e f", e=E)
    down = c.arena[:, 2 * n:3 * n].rearrange("p (e c d) -> p e c d", e=E, c=FC)
    return gate, up, down


def opening(c):
    nc = c.nc
    with ExitStack() as ctx:
        sem = PartSemaphores(nc, ctx)
        x_in = [sem(f"x_in{h}") for h in range(4)]
        small_in, made = sem("small_in"), sem("made")
        with nc.Block() as block:
            @block.sync
            def _(sp):
                for h in range(4):
                    sp.dma_start(c.X[:, 8 * h:8 * h + 8, :], c.ins["x"][:, 8 * h:8 * h + 8, :]).then_inc(x_in[h], 16)
                sp.dma_start(c.small[:, :], c.ins["small"]).then_inc(small_in, 16)
                sp.wait_ge(small_in, 16)

            @block.scalar
            def _(act):
                gate, up, down = moe0_weights(c)
                act.dma_start(gate, c.ins["L0_ffn_w_gate"].rearrange("e d f -> d e f")).then_inc(c.arena_in, 16)
                act.dma_start(up, c.ins["L0_ffn_w_up"].rearrange("e d f -> d e f")).then_inc(c.arena_in, 16)
                for e in range(E):
                    act.dma_start(down[:, e], c.ins["L0_ffn_w_down"][e].rearrange("(c p) d -> p c d", p=128)
                                  ).then_inc(c.arena_in, 16)
                act.dma_start(c.wide[:, 3840:7680], c.ins["cell_mask"]).then_inc(c.wide_in, 16)
                act.dma_start(c.wide[:, 7680:11520], c.ins["seq_mask"].partition_broadcast(S)).then_inc(c.wide_in, 16)
                w1 = c.w1_in[:, :, :].rearrange("p b w -> p (b w)")
                for k, x in enumerate(("up", "gate")):
                    act.dma_start(w1[:, k * F1:(k + 1) * F1].rearrange("p (c i) -> p c i", c=F1 // 128),
                                  c.ins[f"L1_ffn_w_{x}"].rearrange("(c p) i -> p c i", p=128)).then_inc(c.w1_sem, 16)
                act.dma_start(w1[:, 2 * F1:], c.ins["L1_ffn_w_down"]).then_inc(c.w1_sem, 16)
                for k, x in enumerate(("gate", "up")):
                    act.dma_start(c.w3_in[:, k, :].rearrange("p (c i) -> p c i", c=FC),
                                  c.ins[f"L3_ffn_w_{x}"].rearrange("(c p) i -> p c i", p=128)).then_inc(c.w3_sem, 16)
                act.dma_start(c.w3_in[:, 2, :], c.ins["L3_ffn_w_down"]).then_inc(c.w3_sem, 16)
                act.wait_ge(small_in, 16)
                nc.scalar.activation(c.ident16[:, :], c.w("ident"), ACT.Copy).then_inc(made, 1)
                nc.scalar.activation(c.neg_ident16[:, :], c.w("ident"), ACT.Copy, scale=-1.0).then_inc(made, 1)

            @block.vector
            def _(dve):
                nc.vector.memset(c.ones_row[:, :], 1.0).then_inc(made, 1)
                nc.vector.memset(c.ones_row16[:, :], 1.0).then_inc(made, 1)
                for b in range(B):
                    if b % 8 == 0:
                        dve.wait_ge(x_in[b // 8], 16)
                    nc.vector.bn_stats(c.stats6[:, b, :], c.X[:, b, :])


NORM_STEPS = 5


def rstd_on_scalar(c, act, steps, rooted):
    act.wait_ge(steps, NORM_STEPS)
    c.nc.scalar.activation(c.rstd[:, :], c.rstd[:, :], ACT.Sqrt).then_inc(rooted, 1)


def rstd_on_vector(c, dve, steps, rooted):
    nc, v = c.nc, c.nc.vector
    even_mean, even_sq, odd_mean, odd_sq = (c.stats6[:, :, k] for k in (1, 2, 4, 5))
    mean, var, work, diff = c.stat[:, :, 0], c.stat[:, :, 1], c.norm_work[:, 0, :], c.norm_work[:, 1, :]
    v.tensor_tensor(work, even_mean, odd_mean, ALU.add)
    v.tensor_tensor(diff, even_mean, odd_mean, ALU.subtract)
    v.tensor_tensor(var, even_sq, odd_sq, ALU.add).then_inc(steps, 1)
    dve.wait_ge(steps, 1)
    v.tensor_scalar(mean, work, 0.5, None, ALU.mult)
    v.tensor_tensor(diff, diff, diff, ALU.mult).then_inc(steps, 1)
    dve.wait_ge(steps, 2)
    v.scalar_tensor_tensor(out=var, in0=diff, scalar=D / 4, in1=var, op0=ALU.mult, op1=ALU.add).then_inc(steps, 1)
    dve.wait_ge(steps, 3)
    v.tensor_scalar(var, var, 1 / D, None, ALU.mult).then_inc(steps, 1)
    dve.wait_ge(steps, 4)
    v.tensor_scalar(c.rstd[:, :], var, EPS, None, ALU.add).then_inc(steps, 1)
    dve.wait_ge(rooted, 1)
    v.reciprocal(c.rstd[:, :], c.rstd[:, :]).then_inc(rooted, 1)
    dve.wait_ge(rooted, 2)


def wait_apart(eng, sem, value, apart):
    eng.wait_ge(sem, value)
    eng.sem_inc(apart, 1)


def one_head(c, n, masked, scale):
    nc = c.nc
    with ExitStack() as ctx:
        def sb(name, shape, dt=F32):
            return ctx.enter_context(nc.sbuf_tensor(f"{n}_{name}", shape, dt))

        take = PartSemaphores(nc, ctx)

        def sem(name):
            return take(f"{n}_{name}")

        xn, xnT = sb("xn", [S, QUAD, D]), sb("xnT", [D, TOK])
        ctxT = sb("ctxT", [D, QUAD * KEYS])
        qT = xnT if masked else sb("qT", [D, TOK])
        kT = sb("kT", [D, QUAD * KEYS])
        V = sb("V", [KEYS, QUAD, D])
        P, Pn = sb("P", [S, 2, KEYS]), sb("Pn", [S, 2, KEYS])
        scored = sb("scored", [S, 2, KEYS])
        PT, OT = sb("PT", [KEYS, 2, S]), sb("OT", [D, 2, S])
        col = sb("col", [S, 2, 4])
        log_mask = c.wide[:, 0:B * KEYS]
        seq_shut = None if masked else sb("seq_shut", [S, B * KEYS])
        shifted, rooted = sem("shifted"), sem("rooted")
        ctx_in = Tally(sem("ctx_in"), 16)
        val_in = Tally(sem("val_in"), 16)
        normed = Tally(sem("normed"), QUAD)
        turned = Tally(sem("turned"), 1, 1)
        xnT_made = Tally(sem("xnT_made"), 1)
        q_done, q_made = Tally(sem("q_done"), 1), Tally(sem("q_made"), 1)
        k_done, k_made = Tally(sem("k_done"), 1, 1), Tally(sem("k_made"), 1)
        v_done, v_made = Tally(sem("v_done"), 1, 1), Tally(sem("v_made"), 1)
        s_done = Tally(sem("s_done"), QUAD)
        maxed = Tally(sem("maxed"), QUAD)
        exped = Tally(sem("exped"), QUAD, 2)
        scaled = Tally(sem("scaled"), QUAD, 2)
        p_turned = Tally(sem("p_turned"), QUAD, 2)
        pT_made = Tally(sem("pT_made"), QUAD, 1)
        pv_done = Tally(sem("pv_done"), QUAD, 2)
        oT_made = Tally(sem("oT_made"), QUAD, 1)
        o_done = Tally(sem("o_done"), QUAD, 2)
        added = Tally(sem("added"), QUAD, 2)
        chain_sem = sem("dve_chain")
        block = ctx.enter_context(nc.Block())

        @block.sync
        def _(sp):
            with sp.Fori(0, TURNS) as i:
                read = k_done if masked else v_done
                sp.wait_ge(read.sem, read.at(i, -1))
                sp.dma_start(ctxT[:, :], c.ins["ctxT"][:, bass.ds(i * (QUAD * KEYS), QUAD * KEYS)]
                             ).then_inc(ctx_in.sem, 16)
                if masked:
                    sp.wait_ge(pv_done.sem, pv_done.at(i, -1))
                    sp.dma_start(V[:, :, :], c.ins["ctx"][:, bass.ds(i * QUAD, QUAD), :]).then_inc(val_in.sem, 16)

        @block.gpsimd
        def _(pool):
            if not masked:
                masks_for_layer1(c, pool, seq_shut)

        @block.scalar
        def _(act):
            rstd_on_scalar(c, act, shifted, rooted)
            act.sem_inc(exped.sem, exped.credit)
            act.sem_inc(pT_made.sem, pT_made.credit)
            act.sem_inc(oT_made.sem, oT_made.credit)
            with act.Fori(0, TURNS) as i:
                act.wait_ge(turned.sem, turned.at(i, 0))
                act.wait_ge(o_done.sem, o_done.at(i, -1))
                nc.scalar.activation(xnT[:, :], c.bank[0][:, :], ACT.Copy).then_inc(xnT_made.sem, 1)
                if not masked:
                    act.wait_ge(q_done.sem, q_done.at(i, 0))
                    nc.scalar.activation(qT[:, :], c.bank[1][:, :], ACT.Identity, bias=c.w("L0_bq")
                                         ).then_inc(q_made.sem, 1)
                for t in range(QUAD + 2):
                    if t < QUAD:
                        act.wait_ge(maxed.sem, maxed.at(i, t))
                        act.wait_ge(scaled.sem, scaled.at(i, t - 2))
                        src = scored[:, t % 2, :] if masked else c.bank[2 + t % 2][:, 0:KEYS]
                        nc.scalar.activation(P[:, t % 2, :], src, ACT.Exp, bias=col[:, t % 2, 0:1],
                                             scale=scale, accum_out=col[:, t % 2, 1:2]).then_inc(exped.sem, 1)
                    if 1 <= t <= QUAD:
                        act.wait_ge(p_turned.sem, p_turned.at(i, t - 1))
                        act.wait_ge(pv_done.sem, pv_done.at(i, t - 3))
                        nc.scalar.activation(PT[:, (t - 1) % 2, :], c.bank[4][0:KEYS, 0:S], ACT.Copy
                                             ).then_inc(pT_made.sem, 1)
                    if t >= 2:
                        act.wait_ge(pv_done.sem, pv_done.at(i, t - 2))
                        act.wait_ge(o_done.sem, o_done.at(i, t - 4))
                        nc.scalar.activation(OT[:, (t - 2) % 2, :], c.bank[5][:, 0:S], ACT.Copy
                                             ).then_inc(oT_made.sem, 1)
            if not masked:
                act.wait_ge(c.masks_made, 5)
                nc.scalar.activation(c.wide[:, 3840:7680], c.wide[:, 3840:7680], ACT.Ln).then_inc(c.masks_logged, 1)
                nc.scalar.activation(c.wide[:, 7680:11520], c.wide[:, 7680:11520], ACT.Ln).then_inc(c.masks_logged, 1)

        @block.vector
        def _(dve):
            chain = Chain(dve, chain_sem, QUAD * (3 if masked else 2))
            rstd_on_vector(c, dve, shifted, rooted)
            dve.sem_inc(scaled.sem, scaled.credit)
            dve.sem_inc(added.sem, added.credit)
            with dve.Fori(0, TURNS) as i:
                chain.start(i)
                for b in range(QUAD):
                    if b == 0:
                        dve.wait_ge(turned.sem, turned.at(i, -1))
                    at = i * QUAD + b
                    nc.vector.tensor_scalar(xn[:, b, :], c.X[:, bass.ds(at, 1), :], c.stat[:, bass.ds(at, 1), 0],
                                            c.rstd[:, bass.ds(at, 1)], ALU.subtract, ALU.mult).then_inc(normed.sem, 1)
                dve.wait_ge(k_done.sem, k_done.at(i, 0))
                if masked:
                    nc.vector.tensor_scalar(kT[:, :], c.bank[6][:, 0:QUAD * KEYS], c.w("L1_bk"), None, ALU.add
                                            ).then_inc(k_made.sem, 1)
                else:
                    nc.vector.tensor_copy(kT[:, :], c.bank[6][:, 0:QUAD * KEYS]).then_inc(k_made.sem, 1)
                    dve.wait_ge(v_done.sem, v_done.at(i, 0))
                    dve.wait_ge(pv_done.sem, pv_done.at(i, -1))
                    nc.vector.tensor_tensor(V[:, :, :], c.bank[7][0:KEYS, :].rearrange("k (b d) -> k b d", b=QUAD),
                                            c.w("L0_bv", KEYS).unsqueeze(1).broadcast_to([KEYS, QUAD, D]), ALU.add
                                            ).then_inc(v_made.sem, 1)
                for t in range(QUAD + 3):
                    if t < QUAD:
                        r = t % 2
                        dve.wait_ge(s_done.sem, s_done.at(i, t))
                        dve.wait_ge(exped.sem, exped.at(i, t - 2))
                        src = c.bank[2 + r][:, 0:KEYS]
                        if masked:
                            chain.link(nc.vector.tensor_tensor(scored[:, r, :], src, log_mask[:, bass.ds((i * QUAD + t) * KEYS, KEYS)], ALU.add))
                            src = scored[:, r, :]
                        chain.link(nc.vector.reduce_max(col[:, r, 3:4], src, AX.X))
                        nc.vector.tensor_scalar(col[:, r, 0:1], col[:, r, 3:4], -scale, None, ALU.mult).then_inc(maxed.sem, 1)
                    if 1 <= t <= QUAD:
                        r = (t - 1) % 2
                        dve.wait_ge(exped.sem, exped.at(i, t - 1))
                        dve.wait_ge(p_turned.sem, p_turned.at(i, t - 3))
                        chain.link(nc.vector.reciprocal(col[:, r, 2:3], col[:, r, 1:2]))
                        nc.vector.tensor_scalar(Pn[:, r, :], P[:, r, :], col[:, r, 2:3], None, ALU.mult).then_inc(scaled.sem, 1)
                    if t >= 3:
                        b = t - 3
                        at = i * QUAD + b
                        X = c.X[:, bass.ds(at, 1), :]
                        dve.wait_ge(o_done.sem, o_done.at(i, b))
                        nc.vector.tensor_tensor(X, X, c.bank[6 + b % 2][:, 0:D], ALU.add).then_inc(added.sem, 1)
                        wait_apart(dve, added.sem, added.at(i, b), c.apart)
                        nc.vector.bn_stats(c.stats6[:, bass.ds(at, 1), :], X)
                assert chain.n == chain.per, chain.n

        @block.tensor
        def _(pe):
            pe.sem_inc(turned.sem, turned.credit)
            pe.sem_inc(v_done.sem, v_done.credit)
            pe.sem_inc(k_done.sem, k_done.credit)
            pe.sem_inc(p_turned.sem, p_turned.credit)
            pe.sem_inc(pv_done.sem, pv_done.credit)
            pe.sem_inc(o_done.sem, o_done.credit)
            with pe.Fori(0, TURNS) as i:
                for b in range(QUAD):
                    pe.wait_ge(normed.sem, normed.at(i, b))
                    last = nc.tensor.transpose(c.bank[0][:, b * S:(b + 1) * S], xn[:, b, :], c.w("ident"))
                last.then_inc(turned.sem, 1)
                pe.wait_ge(ctx_in.sem, ctx_in.at(i, 15))
                pe.wait_ge(added.sem, added.at(i, -2))
                nc.tensor.matmul(c.bank[6][:, 0:QUAD * KEYS], c.w(n + "_wk"), ctxT[:, :], start=True, stop=True).then_inc(k_done.sem, 1)
                pe.wait_ge(added.sem, added.at(i, -1))
                if not masked:
                    for b in range(QUAD):
                        last = nc.tensor.matmul(c.bank[7][0:KEYS, b * D:(b + 1) * D], ctxT[:, b * KEYS:(b + 1) * KEYS],
                                                c.w("L0_wv"), start=True, stop=True)
                    last.then_inc(v_done.sem, 1)
                pe.wait_ge(xnT_made.sem, xnT_made.at(i, 0))
                if not masked:
                    nc.tensor.matmul(c.bank[1][:, :], c.w("L0_wq"), xnT[:, :], start=True, stop=True).then_inc(q_done.sem, 1)
                    pe.wait_ge(q_made.sem, q_made.at(i, 0))
                pe.wait_ge(k_made.sem, k_made.at(i, 0))
                for t in range(QUAD + 3):
                    if t < QUAD:
                        pe.wait_ge(exped.sem, exped.at(i, t - 2))
                        nc.tensor.matmul(c.bank[2 + t % 2][:, 0:KEYS], qT[:, t * S:(t + 1) * S],
                                         kT[:, t * KEYS:(t + 1) * KEYS], start=True, stop=True).then_inc(s_done.sem, 1)
                    if 1 <= t <= QUAD:
                        pe.wait_ge(scaled.sem, scaled.at(i, t - 1))
                        pe.wait_ge(pT_made.sem, pT_made.at(i, t - 2))
                        nc.tensor.transpose(c.bank[4][0:KEYS, 0:S], Pn[:, (t - 1) % 2, :], c.w("ident")).then_inc(p_turned.sem, 1)
                    if 2 <= t <= QUAD + 1:
                        pe.wait_ge(pT_made.sem, pT_made.at(i, t - 2))
                        if t == 2:
                            if masked:
                                pe.wait_ge(val_in.sem, val_in.at(i, 15))
                            else:
                                pe.wait_ge(v_made.sem, v_made.at(i, 0))
                        pe.wait_ge(oT_made.sem, oT_made.at(i, t - 3))
                        nc.tensor.matmul(c.bank[5][:, 0:S], V[:, t - 2, :], PT[:, (t - 2) % 2, :], start=True, stop=True).then_inc(pv_done.sem, 1)
                    if t >= 3:
                        b = t - 3
                        pe.wait_ge(oT_made.sem, oT_made.at(i, b))
                        pe.wait_ge(added.sem, added.at(i, b - 2))
                        nc.tensor.matmul(c.bank[6 + b % 2][:, 0:D], OT[:, b % 2, :], c.w(n + "_wo"), start=True, stop=False)
                        nc.tensor.matmul(c.bank[6 + b % 2][:, 0:D], c.ones_row[:, 0:S], c.w(n + "_bo", 1), start=False, stop=True).then_inc(o_done.sem, 1)


def masks_for_layer1(c, pool, seq_shut):
    nc = c.nc
    least = 2.0 ** -63
    shut, cell, seq = c.wide[:, 0:3840], c.wide[:, 3840:7680], c.wide[:, 7680:11520]
    pool.wait_ge(c.wide_in, 32)
    nc.gpsimd.tensor_scalar(shut, cell, 0.0, -1e30, ALU.is_le, ALU.mult).then_inc(c.masks_made, 1)
    nc.gpsimd.tensor_scalar(seq_shut[:, :], seq, 0.0, -1e30, ALU.is_le, ALU.mult).then_inc(c.masks_made, 1)
    pool.wait_ge(c.masks_made, 2)
    nc.gpsimd.tensor_tensor(shut, shut, seq_shut[:, :], ALU.add).then_inc(c.masks_made, 1)
    nc.gpsimd.tensor_scalar(cell, cell, least, None, ALU.max).then_inc(c.masks_made, 1)
    nc.gpsimd.tensor_scalar(seq, seq, least, None, ALU.max).then_inc(c.masks_made, 1)


def masks_for_layer1_end(c, pool, sem):
    nc = c.nc
    shut, cell, seq = c.wide[:, 0:3840], c.wide[:, 3840:7680], c.wide[:, 7680:11520]
    pool.wait_ge(c.masks_logged, 2)
    nc.gpsimd.tensor_tensor(cell, cell, seq, ALU.add).then_inc(sem, 1)
    pool.wait_ge(sem, 1)
    nc.gpsimd.tensor_tensor(shut, shut, cell, ALU.add).then_inc(sem, 1)


def experts(c, n, second):
    nc = c.nc
    LOGITS = E if second else 2 * E
    X = c.inner if second else c.X
    with ExitStack() as ctx:
        def sb(name, shape, dt=F32):
            return ctx.enter_context(nc.sbuf_tensor(f"{n}_{name}", shape, dt))

        take = PartSemaphores(nc, ctx)

        def sem(name):
            return take(f"{n}_{name}")

        XT = sb("XT", [D, B * S])
        xn = sb("xn", [S, QUAD, D])
        xs = sb("xs", [D, TOK])
        logits = sb("logits", [S, B, LOGITS])
        weight = sb("weight", [S, B, E])
        tmp, tmp2, tmp3 = sb("tmp", [S, B, LOGITS]), sb("tmp2", [S, B, E]), sb("tmp3", [S, B, E])
        best = sb("best", [S, B, 4])
        left = sb("left", [S, B, E])
        parts = sb("parts", [S, B, 3 * E], BF16)
        partsT = sb("partsT", [3 * E, B * S], BF16)
        b2_parts = sb("b2_parts", [3 * E, 3, D], BF16)
        pick = sb("pick", [3 * E, E, D], BF16)
        shifted, rooted = sem("shifted"), sem("rooted")
        pick_made = sem("pick_made")
        normed = Tally(sem("normed"), QUAD)
        turned = Tally(sem("turned"), 1, 1)
        xs_made = Tally(sem("xs_made"), 1)
        kept = Tally(sem("kept"), 1, 1)
        routed = Tally(sem("routed"), 1, 1)
        logits_made = Tally(sem("logits_made"), 1, 1)
        powers, weighed = sem("powers"), sem("weighed")
        parts_turned, partsT_made = sem("parts_turned"), sem("partsT_made")
        chain_sem = sem("dve_chain")
        with nc.Block() as block:
            @block.gpsimd
            def _(pool):
                if not second:
                    masks_for_layer1_end(c, pool, sem("masks_end"))
                pool.sem_inc(kept.sem, kept.credit)
                with pool.Fori(0, TURNS) as i:
                    pool.wait_ge(xs_made.sem, xs_made.at(i, 0))
                    nc.gpsimd.tensor_copy(XT[:, bass.ds(i * TOK, TOK)], xs[:, :]).then_inc(kept.sem, 1)
                nc.gpsimd.memset(pick[:, :, :], 0.0).then_inc(pick_made, 1)
                for third in range(3):
                    pool.wait_ge(pick_made, third + 1)
                    nc.gpsimd.affine_select(out=pick[:, :, :], in_=pick[:, :, :], compare_op=ALU.not_equal, fill=1.0,
                                            base=-third * E, pattern=[[-1, E], [0, D]], channel_multiplier=1
                                            ).then_inc(pick_made, 1)

            @block.scalar
            def _(act):
                rstd_on_scalar(c, act, shifted, rooted)
                with act.Fori(0, TURNS) as i:
                    act.wait_ge(turned.sem, turned.at(i, 0))
                    act.wait_ge(routed.sem, routed.at(i, -1))
                    act.wait_ge(kept.sem, kept.at(i, -1))
                    if second:
                        nc.scalar.activation(xs[:, :], c.bank[0][:, :], ACT.Identity, scale=c.w("ln2_w"), bias=c.w("ln2_b")
                                             ).then_inc(xs_made.sem, 1)
                    else:
                        nc.scalar.activation(xs[:, :], c.bank[0][:, :], ACT.Copy).then_inc(xs_made.sem, 1)
                act.wait_ge(powers, 1)
                nc.scalar.activation(tmp[:, :, 0:E], logits[:, :, 0:E], ACT.Exp).then_inc(powers, 1)
                if not second:
                    nc.scalar.activation(tmp[:, :, E:], logits[:, :, E:], ACT.Exp, scale=1 / 0.1).then_inc(powers, 1)
                for q in range(TURNS):
                    act.wait_ge(parts_turned, q + 1)
                    nc.scalar.activation(partsT[:, q * TOK:(q + 1) * TOK], c.bank[2 + q % 2][0:3 * E, :], ACT.Copy
                                         ).then_inc(partsT_made, 1)

            @block.vector
            def _(dve):
                rstd_on_vector(c, dve, shifted, rooted)
                dve.sem_inc(logits_made.sem, logits_made.credit)
                with dve.Fori(0, TURNS) as i:
                    dve.wait_ge(turned.sem, turned.at(i, -1))
                    for b in range(QUAD):
                        at = i * QUAD + b
                        nc.vector.tensor_scalar(xn[:, b, :], X[:, bass.ds(at, 1), :], c.stat[:, bass.ds(at, 1), 0],
                                                c.rstd[:, bass.ds(at, 1)], ALU.subtract, ALU.mult).then_inc(normed.sem, 1)
                    dve.wait_ge(routed.sem, routed.at(i, 0))
                    nc.vector.tensor_copy(logits[:, bass.ds(i * QUAD, QUAD), :],
                                          c.bank[1][:, 0:QUAD * LOGITS].rearrange("p (b l) -> p b l", b=QUAD)
                                          ).then_inc(logits_made.sem, 1)
                dve.wait_ge(logits_made.sem, logits_made.at(TURNS - 1, 0))
                chain = Chain(dve, chain_sem)
                link = chain.link
                by8 = lambda ap: ap[:, :, :].rearrange("p b (s e) -> p (b s) e", e=E)
                R = B * LOGITS // E
                wide = lambda ap: ap.unsqueeze(2).broadcast_to([S, ap.shape[1], E])
                one = best[:, :, :].rearrange("p b k -> p (b k)")[:, 0:R]
                link(nc.vector.reduce_max(one, by8(logits), AX.X))
                nc.vector.tensor_tensor(by8(logits), by8(logits), wide(one), ALU.subtract).then_inc(powers, 1)
                dve.wait_ge(powers, 2 if second else 3)
                link(nc.vector.reduce_sum(one, by8(tmp), AX.X))
                link(nc.vector.reciprocal(one, one))
                link(nc.vector.tensor_tensor(by8(tmp), by8(tmp), wide(one), ALU.mult))
                total = best[:, :, 0]
                if second:
                    p, rank = tmp[:, :, :], c.w("expert_rank").unsqueeze(1).broadcast_to([S, B, E])
                    for found, among in ((tmp2, p), (tmp3, left[:, :, :])):
                        found = found[:, :, :]
                        link(nc.vector.reduce_max(total, among, AX.X))
                        link(nc.vector.tensor_tensor(found, among, wide(total), ALU.is_equal))
                        link(nc.vector.tensor_tensor(found, found, rank, ALU.mult))
                        link(nc.vector.reduce_max(total, found, AX.X))
                        link(nc.vector.tensor_tensor(found, found, wide(total), ALU.is_equal))
                        link(nc.vector.scalar_tensor_tensor(out=left[:, :, :], in0=found, scalar=-2.0, in1=p,
                                                            op0=ALU.mult, op1=ALU.add))
                    link(nc.vector.tensor_tensor(tmp2[:, :, :], tmp2[:, :, :], tmp3[:, :, :], ALU.add))
                    link(nc.vector.tensor_tensor(weight[:, :, :], tmp2[:, :, :], p, ALU.mult))
                    link(nc.vector.reduce_sum(total, weight[:, :, :], AX.X))
                else:
                    link(nc.vector.tensor_tensor(weight[:, :, :], tmp[:, :, 0:E], tmp[:, :, E:], ALU.mult))
                    link(nc.vector.reduce_sum(total, weight[:, :, :], AX.X))
                    link(nc.vector.tensor_scalar(total, total, 1e-9, None, ALU.add))
                link(nc.vector.reciprocal(total, total))
                link(nc.vector.tensor_tensor(weight[:, :, :], weight[:, :, :], wide(total), ALU.mult))
                link(nc.vector.tensor_copy(parts[:, :, 0:E], weight[:, :, :]))
                link(nc.vector.tensor_tensor(tmp2[:, :, :], weight[:, :, :], parts[:, :, 0:E], ALU.subtract))
                link(nc.vector.tensor_copy(parts[:, :, E:2 * E], tmp2[:, :, :]))
                link(nc.vector.tensor_tensor(tmp3[:, :, :], tmp2[:, :, :], parts[:, :, E:2 * E], ALU.subtract))
                if second:
                    rest = tmp[:, :, :].rearrange("p b e -> p (b e)")[0:3 * E, 0:D]
                    b2 = c.w("b2", 3 * E)
                    link(nc.vector.tensor_copy(b2_parts[:, 0, :], b2))
                    link(nc.vector.tensor_tensor(rest, b2, b2_parts[:, 0, :], ALU.subtract))
                    link(nc.vector.tensor_copy(b2_parts[:, 1, :], rest))
                    link(nc.vector.tensor_tensor(rest, rest, b2_parts[:, 1, :], ALU.subtract))
                    link(nc.vector.tensor_copy(b2_parts[:, 2, :], rest))
                nc.vector.tensor_copy(parts[:, :, 2 * E:], tmp3[:, :, :]).then_inc(weighed, 1)

            @block.tensor
            def _(pe):
                pe.sem_inc(turned.sem, turned.credit)
                pe.sem_inc(routed.sem, routed.credit)
                with pe.Fori(0, TURNS) as i:
                    for b in range(QUAD):
                        pe.wait_ge(normed.sem, normed.at(i, b))
                        last = nc.tensor.transpose(c.bank[0][:, b * S:(b + 1) * S], xn[:, b, :], c.w("ident"))
                    last.then_inc(turned.sem, 1)
                    pe.wait_ge(xs_made.sem, xs_made.at(i, 0))
                    pe.wait_ge(logits_made.sem, logits_made.at(i, -1))
                    for b in range(QUAD):
                        last = nc.tensor.matmul(c.bank[1][:, b * LOGITS:(b + 1) * LOGITS], xs[:, b * S:(b + 1) * S],
                                                c.w("gate2" if second else "router"), start=True, stop=True)
                    last.then_inc(routed.sem, 1)
                pe.wait_ge(weighed, 1)
                for q in range(TURNS):
                    if q >= 2:
                        pe.wait_ge(partsT_made, q - 1)
                    for b in range(QUAD):
                        last = nc.tensor.matmul(c.bank[2 + q % 2][0:3 * E, b * S:(b + 1) * S], parts[:, q * QUAD + b, :],
                                                c.ident16[:, :], start=True, stop=True)
                    last.then_inc(parts_turned, 1)

        if second:
            up, down = moe2_weights(c)
            gate = up
        else:
            gate, up, down = moe0_weights(c)
        UNITS = E * FC
        xu = None if second else sb("xu", [D, 2, TOK])
        act_out = sb("act_out", [128, 2, TOK])
        h = sb("h", [128, 2, TOK])
        yT = sb("yT", [D, TOK])
        spread = Tally(sem("spread"), E)
        xu_made = Tally(sem("xu_made"), E, 2)
        gated = Tally(sem("gated"), UNITS, 2)
        upped = Tally(sem("upped"), UNITS, FC + 1)
        acted = Tally(sem("acted"), UNITS, 2)
        h_made = Tally(sem("h_made"), UNITS, FC + 1)
        downed = Tally(sem("downed"), UNITS, 2)
        yT_made = Tally(sem("yT_made"), 1, 1)
        y_turned = Tally(sem("y_turned"), 1, 1)
        added = Tally(sem("added"), 1, 1)
        with nc.Block() as block:
            @block.scalar
            def _(act):
                act.sem_inc(acted.sem, acted.credit)
                act.sem_inc(yT_made.sem, yT_made.credit)
                with act.Fori(0, TURNS) as i:
                    for u in range(UNITS):
                        act.wait_ge(gated.sem, gated.at(i, u))
                        act.wait_ge(h_made.sem, h_made.at(i, u - 2))
                        if second:
                            nc.scalar.activation(act_out[:, u % 2, :], c.bank[u % 2][:, :], ACT.Gelu_apprx_tanh,
                                                 bias=c.w("b1")[:, u:u + 1]).then_inc(acted.sem, 1)
                        else:
                            nc.scalar.activation(act_out[:, u % 2, :], c.bank[u % 2][:, :], ACT.Silu).then_inc(acted.sem, 1)
                    act.wait_ge(downed.sem, downed.at(i, UNITS - 1))
                    act.wait_ge(y_turned.sem, y_turned.at(i, -1))
                    nc.scalar.activation(yT[:, :], c.bank[6][:, :], ACT.Copy).then_inc(yT_made.sem, 1)

            @block.vector
            def _(dve):
                dve.sem_inc(h_made.sem, h_made.credit)
                dve.sem_inc(added.sem, added.credit)
                if not second:
                    dve.sem_inc(xu_made.sem, xu_made.credit)
                with dve.Fori(0, TURNS) as i:
                    for u in range(UNITS):
                        e = u // FC
                        if not second and u % FC == 0:
                            dve.wait_ge(spread.sem, spread.at(i, e))
                            dve.wait_ge(upped.sem, upped.at(i, u - FC - 1))
                            nc.vector.tensor_tensor(xu[:, e % 2, :], XT[:, bass.ds(i * TOK, TOK)], c.bank[4 + e % 2][:, :],
                                                    ALU.mult).then_inc(xu_made.sem, 1)
                        dve.wait_ge(acted.sem, acted.at(i, u))
                        dve.wait_ge(downed.sem, downed.at(i, u - 2))
                        if second:
                            if u % FC == 0:
                                dve.wait_ge(spread.sem, spread.at(i, e))
                            other = c.bank[4 + e % 2][:, :]
                        else:
                            dve.wait_ge(upped.sem, upped.at(i, u))
                            other = c.bank[2 + u % 2][:, :]
                        nc.vector.tensor_tensor(h[:, u % 2, :], act_out[:, u % 2, :], other, ALU.mult).then_inc(h_made.sem, 1)
                    dve.wait_ge(y_turned.sem, y_turned.at(i, 0))
                    Xt = c.X[:, bass.ds(i * QUAD, QUAD), :]
                    nc.vector.tensor_tensor(Xt, Xt, c.bank[7][:, :].rearrange("p (b d) -> p b d", b=QUAD), ALU.add
                                            ).then_inc(added.sem, 1)
                    wait_apart(dve, added.sem, added.at(i, 0), c.apart)
                    for b in range(QUAD):
                        nc.vector.bn_stats(c.stats6[:, bass.ds(i * QUAD + b, 1), :], c.X[:, bass.ds(i * QUAD + b, 1), :])

            @block.tensor
            def _(pe):
                if second:
                    pe.wait_ge(c.arena2_in, 16 * (1 + E))
                else:
                    pe.wait_ge(c.arena_in, 16 * (2 + E))
                pe.wait_ge(pick_made, 4)
                for t in (gated, upped, downed, y_turned):
                    if t is not upped or not second:
                        pe.sem_inc(t.sem, t.credit)
                with pe.Fori(0, TURNS) as i:
                    xT = XT[:, bass.ds(i * TOK, TOK)]

                    def spread_weights(e):
                        if second:
                            wait_apart(pe, h_made.sem, h_made.at(i, e * FC - FC - 1), c.apart)
                        else:
                            wait_apart(pe, xu_made.sem, xu_made.at(i, e - 2), c.apart)
                        nc.tensor.matmul(c.bank[4 + e % 2][:, :], pick[:, e, :], partsT[:, bass.ds(i * TOK, TOK)],
                                         start=True, stop=True).then_inc(spread.sem, 1)

                    spread_weights(0)
                    for t in range(UNITS + 2):
                        if t < UNITS:
                            e, f = t // FC, t % FC
                            cols = slice(f * 128, (f + 1) * 128)
                            pe.wait_ge(acted.sem, acted.at(i, t - 2))
                            nc.tensor.matmul(c.bank[t % 2][:, :], gate[:, e, cols], xT, start=True, stop=True
                                             ).then_inc(gated.sem, 1)
                            if not second:
                                pe.wait_ge(xu_made.sem, xu_made.at(i, e))
                                pe.wait_ge(h_made.sem, h_made.at(i, t - 2))
                                nc.tensor.matmul(c.bank[2 + t % 2][:, :], up[:, e, cols], xu[:, e % 2, :], start=True, stop=True
                                                 ).then_inc(upped.sem, 1)
                            if f == 2 and e + 1 < E:
                                spread_weights(e + 1)
                        if t >= 2:
                            u = t - 2
                            pe.wait_ge(h_made.sem, h_made.at(i, u))
                            if u == 0:
                                wait_apart(pe, yT_made.sem, yT_made.at(i, -1), c.apart)
                                if second:
                                    for third in range(3):
                                        nc.tensor.matmul(c.bank[6][:, :], b2_parts[:, third, :],
                                                         partsT[:, bass.ds(i * TOK, TOK)], start=(third == 0), stop=False)
                            nc.tensor.matmul(c.bank[6][:, :], down[:, u // FC, u % FC, :], h[:, u % 2, :],
                                             start=(u == 0 and not second), stop=(u == UNITS - 1)).then_inc(downed.sem, 1)
                    pe.wait_ge(yT_made.sem, yT_made.at(i, 0))
                    pe.wait_ge(added.sem, added.at(i, -1))
                    for b in range(QUAD):
                        last = nc.tensor.transpose(c.bank[7][:, b * S:(b + 1) * S], yT[:, b * S:(b + 1) * S], c.w("ident"))
                    last.then_inc(y_turned.sem, 1)


def ffn1(c):
    nc = c.nc
    RMAX = bass.bass_isa.ReduceOp.max
    CH = F1 // 128
    QMAX = 32767.0
    with ExitStack() as ctx:
        def sb(name, shape, dt=F32):
            return ctx.enter_context(nc.sbuf_tensor(f"G1_{name}", shape, dt))

        take = PartSemaphores(nc, ctx)

        def sem(name):
            return take(f"G1_{name}")

        XT = sb("XT", [D, B * S])
        xn = sb("xn", [S, QUAD, D])
        up = c.arena[:, :].rearrange("p (c t) -> p c t", c=CH)
        gate = c.wide[:, :].rearrange("p (c t) -> p c t", c=CH)
        W = c.w1_in[:, :, :]
        WQ = sb("WQ", [128, 3 * CH * 128])
        WT = sb("WT", [128, 3, CH, 128])
        block_max, block_inv = sb("block_max", [128, 36]), sb("block_inv", [128, 36])
        sig = sb("sig", [128, 2, CH, TOK])
        yT = sb("yT", [D, TOK])
        tops = sb("tops", [128, 5, 2 * CH * TURNS])
        top, tops_all = sb("top", [128, 8]), sb("tops_all", [128, 8])
        scale, inv = sb("scale", [128, 8]), sb("inv", [128, 8])
        shifted, rooted = sem("shifted"), sem("rooted")
        w_quantised, w_turned, wt_made = sem("w_quantised"), sem("w_turned"), sem("wt_made")
        normed, turned = Tally(sem("normed"), QUAD), Tally(sem("turned"), 1, 2)
        xt_made = Tally(sem("xt_made"), 1, 2)
        x_topped = Tally(sem("x_topped"), 1, 2)
        top_ready, top_spread = sem("top_ready"), sem("top_spread")
        x_rounded = sem("x_rounded")
        multiplied = Tally(sem("multiplied"), 2 * CH)
        stored = Tally(sem("stored"), 2 * CH, 2 * CH)
        topped = Tally(sem("topped"), 2 * CH, 2 * CH)
        gate_rounded = Tally(sem("gate_rounded"), 1)
        sig_made = Tally(sem("sig_made"), 1)
        sig_used = Tally(sem("sig_used"), 1, 2)
        o_rounded = sem("o_rounded")
        down_done, yT_made = Tally(sem("down_done"), 1), Tally(sem("yT_made"), 1, 1)
        y_turned, added = Tally(sem("y_turned"), 1, 1), Tally(sem("added"), 1, 1)
        chain_sem, scales_ready = sem("dve_chain"), sem("scales_ready")
        carried = sb("carried", [128, 4])
        block = ctx.enter_context(nc.Block())
        X0, UP, GATE, GS, O = range(5)

        @block.gpsimd
        def _(pool):
            for k in range(4):
                pool.wait_ge(top_ready, k + 1)
                at, width = ((X0, 1), (UP, 2), (GS, 1), (O, 1))[k]
                nc.gpsimd.partition_all_reduce(tops_all[:, at:at + width], top[:, at:at + width], 128, RMAX
                                               ).then_inc(top_spread, 1)

        @block.scalar
        def _(act):
            rstd_on_scalar(c, act, shifted, rooted)
            for k in range(3):
                act.wait_ge(w_turned, k + 1)
                nc.scalar.activation(WT[:, k, :, :], c.bank[2 + k][:, 0:CH * 128].rearrange("p (c o) -> p c o", c=CH), ACT.Copy
                                     ).then_inc(wt_made, 1)
            act.sem_inc(xt_made.sem, xt_made.credit)
            act.sem_inc(stored.sem, stored.credit)
            act.sem_inc(yT_made.sem, yT_made.credit)
            with act.Fori(0, TURNS // 2) as j:
                for r in range(2):
                    act.wait_ge(turned.sem, 2 * j + r + 1 + turned.credit)
                    nc.scalar.activation(XT[:, bass.ds((2 * j + r) * TOK, TOK)], c.bank[r][:, :], ACT.Copy).then_inc(xt_made.sem, 1)
            with act.Fori(0, TURNS) as i:
                for k in range(2 * CH):
                    act.wait_ge(multiplied.sem, multiplied.at(i, k))
                    dst = (up, gate)[k // CH][:, k % CH, bass.ds(i * TOK, TOK)]
                    nc.scalar.activation(dst, c.bank[2 + k][:, :], ACT.Copy).then_inc(stored.sem, 1)
            with act.Fori(0, TURNS // 2) as j:
                for r in range(2):
                    act.wait_ge(gate_rounded.sem, 2 * j + r + 1)
                    act.wait_ge(sig_used.sem, 2 * j + r + 1)
                    nc.scalar.activation(sig[:, r, :, :], gate[:, :, bass.ds((2 * j + r) * TOK, TOK)], ACT.Sigmoid,
                                         scale=scale[:, GATE:GATE + 1]).then_inc(sig_made.sem, 1)
            with act.Fori(0, TURNS) as i:
                act.wait_ge(down_done.sem, down_done.at(i, 0))
                act.wait_ge(y_turned.sem, y_turned.at(i, -1))
                nc.scalar.activation(yT[:, :], c.bank[0][:, :], ACT.Copy, scale=scale[:, O:O + 1]).then_inc(yT_made.sem, 1)

        @block.vector
        def _(dve):
            chain = Chain(dve, chain_sem)
            link = chain.link
            rstd_on_vector(c, dve, shifted, rooted)
            for t in (x_topped, topped, sig_used, added):
                dve.sem_inc(t.sem, t.credit)
            dve.wait_ge(c.w1_sem, 48)
            w3 = WQ[:, :].rearrange("p (b w) -> p b w", w=32)
            spread = lambda ap: ap[:, :].unsqueeze(2).broadcast_to([128, 36, 32])
            link(nc.vector.tensor_reduce(block_max[:, :], W, AX.X, ALU.max, apply_absolute_value=True))
            link(nc.vector.tensor_scalar(block_max[:, :], block_max[:, :], 1 / 7.0, 1e-12, ALU.mult, ALU.max))
            link(nc.vector.reciprocal(block_inv[:, :], block_max[:, :]))
            link(nc.vector.tensor_tensor(w3, W, spread(block_inv), ALU.mult))
            link(nc.vector.tensor_scalar(w3, w3, ROUND, ROUND + 7.0, ALU.add, ALU.min))
            link(nc.vector.tensor_scalar(w3, w3, ROUND - 8.0, ROUND, ALU.max, ALU.subtract))
            nc.vector.tensor_tensor(w3, w3, spread(block_max), ALU.mult).then_inc(w_quantised, 1)

            with dve.Fori(0, TURNS // 2) as j:
                for r in range(2):
                    turn = 2 * j + r
                    dve.wait_ge(turned.sem, turn + turned.credit)
                    for b in range(QUAD):
                        at = turn * QUAD + b
                        nc.vector.tensor_scalar(xn[:, b, :], c.X[:, bass.ds(at, 1), :], c.stat[:, bass.ds(at, 1), 0],
                                                c.rstd[:, bass.ds(at, 1)], ALU.subtract, ALU.mult).then_inc(normed.sem, 1)
                    dve.wait_ge(xt_made.sem, turn + 1 + xt_made.credit)
                    nc.vector.tensor_reduce(tops[:, X0, bass.ds(turn, 1)], XT[:, bass.ds(turn * TOK, TOK)], AX.X, ALU.max,
                                            apply_absolute_value=True).then_inc(x_topped.sem, 1)

            def find_scales(first, last, count, carried, k):
                nc.vector.reduce_max(top[:, first:last], tops[:, first:last, 0:count], AX.X).then_inc(top_ready, 1)
                dve.wait_ge(top_spread, k + 1)
                s = scale[:, first:last]
                link(nc.vector.tensor_tensor(s, tops_all[:, first:last], carried, ALU.mult))
                link(nc.vector.tensor_scalar(s, s, 1 / QMAX, 1e-12, ALU.mult, ALU.max))
                link(nc.vector.reciprocal(inv[:, first:last], s))
                link(nc.vector.tensor_tensor(inv[:, first:last], inv[:, first:last], carried, ALU.mult))

            def rounded(dst, who):
                return nc.vector.tensor_scalar(dst, dst, inv[:, who:who + 1], ROUND, ALU.mult, ALU.add)

            def settled(dst):
                return nc.vector.tensor_scalar(dst, dst, ROUND + QMAX, ROUND, ALU.min, ALU.subtract)

            link(nc.vector.memset(carried[:, :], 1.0))
            dve.wait_ge(x_topped.sem, TURNS + x_topped.credit)
            find_scales(X0, X0 + 1, TURNS, carried[:, 0:1], 0)
            dve.wait_ge(xt_made.sem, TURNS + xt_made.credit)
            for i in range(TURNS):
                cols = XT[:, i * TOK:(i + 1) * TOK]
                link(rounded(cols, X0))
                settled(cols).then_inc(x_rounded, 1)
            with dve.Fori(0, TURNS) as i:
                for k in range(2 * CH):
                    dve.wait_ge(stored.sem, stored.at(i, k))
                    src = (up, gate)[k // CH][:, k % CH, bass.ds(i * TOK, TOK)]
                    nc.vector.tensor_reduce(tops[:, UP + k // CH, bass.ds(i * CH + k % CH, 1)], src, AX.X, ALU.max,
                                            apply_absolute_value=True).then_inc(topped.sem, 1)
            dve.wait_ge(topped.sem, (TURNS + 1) * 2 * CH)
            dve.wait_ge(stored.sem, (TURNS + 1) * 2 * CH)
            link(nc.vector.tensor_copy(carried[:, 0:2], scale[:, X0:X0 + 1].broadcast_to([128, 2])))
            find_scales(UP, UP + 2, TURNS * CH, carried[:, 0:2], 1)
            nc.vector.tensor_scalar(carried[:, 2:3], scale[:, GATE:GATE + 1], 1 / 65536.0, None, ALU.mult
                                    ).then_inc(scales_ready, 1)

            steps = Chain(dve, sem("sigmoid_steps"), 12)
            with dve.Fori(0, TURNS // 2) as j:
                steps.start(j)
                for r in range(2):
                    turn = 2 * j + r
                    g, u = gate[:, :, bass.ds(turn * TOK, TOK)], up[:, :, bass.ds(turn * TOK, TOK)]
                    sg = sig[:, r, :, :]
                    steps.link(rounded(g, GATE))
                    settled(g).then_inc(gate_rounded.sem, 1)
                    steps.link(rounded(u, UP))
                    steps.link(settled(u))
                    dve.wait_ge(sig_made.sem, turn + 1)
                    steps.link(nc.vector.tensor_scalar(sg, sg, 65536.0, ROUND, ALU.mult, ALU.add))
                    steps.link(nc.vector.tensor_scalar(sg, sg, ROUND + 65535.0, ROUND, ALU.min, ALU.subtract))
                    nc.vector.tensor_tensor(g, g, sg, ALU.mult).then_inc(sig_used.sem, 1)
                    dve.wait_ge(sig_used.sem, turn + 1 + sig_used.credit)
                    steps.link(nc.vector.tensor_reduce(tops[:, GS, bass.ds(turn, 1)], g, AX.XY, ALU.max,
                                                       apply_absolute_value=True))
            assert steps.n == steps.per
            find_scales(GS, GS + 1, TURNS, carried[:, 2:3], 2)

            steps = Chain(dve, sem("product_steps"), 4)
            with dve.Fori(0, TURNS) as i:
                steps.start(i)
                g, u = gate[:, :, bass.ds(i * TOK, TOK)], up[:, :, bass.ds(i * TOK, TOK)]
                steps.link(rounded(g, GS))
                steps.link(settled(g))
                steps.link(nc.vector.tensor_tensor(g, g, u, ALU.mult))
                steps.link(nc.vector.tensor_reduce(tops[:, O, bass.ds(i, 1)], g, AX.XY, ALU.max, apply_absolute_value=True))
            assert steps.n == steps.per
            link(nc.vector.tensor_tensor(carried[:, 3:4], scale[:, GS:GS + 1], scale[:, UP:UP + 1], ALU.mult))
            find_scales(O, O + 1, TURNS, carried[:, 3:4], 3)

            steps = Chain(dve, sem("o_steps"), 1)
            with dve.Fori(0, TURNS) as i:
                steps.start(i)
                g = gate[:, :, bass.ds(i * TOK, TOK)]
                steps.link(rounded(g, O))
                settled(g).then_inc(o_rounded, 1)
            with dve.Fori(0, TURNS) as i:
                dve.wait_ge(y_turned.sem, y_turned.at(i, 0))
                Xt = c.X[:, bass.ds(i * QUAD, QUAD), :]
                nc.vector.tensor_tensor(Xt, Xt, c.bank[1][:, :].rearrange("p (b d) -> p b d", b=QUAD), ALU.add
                                        ).then_inc(added.sem, 1)
                wait_apart(dve, added.sem, added.at(i, 0), c.apart)
                for b in range(QUAD):
                    nc.vector.bn_stats(c.stats6[:, bass.ds(i * QUAD + b, 1), :], c.X[:, bass.ds(i * QUAD + b, 1), :])

        @block.tensor
        def _(pe):
            for t in (turned, y_turned):
                pe.sem_inc(t.sem, t.credit)
            pe.wait_ge(w_quantised, 1)
            for k in range(3):
                for q in range(CH):
                    at = (k * CH + q) * 128
                    last = nc.tensor.transpose(c.bank[2 + k][:, q * 128:(q + 1) * 128], WQ[:, at:at + 128], c.w("ident"))
                last.then_inc(w_turned, 1)
            pe.wait_ge(wt_made, 3)
            with pe.Fori(0, TURNS // 2) as j:
                for r in range(2):
                    turn = 2 * j + r
                    pe.wait_ge(xt_made.sem, turn + 1)
                    for b in range(QUAD):
                        pe.wait_ge(normed.sem, turn * QUAD + b + 1)
                        last = nc.tensor.transpose(c.bank[r][:, b * S:(b + 1) * S], xn[:, b, :], c.w("ident"))
                    last.then_inc(turned.sem, 1)
            pe.wait_ge(x_rounded, TURNS)
            with pe.Fori(0, TURNS) as i:
                for k in range(2 * CH):
                    pe.wait_ge(stored.sem, stored.at(i, k - 2 * CH))
                    nc.tensor.matmul(c.bank[2 + k][:, :], WT[:, k // CH, k % CH, :], XT[:, bass.ds(i * TOK, TOK)],
                                     start=True, stop=True).then_inc(multiplied.sem, 1)
            with pe.Fori(0, TURNS) as i:
                pe.wait_ge(o_rounded, i + 1)
                pe.wait_ge(yT_made.sem, yT_made.at(i, -1))
                for q in range(CH):
                    last = nc.tensor.matmul(c.bank[0][:, :], WT[:, 2, q, :], gate[:, q, bass.ds(i * TOK, TOK)],
                                            start=(q == 0), stop=(q == CH - 1))
                last.then_inc(down_done.sem, 1)
                pe.wait_ge(yT_made.sem, yT_made.at(i, 0))
                pe.wait_ge(added.sem, added.at(i, -1))
                for b in range(QUAD):
                    last = nc.tensor.transpose(c.bank[1][:, b * S:(b + 1) * S], yT[:, b * S:(b + 1) * S], c.w("ident"))
                last.then_inc(y_turned.sem, 1)


def many_heads(c, n, own, mask):
    nc = c.nc
    NK = S if own else KEYS
    UNITS = QUAD * GROUPS
    scale = 1.0 if mask == "pairs" else DH ** -0.5
    with ExitStack() as ctx:
        def sb(name, shape, dt=F32):
            return ctx.enter_context(nc.sbuf_tensor(f"{n}_{name}", shape, dt))

        take = PartSemaphores(nc, ctx)

        def sem(name):
            return take(f"{n}_{name}")

        xn, xnT = sb("xn", [S, QUAD, D]), sb("xnT", [D, TOK])
        normed_once = sb("normed_once", [S, QUAD, D]) if own else None
        rstd_twice = sb("rstd_twice", [S, B]) if own else c.rstd
        keysT = xnT if own else sb("ctxT", [D, QUAD * KEYS])
        QS, KS = sb("QS", [128, GROUPS, TOK], F16), sb("KS", [128, GROUPS, QUAD * NK], F16)
        low = sb("low", [128, 2, TOK], F16)
        low_bias = sb("low_bias", [128, 2 * GROUPS])
        V = sb("V", [NK, QUAD, HEADS, 32])
        neg_max = sb("neg_max", [S, 3, PER], BF16)
        P, PT = sb("P", [S, 2, PER * NK]), sb("PT", [NK, 2, PER * S])
        OT = sb("OT", [128, 2, GROUPS * S])
        rcp = sb("rcp", [S, 2, HEADS])
        out, outT = sb("out", [S, 2, HEADS, DH]), sb("outT", [D, 2, S])
        if mask:
            shut = sb("shut", [S, B * KEYS], BF16)
            raw = c.wide[:, B * D:B * D + B * KEYS].bitcast(I32)
            if mask == "pairs":
                raw_words = c.wide[:, B * D:B * D + B * KEYS // 4].bitcast(I32)
                raw = c.wide[:, B * D:B * D + B * KEYS // 4].bitcast(U8)
        shifted, rooted = sem("shifted"), sem("rooted")
        rooted_twice = sem("rooted_twice")
        mask_in, mask_made, v_ready = sem("mask_in"), sem("mask_made"), sem("v_ready")
        ctx_in = Tally(sem("ctx_in"), 16)
        normed = Tally(sem("normed"), QUAD)
        projected = Tally(sem("projected"), 2 + 2 * GROUPS, 1)
        xnT_made = Tally(sem("xnT_made"), 1)
        low_made = Tally(sem("low_made"), 2 * GROUPS)
        qk_made = Tally(sem("qk_made"), 2 * GROUPS, 2)
        v_made = Tally(sem("v_made"), 1)
        scored = Tally(sem("scored"), UNITS)
        maxed = Tally(sem("maxed"), UNITS)
        lessened = Tally(sem("lessened"), UNITS)
        exped = Tally(sem("exped"), UNITS, 3)
        p_turned = Tally(sem("p_turned"), UNITS, 2)
        pT_made = Tally(sem("pT_made"), UNITS, 2)
        pv_done = Tally(sem("pv_done"), UNITS, 2)
        oT_made = Tally(sem("oT_made"), QUAD, 2)
        o_turned = Tally(sem("o_turned"), QUAD, 2)
        out_made = Tally(sem("out_made"), QUAD)
        out_turned = Tally(sem("out_turned"), QUAD, 2)
        outT_made = Tally(sem("outT_made"), QUAD)
        o_done = Tally(sem("o_done"), QUAD, 2)
        added = Tally(sem("added"), QUAD, 1)
        chain_sem = sem("dve_chain")
        block = ctx.enter_context(nc.Block())
        S_BANK = c.bank[0:3]
        PT_BANK = c.bank[3:5]
        OT_BANK = (c.bank[5], c.bank[7])
        TAIL = c.bank[6]

        def proj_bank(k):
            return c.bank[3 if k % 2 else 7]

        @block.sync
        def _(sp):
            if mask:
                sp.wait_ge(c.wide_in, 32)
            if mask == "keys":
                sp.dma_start(raw, c.ins["mask2"].partition_broadcast(S)).then_inc(mask_in, 16)
                up, down = moe2_weights(c)
                sp.wait_ge(c.arena_in, 16 * (2 + E))
                sp.dma_start(up, c.ins["L2_ffn_w1"].rearrange("e d f -> d e f")).then_inc(c.arena2_in, 16)
                for e in range(E):
                    sp.dma_start(down[:, e], c.ins["L2_ffn_w2"][e].rearrange("(c p) d -> p c d", p=128)
                                 ).then_inc(c.arena2_in, 16)
            if mask == "pairs":
                sp.dma_start(raw_words, c.ins["mask3"]).then_inc(mask_in, 16)
            if not own:
                with sp.Fori(0, TURNS) as i:
                    sp.wait_ge(projected.sem, projected.at(i, -1))
                    sp.dma_start(keysT[:, :], c.ins["ctxT"][:, bass.ds(i * (QUAD * KEYS), QUAD * KEYS)]
                                 ).then_inc(ctx_in.sem, 16)

        @block.gpsimd
        def _(pool):
            nc.gpsimd.memset(V[:, :, :, :], 0.0).then_inc(v_ready, 1)
            pool.wait_ge(v_ready, 1)
            nc.gpsimd.memset(V[:, :, :, DH:DH + 1], 1.0).then_inc(v_ready, 1)

        @block.scalar
        def _(act):
            rstd_on_scalar(c, act, shifted, rooted)
            if own:
                act.wait_ge(rooted_twice, 1)
                nc.scalar.activation(rstd_twice[:, :], rstd_twice[:, :], ACT.Sqrt).then_inc(rooted_twice, 1)
            for t in (exped, pT_made, oT_made):
                act.sem_inc(t.sem, t.credit)
            with act.Fori(0, TURNS) as i:
                act.wait_ge(projected.sem, projected.at(i, 0))
                if own:
                    nc.scalar.activation(xnT[:, :], proj_bank(0)[:, :], ACT.Identity, scale=c.w("ln1_w"), bias=c.w("ln1_b")
                                         ).then_inc(xnT_made.sem, 1)
                else:
                    nc.scalar.activation(xnT[:, :], proj_bank(0)[:, :], ACT.Copy).then_inc(xnT_made.sem, 1)
                for k in range(2 * GROUPS):
                    width = TOK if k < GROUPS else QUAD * NK
                    act.wait_ge(projected.sem, projected.at(i, 1 + k))
                    act.wait_ge(qk_made.sem, qk_made.at(i, k - 2))
                    nc.scalar.activation(low[:, k % 2, 0:width], proj_bank(1 + k)[:, 0:width], ACT.Identity,
                                         scale=c.w("q_low" if k < GROUPS else "k_low"), bias=low_bias[:, k:k + 1]
                                         ).then_inc(low_made.sem, 1)
                for t in range(UNITS + 6):
                    u = t - 1
                    if 0 <= u < UNITS:
                        act.wait_ge(lessened.sem, lessened.at(i, u))
                        act.wait_ge(p_turned.sem, p_turned.at(i, u - 2))
                        nc.scalar.activation(P[:, u % 2, :], S_BANK[u % 3][:, 0:PER * NK], ACT.Exp, scale=scale
                                             ).then_inc(exped.sem, 1)
                    b, when = (t - 8) // GROUPS, (t - 8) % GROUPS
                    if when == 0 and 0 <= b < QUAD:
                        act.wait_ge(out_turned.sem, out_turned.at(i, b))
                        act.wait_ge(o_done.sem, o_done.at(i, b - 2))
                        nc.scalar.activation(outT[:, b % 2, :], TAIL[:, 0:S], ACT.Copy).then_inc(outT_made.sem, 1)
                    u = t - 2
                    if 0 <= u < UNITS:
                        act.wait_ge(p_turned.sem, p_turned.at(i, u))
                        act.wait_ge(pv_done.sem, pv_done.at(i, u - 2))
                        nc.scalar.activation(PT[:, u % 2, :], PT_BANK[u % 2][0:NK, :], ACT.Copy).then_inc(pT_made.sem, 1)
                    b, when = (t - 6) // GROUPS, (t - 6) % GROUPS
                    if when == 0 and 0 <= b < QUAD:
                        act.wait_ge(pv_done.sem, pv_done.at(i, 4 * b + 3))
                        act.wait_ge(o_turned.sem, o_turned.at(i, b - 2))
                        nc.scalar.activation(OT[:, b % 2, :], OT_BANK[b % 2][:, :], ACT.Copy).then_inc(oT_made.sem, 1)

        @block.vector
        def _(dve):
            rstd_on_vector(c, dve, shifted, rooted)
            setup = Chain(dve, sem("setup_chain"))
            if own:
                setup.link(nc.vector.tensor_tensor(rstd_twice[:, :], c.rstd[:, :], c.rstd[:, :], ALU.mult))
                setup.link(nc.vector.tensor_tensor(rstd_twice[:, :], rstd_twice[:, :], c.stat[:, :, 1], ALU.mult))
                nc.vector.tensor_scalar(rstd_twice[:, :], rstd_twice[:, :], EPS, None, ALU.add).then_inc(rooted_twice, 1)
                dve.wait_ge(rooted_twice, 2)
                setup.link(nc.vector.reciprocal(rstd_twice[:, :], rstd_twice[:, :]))
                setup.link(nc.vector.tensor_tensor(rstd_twice[:, :], rstd_twice[:, :], c.rstd[:, :], ALU.mult))
            nc.vector.tensor_scalar(low_bias[:, 0:GROUPS], c.w(n + "_bq"), c.w("q_low"), None, ALU.mult)
            setup.link(nc.vector.tensor_scalar(low_bias[:, GROUPS:], c.w(n + "_bk"), c.w("k_low"), None, ALU.mult))
            if mask:
                dve.wait_ge(mask_in, 16)
            if mask == "keys":
                nc.vector.tensor_scalar(shut[:, :], raw, 0.0, SHUT, ALU.is_equal, ALU.mult).then_inc(mask_made, 1)
            if mask == "pairs":
                nc.vector.tensor_scalar(shut[:, :], raw, SHUT, None, ALU.mult).then_inc(mask_made, 1)
            for t in (qk_made, added):
                dve.sem_inc(t.sem, t.credit)
            chain = Chain(dve, chain_sem, QUAD)
            with dve.Fori(0, TURNS) as i:
                chain.start(i)
                dve.wait_ge(projected.sem, projected.at(i, -1))
                for b in range(QUAD):
                    at = i * QUAD + b
                    x, mean = c.X[:, bass.ds(at, 1), :], c.stat[:, bass.ds(at, 1), 0]
                    if own:
                        if b == 0:
                            dve.wait_ge(added.sem, added.at(i, -1))
                        nc.vector.tensor_scalar(normed_once[:, b, :], x, mean, c.rstd[:, bass.ds(at, 1)],
                                                ALU.subtract, ALU.mult)
                    nc.vector.tensor_scalar(xn[:, b, :], x, mean, rstd_twice[:, bass.ds(at, 1)], ALU.subtract, ALU.mult
                                            ).then_inc(normed.sem, 1)
                for k in range(2 * GROUPS):
                    g = k % GROUPS
                    dst, bias, width = (QS, "_bq", TOK) if k < GROUPS else (KS, "_bk", QUAD * NK)
                    dve.wait_ge(low_made.sem, low_made.at(i, k))
                    nc.vector.scalar_tensor_tensor(out=dst[:, g, :], in0=proj_bank(1 + k)[:, 0:width],
                                                   scalar=c.w(n + bias)[:, g:g + 1], in1=low[:, k % 2, 0:width],
                                                   op0=ALU.add, op1=ALU.subtract).then_inc(qk_made.sem, 1)
                dve.wait_ge(projected.sem, projected.at(i, 1 + 2 * GROUPS))
                dve.wait_ge(v_ready, 2)
                for b in range(QUAD):
                    last = nc.vector.tensor_tensor(
                        V[:, b, :, 0:DH], proj_bank(9)[0:NK, b * D:(b + 1) * D].rearrange("k (h d) -> k h d", h=HEADS),
                        c.w(n + "_bv", NK).rearrange("k (h d) -> k h d", h=HEADS), ALU.add)
                last.then_inc(v_made.sem, 1)
                for t in range(UNITS + 6):
                    if t < UNITS:
                        dve.wait_ge(scored.sem, scored.at(i, t))
                        nc.vector.tensor_reduce(neg_max[:, t % 3, :],
                                                S_BANK[t % 3][:, 0:PER * NK].rearrange("q (j k) -> q j k", j=PER),
                                                AX.X, ALU.max, negate=True).then_inc(maxed.sem, 1)
                    b, when = (t - 7) // GROUPS, (t - 7) % GROUPS
                    if when == 0 and 0 <= b < QUAD:
                        dve.wait_ge(o_turned.sem, o_turned.at(i, b))
                        dve.wait_ge(out_turned.sem, out_turned.at(i, b - 2))
                        by_head = TAIL[:, :].rearrange("q (h w) -> q h w", h=HEADS)
                        chain.link(nc.vector.reciprocal(rcp[:, b % 2, :], by_head[:, :, DH]))
                        nc.vector.tensor_tensor(out[:, b % 2, :, :], by_head[:, :, 0:DH],
                                                rcp[:, b % 2, :].unsqueeze(2).broadcast_to([S, HEADS, DH]), ALU.mult
                                                ).then_inc(out_made.sem, 1)
                    b, when = (t - 9) // GROUPS, (t - 9) % GROUPS
                    if when == 0 and 0 <= b < QUAD:
                        at = i * QUAD + b
                        X, result = c.X[:, bass.ds(at, 1), :], TAIL[:, S:2 * S]
                        dve.wait_ge(o_done.sem, o_done.at(i, b))
                        if own:
                            h = c.inner[:, bass.ds(at, 1), :]
                            nc.vector.tensor_tensor(h, normed_once[:, b, :], result, ALU.add).then_inc(added.sem, 1)
                            wait_apart(dve, added.sem, added.at(i, b), c.apart)
                            nc.vector.bn_stats(c.stats6[:, bass.ds(at, 1), :], h)
                            nc.vector.tensor_tensor(X, X, h, ALU.add)
                        else:
                            nc.vector.tensor_tensor(X, X, result, ALU.add).then_inc(added.sem, 1)
                            wait_apart(dve, added.sem, added.at(i, b), c.apart)
                            nc.vector.bn_stats(c.stats6[:, bass.ds(at, 1), :], X)
            assert chain.n == chain.per, (chain.n, chain.per)

        @block.tensor
        def _(pe):
            for t in (projected, p_turned, pv_done, o_turned, out_turned, o_done):
                pe.sem_inc(t.sem, t.credit)
            if mask:
                pe.wait_ge(mask_made, 1)
            with pe.Fori(0, TURNS) as i:
                pe.wait_ge(oT_made.sem, oT_made.at(i, -1))
                for b in range(QUAD):
                    pe.wait_ge(normed.sem, normed.at(i, b))
                    last = nc.tensor.transpose(proj_bank(0)[:, b * S:(b + 1) * S], xn[:, b, :], c.w("ident"))
                last.then_inc(projected.sem, 1)
                pe.wait_ge(xnT_made.sem, xnT_made.at(i, 0))
                pe.wait_ge(pT_made.sem, pT_made.at(i, -2))
                for k in range(2 * GROUPS):
                    if k >= 2:
                        pe.wait_ge(qk_made.sem, qk_made.at(i, k - 2))
                    if k == GROUPS and not own:
                        pe.wait_ge(ctx_in.sem, ctx_in.at(i, 15))
                    g = k % GROUPS
                    w, src, width = (("_wq", xnT, TOK), ("_wk", keysT, QUAD * NK))[k // GROUPS]
                    nc.tensor.matmul(proj_bank(1 + k)[:, 0:width], c.w(n + w)[:, g * 128:(g + 1) * 128], src[:, :],
                                     start=True, stop=True).then_inc(projected.sem, 1)
                pe.wait_ge(qk_made.sem, qk_made.at(i, 2 * GROUPS - 2))
                for b in range(QUAD):
                    last = nc.tensor.matmul(proj_bank(9)[0:NK, b * D:(b + 1) * D], keysT[:, b * NK:(b + 1) * NK],
                                            c.w(n + "_wv"), start=True, stop=True)
                last.then_inc(projected.sem, 1)
                pe.wait_ge(qk_made.sem, qk_made.at(i, 2 * GROUPS - 1))
                for t in range(UNITS + 6):
                    if t < UNITS:
                        b, j = t // PER, t % PER
                        rows = slice(32 * j, 32 * j + 32)
                        pe.wait_ge(exped.sem, exped.at(i, t - 3))
                        for g in range(GROUPS):
                            last = nc.tensor.matmul(S_BANK[t % 3][:, g * NK:(g + 1) * NK], QS[rows, g, b * S:(b + 1) * S],
                                                    KS[rows, g, b * NK:(b + 1) * NK], start=(g == 0), stop=False,
                                                    skip_group_check=True)
                        if mask:
                            last = nc.tensor.matmul(S_BANK[t % 3][:, 0:PER * NK].rearrange("q (j k) -> q j k", j=PER), c.ident16[:, :],
                                                    shut[:, bass.ds((i * QUAD + b) * NK, NK)].unsqueeze(1).broadcast_to([S, PER, NK]),
                                                    start=False, stop=True, skip_group_check=True)
                        last.then_inc(scored.sem, 1)
                    u = t - 1
                    if 0 <= u < UNITS:
                        pe.wait_ge(maxed.sem, maxed.at(i, u))
                        nc.tensor.matmul(S_BANK[u % 3][:, 0:PER * NK].rearrange("q (j k) -> q j k", j=PER), c.ident16[:, :],
                                         neg_max[:, u % 3, :].unsqueeze(2).broadcast_to([S, PER, NK]),
                                         start=False, stop=True, skip_group_check=True).then_inc(lessened.sem, 1)
                    b, when = (t - 7) // GROUPS, (t - 7) % GROUPS
                    if when == 0 and 0 <= b < QUAD:
                        pe.wait_ge(oT_made.sem, oT_made.at(i, b))
                        pe.wait_ge(added.sem, added.at(i, b - 1))
                        for g in range(GROUPS):
                            last = nc.tensor.transpose(TAIL[:, g * S:(g + 1) * S], OT[:, b % 2, g * S:(g + 1) * S], c.w("ident"))
                        last.then_inc(o_turned.sem, 1)
                    b, when = (t - 8) // GROUPS, (t - 8) % GROUPS
                    if when == 0 and 0 <= b < QUAD:
                        pe.wait_ge(out_made.sem, out_made.at(i, b))
                        nc.tensor.transpose(TAIL[:, 0:S], out[:, b % 2, :, :].rearrange("q h d -> q (h d)"), c.w("ident")
                                            ).then_inc(out_turned.sem, 1)
                    b, when = (t - 9) // GROUPS, (t - 9) % GROUPS
                    if when == 0 and 0 <= b < QUAD:
                        pe.wait_ge(outT_made.sem, outT_made.at(i, b))
                        nc.tensor.matmul(TAIL[:, S:2 * S], outT[:, b % 2, :], c.w(n + "_wo"), start=True, stop=False)
                        nc.tensor.matmul(TAIL[:, S:2 * S], c.ones_row[:, 0:S], c.w(n + "_bo", 1), start=False, stop=True
                                         ).then_inc(o_done.sem, 1)
                    u = t - 2
                    if 0 <= u < UNITS:
                        pe.wait_ge(exped.sem, exped.at(i, u))
                        pe.wait_ge(pT_made.sem, pT_made.at(i, u - 2))
                        if u == 0:
                            pe.wait_ge(v_made.sem, v_made.at(i, 0))
                        for j in range(PER):
                            last = nc.tensor.transpose(PT_BANK[u % 2][0:NK, j * S:(j + 1) * S], P[:, u % 2, j * NK:(j + 1) * NK],
                                                       c.w("ident"))
                        last.then_inc(p_turned.sem, 1)
                    u = t - 3
                    if 0 <= u < UNITS:
                        b, j = u // PER, u % PER
                        pe.wait_ge(pT_made.sem, pT_made.at(i, u))
                        if j == 0:
                            pe.wait_ge(oT_made.sem, oT_made.at(i, b - 2))
                        for g in range(GROUPS):
                            last = nc.tensor.matmul(OT_BANK[b % 2][32 * g:32 * g + 32, j * S:(j + 1) * S], V[:, b, GROUPS * j + g, :],
                                                    PT[:, u % 2, g * S:(g + 1) * S], start=True, stop=True)
                        last.then_inc(pv_done.sem, 1)


def moe2_weights(c):
    n = E * F0
    return (c.arena[:, 0:n].rearrange("p (e f) -> p e f", e=E),
            c.arena[:, n:2 * n].rearrange("p (e c d) -> p e c d", e=E, c=FC))


def ffn3(c):
    nc = c.nc
    RADD = bass.bass_isa.ReduceOp.add
    BATCH = 8
    LOOPS = B // BATCH
    with ExitStack() as ctx:
        def sb(name, shape, dt=F32):
            return ctx.enter_context(nc.sbuf_tensor(f"G3_{name}", shape, dt))

        take = PartSemaphores(nc, ctx)

        def sem(name):
            return take(f"G3_{name}")

        W = c.w3_in
        W2 = sb("W2", [128, 3, F0])
        WQ = sb("WQ", [128, 3, F0], BF16)
        WT = sb("WT", [128, 3, F0], BF16)
        sums, sums_all, mean, mean_inv = sb("sums", [128, 3]), sb("sums_all", [128, 3]), sb("mean", [128, 3]), sb("mean_inv", [128, 3])
        xn, xq, xqT = sb("xn", [S, 2, D]), sb("xq", [S, 2, D], BF16), sb("xqT", [D, 2, S], BF16)
        xcol, hcol = sb("xcol", [S, 4, 8]), sb("hcol", [S, 4, 8])
        gate = sb("gate", [S, 2, F0])
        h, hq, hqT = sb("h", [S, 2, F0]), sb("hq", [S, 2, F0], BF16), sb("hqT", [128, 2, F0], BF16)
        shifted, rooted = sem("shifted"), sem("rooted")
        summed, summed_all, w_made, w_turned, wt_made = (sem(x) for x in ("summed", "summed_all", "w_made", "w_turned", "wt_made"))
        xq_made = Tally(sem("xq_made"), BATCH)
        x_turned = Tally(sem("x_turned"), BATCH, 2)
        xqT_made = Tally(sem("xqT_made"), BATCH, 1)
        gated = Tally(sem("gated"), BATCH, 2)
        upped = Tally(sem("upped"), BATCH, 2)
        silued = Tally(sem("silued"), BATCH, 2)
        h_made = Tally(sem("h_made"), BATCH, 2)
        h_scaled = Tally(sem("h_scaled"), BATCH)
        h_rounded = Tally(sem("h_rounded"), BATCH)
        hq_made = Tally(sem("hq_made"), BATCH, 2)
        h_turned = Tally(sem("h_turned"), BATCH, 2)
        hqT_made = Tally(sem("hqT_made"), BATCH, 1)
        down_done = Tally(sem("down_done"), BATCH, 2)
        added = Tally(sem("added"), BATCH, 4)
        written = sem("written")
        chain_sem = sem("dve_chain")
        block = ctx.enter_context(nc.Block())

        @block.sync
        def _(sp):
            with sp.Fori(0, LOOPS) as i:
                sp.wait_ge(added.sem, added.at(i, BATCH - 1))
                sp.dma_start(c.outs[0][:, bass.ds(i * BATCH, BATCH), :], c.X[:, bass.ds(i * BATCH, BATCH), :]).then_inc(written, 16)
            sp.wait_ge(written, 16 * LOOPS)

        @block.gpsimd
        def _(pool):
            pool.wait_ge(summed, 1)
            nc.gpsimd.partition_all_reduce(sums_all[:, :], sums[:, :], 128, RADD).then_inc(summed_all, 1)

        @block.scalar
        def _(act):
            rstd_on_scalar(c, act, shifted, rooted)
            for k in range(3):
                act.wait_ge(w_turned, k + 1)
                nc.scalar.activation(WT[:, k, :], c.bank[k][:, :], ACT.Copy).then_inc(wt_made, 1)
            for t in (xqT_made, silued, hqT_made):
                act.sem_inc(t.sem, t.credit)
            with act.Fori(0, LOOPS) as i:
                for t in range(BATCH + 4):
                    b = t - 1
                    if 0 <= b < BATCH:
                        act.wait_ge(x_turned.sem, x_turned.at(i, b))
                        act.wait_ge(upped.sem, upped.at(i, b - 2))
                        nc.scalar.activation(xqT[:, b % 2, :], c.bank[0][:, 0:S], ACT.Copy).then_inc(xqT_made.sem, 1)
                    b = t - 3
                    if 0 <= b < BATCH:
                        act.wait_ge(hq_made.sem, hq_made.at(i, b - 2))
                        act.wait_ge(h_scaled.sem, h_scaled.at(i, b))
                        nc.scalar.activation(h[:, b % 2, :], h[:, b % 2, :], ACT.Copy, scale=hcol[:, b % 4, 2:3], bias=ROUND
                                             ).then_inc(h_rounded.sem, 1)
                    b = t - 2
                    if 0 <= b < BATCH:
                        act.wait_ge(gated.sem, gated.at(i, b))
                        act.wait_ge(h_made.sem, h_made.at(i, b - 2))
                        nc.scalar.activation(gate[:, b % 2, :], c.bank[1 + b % 2][:, :], ACT.Silu, scale=xcol[:, b % 4, 3:4]
                                             ).then_inc(silued.sem, 1)
                    b = t - 4
                    if 0 <= b < BATCH:
                        act.wait_ge(h_turned.sem, h_turned.at(i, b))
                        act.wait_ge(down_done.sem, down_done.at(i, b - 2))
                        nc.scalar.activation(hqT[:, b % 2, :], c.bank[5][:, :], ACT.Copy).then_inc(hqT_made.sem, 1)

        @block.vector
        def _(dve):
            rstd_on_vector(c, dve, shifted, rooted)
            setup = Chain(dve, sem("setup_chain"))
            link = setup.link
            dve.wait_ge(c.w3_sem, 48)
            nc.vector.tensor_reduce(sums[:, :], W[:, :, :], AX.X, ALU.add, apply_absolute_value=True).then_inc(summed, 1)
            dve.wait_ge(summed_all, 1)
            link(nc.vector.tensor_scalar(mean[:, :], sums_all[:, :], 1.0 / (D * F0), 1e-5, ALU.mult, ALU.max))
            link(nc.vector.reciprocal(mean_inv[:, :], mean[:, :]))
            for k in range(3):
                link(nc.vector.tensor_scalar(W2[:, k, :], W[:, k, :], mean_inv[:, k:k + 1], ROUND, ALU.mult, ALU.add))
            link(nc.vector.tensor_scalar(W2[:, :, :], W2[:, :, :], ROUND - 1.0, ROUND + 1.0, ALU.max, ALU.min))
            nc.vector.tensor_scalar(WQ[:, :, :], W2[:, :, :], ROUND, None, ALU.subtract).then_inc(w_made, 1)
            for t in (h_made, hq_made, added):
                dve.sem_inc(t.sem, t.credit)
            chain = Chain(dve, chain_sem, BATCH * 8)
            with dve.Fori(0, LOOPS) as i:
                chain.start(i)
                link = chain.link
                for t in range(BATCH + 5):
                    b = t
                    if b < BATCH:
                        at, r, q = i * BATCH + b, b % 2, b % 4
                        col = xcol[:, q, :]
                        dve.wait_ge(x_turned.sem, x_turned.at(i, b - 2))
                        link(nc.vector.tensor_scalar(xn[:, r, :], c.X[:, bass.ds(at, 1), :], c.stat[:, bass.ds(at, 1), 0],
                                                     c.rstd[:, bass.ds(at, 1)], ALU.subtract, ALU.mult))
                        link(nc.vector.tensor_reduce(col[:, 0:1], xn[:, r, :], AX.X, ALU.max, apply_absolute_value=True))
                        link(nc.vector.tensor_scalar(col[:, 1:2], col[:, 0:1], 1e-5, 1 / 127.0, ALU.max, ALU.mult))
                        link(nc.vector.reciprocal(col[:, 2:3], col[:, 1:2]))
                        nc.vector.tensor_scalar(col[:, 3:5], mean[:, 0:2], col[:, 1:2], None, ALU.mult)
                        link(nc.vector.tensor_scalar(xn[:, r, :], xn[:, r, :], col[:, 2:3], ROUND, ALU.mult, ALU.add))
                        nc.vector.tensor_scalar(xq[:, r, :], xn[:, r, :], ROUND + 127.0, ROUND, ALU.min, ALU.subtract
                                                ).then_inc(xq_made.sem, 1)
                    b = t - 2
                    if 0 <= b < BATCH:
                        r, q = b % 2, b % 4
                        col = hcol[:, q, :]
                        dve.wait_ge(silued.sem, silued.at(i, b))
                        dve.wait_ge(upped.sem, upped.at(i, b))
                        dve.wait_ge(added.sem, added.at(i, b - 4))
                        nc.vector.scalar_tensor_tensor(out=h[:, r, :], in0=c.bank[3 + r][:, :], scalar=xcol[:, q, 4:5],
                                                       in1=gate[:, r, :], op0=ALU.mult, op1=ALU.mult).then_inc(h_made.sem, 1)
                        dve.wait_ge(h_made.sem, h_made.at(i, b))
                        link(nc.vector.tensor_reduce(col[:, 0:1], h[:, r, :], AX.X, ALU.max, apply_absolute_value=True))
                        link(nc.vector.tensor_scalar(col[:, 1:2], col[:, 0:1], 1e-5, 1 / 127.0, ALU.max, ALU.mult))
                        nc.vector.reciprocal(col[:, 2:3], col[:, 1:2]).then_inc(h_scaled.sem, 1)
                        link(nc.vector.tensor_scalar(col[:, 3:4], mean[:, 2:3], col[:, 1:2], None, ALU.mult))
                    b = t - 3
                    if 0 <= b < BATCH:
                        r = b % 2
                        dve.wait_ge(h_rounded.sem, h_rounded.at(i, b))
                        dve.wait_ge(h_turned.sem, h_turned.at(i, b - 2))
                        nc.vector.tensor_scalar(hq[:, r, :], h[:, r, :], ROUND + 127.0, ROUND, ALU.min, ALU.subtract
                                                ).then_inc(hq_made.sem, 1)
                    b = t - 5
                    if 0 <= b < BATCH:
                        X = c.X[:, bass.ds(i * BATCH + b, 1), :]
                        dve.wait_ge(down_done.sem, down_done.at(i, b))
                        nc.vector.scalar_tensor_tensor(out=X, in0=c.bank[6 + b % 2][:, 0:D], scalar=hcol[:, b % 4, 3:4], in1=X,
                                                       op0=ALU.mult, op1=ALU.add).then_inc(added.sem, 1)
            assert chain.n == chain.per, (chain.n, chain.per)

        @block.tensor
        def _(pe):
            pe.wait_ge(w_made, 1)
            for k in range(3):
                for q in range(FC):
                    last = nc.tensor.matmul(c.bank[k][:, q * 128:(q + 1) * 128], WQ[:, k, q * 128:(q + 1) * 128], c.ident16[:, :],
                                            start=True, stop=True)
                last.then_inc(w_turned, 1)
            for t in (x_turned, gated, upped, h_turned, down_done):
                pe.sem_inc(t.sem, t.credit)
            pe.wait_ge(wt_made, 3)
            with pe.Fori(0, LOOPS) as i:
                for t in range(BATCH + 5):
                    b = t - 1
                    if 0 <= b < BATCH:
                        pe.wait_ge(xq_made.sem, xq_made.at(i, b))
                        pe.wait_ge(xqT_made.sem, xqT_made.at(i, b - 1))
                        nc.tensor.matmul(c.bank[0][:, 0:S], xq[:, b % 2, :], c.ident16[:, :], start=True, stop=True
                                         ).then_inc(x_turned.sem, 1)
                    b = t - 2
                    if 0 <= b < BATCH:
                        pe.wait_ge(xqT_made.sem, xqT_made.at(i, b))
                        pe.wait_ge(silued.sem, silued.at(i, b - 2))
                        nc.tensor.matmul(c.bank[1 + b % 2][:, :], xqT[:, b % 2, :], WT[:, 0, :], start=True, stop=True
                                         ).then_inc(gated.sem, 1)
                        pe.wait_ge(h_made.sem, h_made.at(i, b - 2))
                        nc.tensor.matmul(c.bank[3 + b % 2][:, :], xqT[:, b % 2, :], WT[:, 1, :], start=True, stop=True
                                         ).then_inc(upped.sem, 1)
                    b = t - 4
                    if 0 <= b < BATCH:
                        pe.wait_ge(hq_made.sem, hq_made.at(i, b))
                        pe.wait_ge(hqT_made.sem, hqT_made.at(i, b - 1))
                        for q in range(FC):
                            last = nc.tensor.matmul(c.bank[5][:, q * S:(q + 1) * S], hq[:, b % 2, q * 128:(q + 1) * 128],
                                                    c.ident16[:, :], start=True, stop=True)
                        last.then_inc(h_turned.sem, 1)
                    b = t - 5
                    if 0 <= b < BATCH:
                        pe.wait_ge(hqT_made.sem, hqT_made.at(i, b))
                        pe.wait_ge(added.sem, added.at(i, b - 2))
                        for q in range(FC):
                            last = nc.tensor.matmul(c.bank[6 + b % 2][:, 0:D], hqT[:, b % 2, q * S:(q + 1) * S],
                                                    WT[:, 2, q * 128:(q + 1) * 128], start=(q == 0), stop=(q == FC - 1))
                        last.then_inc(down_done.sem, 1)


def closing(c):
    nc = c.nc
    with ExitStack() as ctx:
        stored = PartSemaphores(nc, ctx)("stored")
        with nc.Block() as block:
            @block.sync
            def _(sp):
                sp.dma_start(c.outs[0], c.X[:, :, :]).then_inc(stored, 16)
                sp.wait_ge(stored, 16)
                for loaded, count in ((c.w1_sem, 3), (c.w3_sem, 3), (c.wide_in, 2), (c.arena_in, 2 + E)):
                    sp.wait_ge(loaded, 16 * count)


PARTS = {
    "a0": lambda c: one_head(c, "L0", False, D ** -0.5),
    "e0": lambda c: experts(c, "E0", False),
    "a1": lambda c: one_head(c, "L1", True, 1.0),
    "g1": ffn1,
    "x2": lambda c: many_heads(c, "X2", False, "keys"),
    "f2": lambda c: many_heads(c, "F2", True, None),
    "e2": lambda c: experts(c, "E2", True),
    "x3": lambda c: many_heads(c, "X3", False, "pairs"),
    "g3": ffn3,
}


def program(nc, ins, outs, parts=tuple(PARTS)):
    with ExitStack() as ctx:
        c = Core(nc, ctx, ins, outs)
        opening(c)
        for part in parts:
            PARTS[part](c)
        if parts[-1] != "g3":
            closing(c)


STACKED = ("q_low", "k_low")


def laid_out(inputs):
    a = {k: np.asarray(v) for k, v in inputs.items()}
    small = np.zeros((128, SMALL_WIDTH), np.float32)

    def put(name, rows, value):
        at, width = SMALL[name]
        small[0:rows, at:at + width] = np.broadcast_to(value, (rows, width))

    part = np.arange(128) % 32 // DH
    put("ident", 128, np.eye(128, dtype=np.float32))
    put("q_low", 128, (part >= 2).astype(np.float32)[:, None])
    put("k_low", 128, (part % 2).astype(np.float32)[:, None])
    put("expert_rank", 128, np.arange(E, 0, -1, dtype=np.float32)[None, :])
    for x in ("q", "k", "v", "o"):
        put(f"L0_w{x}", 128, a[f"L0_xattn_W{x}"].T)
    put("L0_bo", 128, a["L0_xattn_bo"][None, :])
    put("L0_bv", 128, a["L0_xattn_bv"][None, :])
    put("L0_bq", 128, a["L0_xattn_bq"][:, None])
    put("L1_wk", 128, a["L1_xattn_W_k"].T)
    put("L1_wo", 128, a["L1_xattn_W_o"].T)
    put("L1_bo", 128, a["L1_xattn_b_o"][None, :])
    put("L1_bk", 128, a["L1_xattn_b_k"][:, None])
    p = np.arange(128)
    stacked = np.concatenate([(p // 32 * GROUPS + g) * DH + p % DH for g in range(GROUPS)])
    wqkv, bqkv = a["L2_ffn_w_qkv"], a["L2_ffn_b_qkv"]
    for l, wq, wk, wv, wo, bq, bk, bv, bo in (
        ("X2", a["L2_xattn_Wq"].T, a["L2_xattn_Wk"].T, a["L2_xattn_Wv"].T, a["L2_xattn_Wo"].T,
         a["L2_xattn_bq"], a["L2_xattn_bk"], a["L2_xattn_bv"], a["L2_xattn_bo"]),
        ("F2", wqkv[:, 0:128], wqkv[:, 128:256], wqkv[:, 256:384], a["L2_ffn_w_o"],
         bqkv[0:128], bqkv[128:256], bqkv[256:384], a["L2_ffn_b_o"]),
        ("X3", a["L3_xattn_wq_w"].T, a["L3_xattn_wk_w"].T, a["L3_xattn_wv_w"].T, a["L3_xattn_wo_w"].T,
         a["L3_xattn_wq_b"], a["L3_xattn_wk_b"], a["L3_xattn_wv_b"], a["L3_xattn_wo_b"]),
    ):
        put(l + "_wq", 128, wq[:, stacked])
        put(l + "_wk", 128, wk[:, stacked])
        put(l + "_wv", 128, wv)
        put(l + "_wo", 128, wo)
        put(l + "_bv", 128, bv[None, :])
        put(l + "_bo", 128, bo[None, :])
        put(l + "_bq", 128, bq[stacked].reshape(GROUPS, 128).T)
        put(l + "_bk", 128, bk[stacked].reshape(GROUPS, 128).T)
    put("router", 128, np.concatenate([a["L0_ffn_w_router"], a["L0_ffn_w_gating"]], axis=1))
    put("gate2", 128, a["L2_ffn_w_gate"])
    for x in ("ln1_w", "ln1_b", "ln2_w", "ln2_b"):
        put(x, 128, a["L2_ffn_" + x][:, None])
    put("b1", 128, a["L2_ffn_b1"].reshape(E * FC, 128).T)
    put("b2", 3 * E, np.tile(a["L2_ffn_b2"], (3, 1)))
    out = {
        "x": a["x"].transpose(1, 0, 2),
        "small": small,
        "ctxT": a["ctx_1024"].transpose(2, 0, 1).reshape(D, B * KEYS),
        "ctx": a["ctx_1024"].transpose(1, 0, 2),
        "cell_mask": a["mask_BxSxS2_ff1"].transpose(1, 0, 2).reshape(S, B * KEYS),
        "seq_mask": a["mask_BxS2_ff1"].reshape(1, B * KEYS),
        "mask2": a["mask_BxS2_ik0"].reshape(1, B * KEYS),
        "mask3": a["mask_Bx1xSxS2_bk1"].reshape(B, S, KEYS).transpose(1, 0, 2).reshape(S, B * KEYS),
    }
    for x in ("L0_ffn_w_gate", "L0_ffn_w_up", "L0_ffn_w_down", "L1_ffn_w_gate", "L1_ffn_w_up", "L1_ffn_w_down",
              "L2_ffn_w1", "L2_ffn_w2", "L3_ffn_w_gate", "L3_ffn_w_up", "L3_ffn_w_down"):
        out[x] = a[x]
    out = {k: np.ascontiguousarray(v) for k, v in out.items()}
    out["mask3"] = out["mask3"].view(np.int32)
    return out


def kernel(**inputs):
    import concourse.bacc as bacc
    from concourse.bass_utils import run_bass_kernel_spmd

    nc = bacc.Bacc("TRN2", target_bir_lowering=False, num_devices=1)
    arrays = laid_out(inputs)
    ins = {k: nc.dram_tensor(f"in_{k}", v.shape, mybir.dt.from_np(v.dtype), kind="ExternalInput").ap()
           for k, v in arrays.items()}
    out = nc.dram_tensor("out_0", (S, B, D), F32, kind="ExternalOutput").ap()
    program(nc, ins, [out])
    r = run_bass_kernel_spmd(nc, [{f"in_{k}": v for k, v in arrays.items()}], core_ids=[0])
    return np.ascontiguousarray(r.results[0]["out_0"].transpose(1, 0, 2))
```

```python
import numpy as np
import concourse.bass as bass
from concourse import mybir
from contextlib import ExitStack

F32, BF16, F16, I32, U8 = (mybir.dt.float32, mybir.dt.bfloat16, mybir.dt.float16, mybir.dt.int32, mybir.dt.uint8)
ALU, ACT, AX = mybir.AluOpType, mybir.ActivationFunctionType, mybir.AxisListType

B, S, D, KEYS = 32, 128, 128, 120
QUAD = 4
TURNS = B // QUAD
TOK = QUAD * S
HEADS, DH = 16, 8
PER = 4
GROUPS = HEADS // PER
EPS = 1e-5
E, F0, F1 = 8, 512, 384
FC = F0 // 128
SHUT = -float(2 ** 44)
ROUND = 1.5 * 2 ** 23

SMALL = {}


def _column(name, width):
    SMALL[name] = (sum(w for _, w in SMALL.values()), width)


for _name, _width in (
    [("ident", 128), ("spread", 4 * HEADS * 32 // 2), ("expert_rank", 8)]
    + [(f"L0_{x}", 128) for x in ("wq", "wk", "wv", "wo", "bo", "bv")] + [("L0_bq", 1)]
    + [(f"L1_{x}", 128) for x in ("wk", "wo", "bo")] + [("L1_bk", 1)]
    + [(f"{l}_{x}", w) for l in ("X2", "F2", "X3")
       for x, w in (("wq", 128), ("wk", 128), ("wv", 128), ("wo", 128), ("bo", 128), ("bv", 128), ("bq", 1), ("bk", 1))]
    + [("router", 16), ("gate2", 8), ("ln1_w", 1), ("ln1_b", 1), ("ln2_w", 1), ("ln2_b", 1), ("b1", E * FC), ("b2", 128)]
):
    _column(_name, _width)
SMALL_WIDTH = sum(w for _, w in SMALL.values())


class Tally:

    def __init__(self, sem, per, credit=0):
        self.sem, self.per, self.credit = sem, per, credit

    def at(self, turn, n):
        assert n + 1 + self.credit > 0
        return turn * self.per + (n + 1 + self.credit)


class Chain:

    def __init__(self, eng, sem, per=0):
        self.eng, self.sem, self.per, self.n, self.turn = eng, sem, per, 0, 0

    def link(self, instruction):
        self.n += 1
        instruction.then_inc(self.sem, 1)
        self.eng.wait_ge(self.sem, self.turn * self.per + self.n)

    def start(self, turn):
        self.turn, self.n = turn, 0


class Core:

    def __init__(self, nc, ctx, ins, outs):
        self.nc, self.ins, self.outs = nc, ins, outs

        def sb(name, shape, dt=F32):
            return ctx.enter_context(nc.sbuf_tensor(name, shape, dt))

        self.X = sb("X", [S, B, D])
        self.stat = sb("stat", [S, B, 2])
        self.stats6 = sb("stats6", [S, B, 6])
        self.norm_work = sb("norm_work", [S, 2, B])
        self.rstd = sb("rstd", [S, B])
        self.small = sb("small", [128, SMALL_WIDTH])
        self.arena = sb("arena", [128, 3 * F0 * (E + 1)])
        self.ident16 = sb("ident16", [128, 128], BF16)
        self.neg_ident16 = sb("neg_ident16", [128, 128], BF16)
        self.ones_row = sb("ones_row", [1, 512])
        self.ones_row16 = sb("ones_row16", [1, 128], BF16)
        self.wide = sb("wide", [128, 12288])
        self.bank = [ctx.enter_context(nc.psum_tensor(f"bank{i}", [128, 512], F32)) for i in range(8)]
        self.apart = ctx.enter_context(nc.semaphore("apart"))
        self.arena_in = ctx.enter_context(nc.semaphore("arena_in"))
        self.wide_in = ctx.enter_context(nc.semaphore("wide_in"))
        self.w1_in = sb("w1_in", [128, 36, 32])
        self.w1_sem = ctx.enter_context(nc.semaphore("w1_in_sem"))
        self.arena2_in = ctx.enter_context(nc.semaphore("arena2_in"))
        self.inner = self.wide[:, 0:B * D].rearrange("p (b d) -> p b d", b=B)
        self.w3_in = sb("w3_in", [128, 3, F0])
        self.w3_sem = ctx.enter_context(nc.semaphore("w3_in_sem"))
        self.masks_made = ctx.enter_context(nc.semaphore("masks_made"))
        self.masks_logged = ctx.enter_context(nc.semaphore("masks_logged"))

    def w(self, name, rows=128):
        at, width = SMALL[name]
        return self.small[0:rows, at:at + width]


class PartSemaphores:

    def __init__(self, nc, ctx):
        self.nc, self.taken = nc, []
        ctx.callback(self.give_back)

    def __call__(self, name):
        self.taken.append(self.nc.alloc_semaphore(name=name))
        return self.taken[-1]

    def give_back(self):
        self.nc.clear_and_free_semaphores(self.taken)
        self.nc.all_engine_barrier()


def opening(c):
    nc = c.nc
    with ExitStack() as ctx:
        sem = PartSemaphores(nc, ctx)
        x_in = [sem(f"x_in{h}") for h in range(4)]
        small_in, made = sem("small_in"), sem("made")
        with nc.Block() as block:
            @block.sync
            def _(sp):
                for h in range(4):
                    sp.dma_start(c.X[:, 8 * h:8 * h + 8, :], c.ins["x"][:, 8 * h:8 * h + 8, :]).then_inc(x_in[h], 16)
                sp.dma_start(c.small[:, :], c.ins["small"]).then_inc(small_in, 16)
                sp.wait_ge(small_in, 16)

            @block.scalar
            def _(act):
                load_experts(c, act, False, c.arena_in)
                act.dma_start(c.wide[:, 3840:7680], c.ins["cell_mask"]).then_inc(c.wide_in, 16)
                act.dma_start(c.wide[:, 7680:11520], c.ins["seq_mask"].partition_broadcast(S)).then_inc(c.wide_in, 16)
                w1 = c.w1_in[:, :, :].rearrange("p b w -> p (b w)")
                for k, x in enumerate(("up", "gate")):
                    act.dma_start(w1[:, k * F1:(k + 1) * F1].rearrange("p (c i) -> p c i", c=F1 // 128),
                                  c.ins[f"L1_ffn_w_{x}"].rearrange("(c p) i -> p c i", p=128)).then_inc(c.w1_sem, 16)
                act.dma_start(w1[:, 2 * F1:], c.ins["L1_ffn_w_down"]).then_inc(c.w1_sem, 16)
                for k, x in enumerate(("gate", "up")):
                    act.dma_start(c.w3_in[:, k, :].rearrange("p (c i) -> p c i", c=FC),
                                  c.ins[f"L3_ffn_w_{x}"].rearrange("(c p) i -> p c i", p=128)).then_inc(c.w3_sem, 16)
                act.dma_start(c.w3_in[:, 2, :], c.ins["L3_ffn_w_down"]).then_inc(c.w3_sem, 16)
                act.wait_ge(small_in, 16)
                nc.scalar.activation(c.ident16[:, :], c.w("ident"), ACT.Copy).then_inc(made, 1)
                nc.scalar.activation(c.neg_ident16[:, :], c.w("ident"), ACT.Copy, scale=-1.0).then_inc(made, 1)

            @block.vector
            def _(dve):
                nc.vector.memset(c.ones_row[:, :], 1.0).then_inc(made, 1)
                nc.vector.memset(c.ones_row16[:, :], 1.0).then_inc(made, 1)
                for b in range(B):
                    if b % 8 == 0:
                        dve.wait_ge(x_in[b // 8], 16)
                    nc.vector.bn_stats(c.stats6[:, b, :], c.X[:, b, :])


NORM_STEPS = 5


def rstd_on_scalar(c, act, steps, rooted):
    act.wait_ge(steps, NORM_STEPS)
    c.nc.scalar.activation(c.rstd[:, :], c.rstd[:, :], ACT.Sqrt).then_inc(rooted, 1)


def rstd_on_vector(c, dve, steps, rooted):
    nc, v = c.nc, c.nc.vector
    even_mean, even_sq, odd_mean, odd_sq = (c.stats6[:, :, k] for k in (1, 2, 4, 5))
    mean, var, work, diff = c.stat[:, :, 0], c.stat[:, :, 1], c.norm_work[:, 0, :], c.norm_work[:, 1, :]
    v.tensor_tensor(work, even_mean, odd_mean, ALU.add)
    v.tensor_tensor(diff, even_mean, odd_mean, ALU.subtract)
    v.tensor_tensor(var, even_sq, odd_sq, ALU.add).then_inc(steps, 1)
    dve.wait_ge(steps, 1)
    v.tensor_scalar(mean, work, 0.5, None, ALU.mult)
    v.tensor_tensor(diff, diff, diff, ALU.mult).then_inc(steps, 1)
    dve.wait_ge(steps, 2)
    v.scalar_tensor_tensor(out=var, in0=diff, scalar=D / 4, in1=var, op0=ALU.mult, op1=ALU.add).then_inc(steps, 1)
    dve.wait_ge(steps, 3)
    v.tensor_scalar(var, var, 1 / D, None, ALU.mult).then_inc(steps, 1)
    dve.wait_ge(steps, 4)
    v.tensor_scalar(c.rstd[:, :], var, EPS, None, ALU.add).then_inc(steps, 1)
    dve.wait_ge(rooted, 1)
    v.reciprocal(c.rstd[:, :], c.rstd[:, :]).then_inc(rooted, 1)
    dve.wait_ge(rooted, 2)


def wait_apart(eng, sem, value, apart):
    eng.wait_ge(sem, value)
    eng.sem_inc(apart, 1)


def one_head(c, n, masked, scale):
    nc = c.nc
    WK = QUAD * KEYS
    with ExitStack() as ctx:
        def sb(name, shape, dt=F32):
            return ctx.enter_context(nc.sbuf_tensor(f"{n}_{name}", shape, dt))

        take = PartSemaphores(nc, ctx)

        def sem(name):
            return take(f"{n}_{name}")

        xn, xnT = sb("xn", [S, QUAD, D]), sb("xnT", [D, TOK])
        ctxT = sb("ctxT", [D, 2, WK])
        qT = xnT if masked else sb("qT", [D, TOK])
        kT = sb("kT", [D, WK])
        V = sb("V", [KEYS, 2, QUAD, D])
        P, Pn = sb("P", [S, QUAD, KEYS]), sb("Pn", [S, QUAD, KEYS])
        scored = sb("scored", [S, WK]) if masked else None
        PT, OT = sb("PT", [KEYS, TOK]), sb("OT", [D, TOK])
        greatest, neg_max = sb("greatest", [S, QUAD]), sb("neg_max", [S, QUAD])
        sums, rcp = sb("sums", [S, QUAD]), sb("rcp", [S, QUAD])
        log_mask = c.wide[:, 0:B * KEYS]
        seq_shut = None if masked else sb("seq_shut", [S, B * KEYS])
        shifted, rooted = sem("shifted"), sem("rooted")
        ctx_in = [Tally(sem(f"ctx_in{k}"), 16) for k in range(2)]
        val_in = [Tally(sem(f"val_in{k}"), 16) for k in range(2)]
        normed = Tally(sem("normed"), QUAD)
        turned = Tally(sem("turned"), 1, 1)
        xnT_made = Tally(sem("xnT_made"), 1, 1)
        q_done, q_made = Tally(sem("q_done"), 1, 1), Tally(sem("q_made"), 1, 1)
        k_done, k_made = Tally(sem("k_done"), 1, 2), Tally(sem("k_made"), 1, 1)
        v_done, v_made = Tally(sem("v_done"), 1, 2), Tally(sem("v_made"), 1, 1)
        s_done = Tally(sem("s_done"), 1, 1)
        s_read = Tally(sem("s_read"), 1, 1)
        maxed = Tally(sem("maxed"), 1)
        exped = Tally(sem("exped"), 1, 1)
        scaled = Tally(sem("scaled"), 1, 1)
        p_turned = Tally(sem("p_turned"), 1, 1)
        pT_made = Tally(sem("pT_made"), 1, 1)
        pv_done = Tally(sem("pv_done"), 1, 2)
        oT_made = Tally(sem("oT_made"), 1, 1)
        o_done = Tally(sem("o_done"), 1, 1)
        added = Tally(sem("added"), 1, 1)
        summed = Tally(sem("summed"), 1)
        topped = Tally(sem("topped"), 1)
        block = ctx.enter_context(nc.Block())
        bank = c.bank

        def slots(eng, slot, first=None):
            if first:
                first(0)
            slot(0, 0, True, True, False)
            with eng.Fori(0, (TURNS - 2) // 2) as j:
                slot(j * 2 + 1, 1, True, True, True)
                slot(j * 2 + 2, 0, True, True, True)
            slot(TURNS - 1, 1, False, True, True)
            slot(TURNS, 0, False, False, True)

        @block.sync
        def _(sp):
            with sp.Fori(0, TURNS // 2) as j:
                for k in range(2):
                    turn = j * 2 + k
                    read = k_done if masked else v_done
                    sp.wait_ge(read.sem, read.at(turn, -2))
                    sp.dma_start(ctxT[:, k, :], c.ins["ctxT"][:, bass.ds(turn * WK, WK)]).then_inc(ctx_in[k].sem, 16)
                    if masked:
                        sp.wait_ge(pv_done.sem, pv_done.at(turn, -2))
                        sp.dma_start(V[:, k, :, :], c.ins["ctx"][:, bass.ds(turn * QUAD, QUAD), :]).then_inc(val_in[k].sem, 16)

        @block.gpsimd
        def _(pool):
            if not masked:
                masks_for_layer1(c, pool, seq_shut)

        @block.scalar
        def _(act):
            rstd_on_scalar(c, act, shifted, rooted)
            for t in (xnT_made, exped, pT_made, oT_made) + (() if masked else (q_made,)):
                act.sem_inc(t.sem, t.credit)

            def slot(s, parity, norms, scores, output):
                last = s - 1
                if output:
                    act.wait_ge(maxed.sem, maxed.at(last, 0))
                    act.wait_ge(scaled.sem, scaled.at(last, -1))
                    for b in range(QUAD):
                        src = scored if masked else bank[2]
                        done = nc.scalar.activation(P[:, b, :], src[:, b * KEYS:(b + 1) * KEYS], ACT.Exp, scale=scale,
                                                    bias=neg_max[:, b:b + 1], accum_out=sums[:, b:b + 1])
                    done.then_inc(exped.sem, 1)
                if scores:
                    act.wait_ge(turned.sem, turned.at(s, 0))
                    read = s_done if masked else q_done
                    act.wait_ge(read.sem, read.at(s, -1))
                    nc.scalar.activation(xnT[:, :], bank[0][:, :], ACT.Copy).then_inc(xnT_made.sem, 1)
                if output:
                    act.wait_ge(p_turned.sem, p_turned.at(last, 0))
                    act.wait_ge(pv_done.sem, pv_done.at(last, -1))
                    nc.scalar.activation(PT[:, :], bank[4][0:KEYS, :], ACT.Copy).then_inc(pT_made.sem, 1)
                if scores and not masked:
                    act.wait_ge(q_done.sem, q_done.at(s, 0))
                    act.wait_ge(s_done.sem, s_done.at(s, -1))
                    nc.scalar.activation(qT[:, :], bank[1][:, :], ACT.Identity, bias=c.w("L0_bq")).then_inc(q_made.sem, 1)
                if output:
                    act.wait_ge(pv_done.sem, pv_done.at(last, 0))
                    act.wait_ge(o_done.sem, o_done.at(last, -1))
                    nc.scalar.activation(OT[:, :], bank[5][:, :], ACT.Copy).then_inc(oT_made.sem, 1)

            slots(act, slot)
            if not masked:
                act.wait_ge(c.masks_made, 5)
                nc.scalar.activation(c.wide[:, 3840:7680], c.wide[:, 3840:7680], ACT.Ln).then_inc(c.masks_logged, 1)
                nc.scalar.activation(c.wide[:, 7680:11520], c.wide[:, 7680:11520], ACT.Ln).then_inc(c.masks_logged, 1)

        @block.vector
        def _(dve):
            rstd_on_vector(c, dve, shifted, rooted)
            for t in (scaled, added, k_made) + ((s_read,) if masked else (v_made,)):
                dve.sem_inc(t.sem, t.credit)

            def norm(turn):
                dve.wait_ge(turned.sem, turned.at(turn, -1))
                for b in range(QUAD):
                    at = turn * QUAD + b
                    nc.vector.tensor_scalar(xn[:, b, :], c.X[:, bass.ds(at, 1), :], c.stat[:, bass.ds(at, 1), 0],
                                            c.rstd[:, bass.ds(at, 1)], ALU.subtract, ALU.mult).then_inc(normed.sem, 1)

            def slot(s, parity, norms, scores, output):
                last = s - 1
                if output:
                    dve.wait_ge(exped.sem, exped.at(last, 0))
                    dve.wait_ge(p_turned.sem, p_turned.at(last, -1))
                    nc.vector.reciprocal(rcp[:, :], sums[:, :]).then_inc(summed.sem, 1)
                    dve.wait_ge(summed.sem, summed.at(last, 0))
                    nc.vector.tensor_tensor(Pn[:, :, :], P[:, :, :], rcp[:, :].unsqueeze(2).broadcast_to([S, QUAD, KEYS]),
                                            ALU.mult).then_inc(scaled.sem, 1)
                if scores:
                    dve.wait_ge(k_done.sem, k_done.at(s, 0))
                    dve.wait_ge(s_done.sem, s_done.at(s, -1))
                    if masked:
                        nc.vector.tensor_scalar(kT[:, :], bank[6][:, 0:WK], c.w("L1_bk"), None, ALU.add
                                                ).then_inc(k_made.sem, 1)
                    else:
                        nc.vector.tensor_copy(kT[:, :], bank[6][:, 0:WK]).then_inc(k_made.sem, 1)
                        dve.wait_ge(v_done.sem, v_done.at(s, 0))
                        dve.wait_ge(pv_done.sem, pv_done.at(s, -2))
                        nc.vector.tensor_tensor(V[:, parity, :, :], bank[7][0:KEYS, :].rearrange("k (b d) -> k b d", b=QUAD),
                                                c.w("L0_bv", KEYS).unsqueeze(1).broadcast_to([KEYS, QUAD, D]), ALU.add
                                                ).then_inc(v_made.sem, 1)
                if norms:
                    norm(s + 1)
                if scores:
                    dve.wait_ge(s_done.sem, s_done.at(s, 0))
                    dve.wait_ge(exped.sem, exped.at(s, -1))
                    src = bank[2][:, 0:WK]
                    if masked:
                        nc.vector.tensor_tensor(scored[:, :], src, log_mask[:, bass.ds(s * WK, WK)], ALU.add
                                                ).then_inc(s_read.sem, 1)
                        dve.wait_ge(s_read.sem, s_read.at(s, 0))
                        src = scored[:, :]
                    nc.vector.reduce_max(greatest[:, :], src.rearrange("q (b k) -> q b k", b=QUAD), AX.X).then_inc(topped.sem, 1)
                    dve.wait_ge(topped.sem, topped.at(s, 0))
                    nc.vector.tensor_scalar(neg_max[:, :], greatest[:, :], -scale, None, ALU.mult).then_inc(maxed.sem, 1)
                if output:
                    X = c.X[:, bass.ds(last * QUAD, QUAD), :]
                    dve.wait_ge(o_done.sem, o_done.at(last, 0))
                    nc.vector.tensor_tensor(X, X, bank[3][:, :].rearrange("p (b d) -> p b d", b=QUAD), ALU.add
                                            ).then_inc(added.sem, 1)
                    wait_apart(dve, added.sem, added.at(last, 0), c.apart)
                    for b in range(QUAD):
                        at = last * QUAD + b
                        nc.vector.bn_stats(c.stats6[:, bass.ds(at, 1), :], c.X[:, bass.ds(at, 1), :])

            slots(dve, slot, norm)

        @block.tensor
        def _(pe):
            for t in (turned, k_done, p_turned, pv_done, o_done, s_done) + (() if masked else (v_done, q_done)):
                pe.sem_inc(t.sem, t.credit)

            def slot(s, parity, norms, scores, output):
                last, other = s - 1, 1 - parity
                arrived = lambda tally, turn, odd: (turn - odd) * 8 + 16

                def turn_probabilities():
                    pe.wait_ge(scaled.sem, scaled.at(last, 0))
                    pe.wait_ge(pT_made.sem, pT_made.at(last, -1))
                    for b in range(QUAD):
                        done = nc.tensor.transpose(bank[4][0:KEYS, b * S:(b + 1) * S], Pn[:, b, :], c.w("ident"))
                    done.then_inc(p_turned.sem, 1)

                def queries():
                    pe.wait_ge(xnT_made.sem, xnT_made.at(s, 0))
                    pe.wait_ge(q_made.sem, q_made.at(s, -1))
                    nc.tensor.matmul(bank[1][:, :], c.w("L0_wq"), xnT[:, :], start=True, stop=True).then_inc(q_done.sem, 1)

                def probabilities_times_values():
                    pe.wait_ge(pT_made.sem, pT_made.at(last, 0))
                    if masked:
                        pe.wait_ge(val_in[other].sem, arrived(val_in, last, other))
                    else:
                        pe.wait_ge(v_made.sem, v_made.at(last, 0))
                    pe.wait_ge(oT_made.sem, oT_made.at(last, -1))
                    for b in range(QUAD):
                        done = nc.tensor.matmul(bank[5][:, b * S:(b + 1) * S], V[:, other, b, :], PT[:, b * S:(b + 1) * S],
                                                start=True, stop=True)
                    done.then_inc(pv_done.sem, 1)

                def scores_of_turn():
                    made = xnT_made if masked else q_made
                    pe.wait_ge(made.sem, made.at(s, 0))
                    pe.wait_ge(k_made.sem, k_made.at(s, 0))
                    read = s_read if masked else exped
                    pe.wait_ge(read.sem, read.at(s, -1))
                    for b in range(QUAD):
                        done = nc.tensor.matmul(bank[2][:, b * KEYS:(b + 1) * KEYS], qT[:, b * S:(b + 1) * S],
                                                kT[:, b * KEYS:(b + 1) * KEYS], start=True, stop=True)
                    done.then_inc(s_done.sem, 1)

                if scores:
                    for b in range(QUAD):
                        if b == 0:
                            pe.wait_ge(xnT_made.sem, xnT_made.at(s, -1))
                        pe.wait_ge(normed.sem, normed.at(s, b))
                        done = nc.tensor.transpose(bank[0][:, b * S:(b + 1) * S], xn[:, b, :], c.w("ident"))
                    done.then_inc(turned.sem, 1)
                    pe.wait_ge(ctx_in[parity].sem, arrived(ctx_in, s, parity))
                    pe.wait_ge(k_made.sem, k_made.at(s, -1))
                    nc.tensor.matmul(bank[6][:, 0:WK], c.w(n + "_wk"), ctxT[:, parity, :], start=True, stop=True
                                     ).then_inc(k_done.sem, 1)
                    if not masked:
                        pe.wait_ge(v_made.sem, v_made.at(s, -1))
                        for b in range(QUAD):
                            done = nc.tensor.matmul(bank[7][0:KEYS, b * D:(b + 1) * D], ctxT[:, parity, b * KEYS:(b + 1) * KEYS],
                                                    c.w("L0_wv"), start=True, stop=True)
                        done.then_inc(v_done.sem, 1)
                if masked and scores:
                    scores_of_turn()
                if output:
                    turn_probabilities()
                if scores and not masked:
                    queries()
                if output:
                    probabilities_times_values()
                if scores and not masked:
                    scores_of_turn()
                if output:
                    pe.wait_ge(added.sem, added.at(last, -1))
                    nc.tensor.matmul(bank[3][:, :].rearrange("p (b d) -> p b d", b=QUAD), c.ones_row[:, 0:S],
                                     c.w(n + "_bo", 1).unsqueeze(1).broadcast_to([1, QUAD, D]), start=True, stop=False,
                                     skip_group_check=True)
                    pe.wait_ge(oT_made.sem, oT_made.at(last, 0))
                    for b in range(QUAD):
                        done = nc.tensor.matmul(bank[3][:, b * D:(b + 1) * D], OT[:, b * S:(b + 1) * S], c.w(n + "_wo"),
                                                start=False, stop=True, skip_group_check=True)
                    done.then_inc(o_done.sem, 1)

            slots(pe, slot)


def masks_for_layer1(c, pool, seq_shut):
    nc = c.nc
    least = 2.0 ** -63
    shut, cell, seq = c.wide[:, 0:3840], c.wide[:, 3840:7680], c.wide[:, 7680:11520]
    pool.wait_ge(c.wide_in, 32)
    nc.gpsimd.tensor_scalar(shut, cell, 0.0, -1e30, ALU.is_le, ALU.mult).then_inc(c.masks_made, 1)
    nc.gpsimd.tensor_scalar(seq_shut[:, :], seq, 0.0, -1e30, ALU.is_le, ALU.mult).then_inc(c.masks_made, 1)
    pool.wait_ge(c.masks_made, 2)
    nc.gpsimd.tensor_tensor(shut, shut, seq_shut[:, :], ALU.add).then_inc(c.masks_made, 1)
    nc.gpsimd.tensor_scalar(cell, cell, least, None, ALU.max).then_inc(c.masks_made, 1)
    nc.gpsimd.tensor_scalar(seq, seq, least, None, ALU.max).then_inc(c.masks_made, 1)


def masks_for_layer1_end(c, pool, sem):
    nc = c.nc
    shut, cell, seq = c.wide[:, 0:3840], c.wide[:, 3840:7680], c.wide[:, 7680:11520]
    pool.wait_ge(c.masks_logged, 2)
    nc.gpsimd.tensor_tensor(cell, cell, seq, ALU.add).then_inc(sem, 1)
    pool.wait_ge(sem, 1)
    nc.gpsimd.tensor_tensor(shut, shut, cell, ALU.add).then_inc(sem, 1)


def split_layout(c, second):
    cols = (2 if second else 3) * F0
    loaded = c.arena[:, cols:(E + 1) * cols]
    return cols, loaded, c.arena[:, 0:E * cols].bitcast(F16).rearrange("p (e part q) -> p e part q", e=E, part=2)


def load_experts(c, eng, second, sem):
    cols, loaded, _ = split_layout(c, second)
    loaded = loaded.rearrange("p (e q) -> p e q", e=E)
    names = ("L2_ffn_w1",) if second else ("L0_ffn_w_gate", "L0_ffn_w_up")
    for k, name in enumerate(names):
        eng.dma_start(loaded[:, :, k * F0:(k + 1) * F0], c.ins[name].rearrange("e d f -> d e f")).then_inc(sem, 16)
    for e in range(E):
        eng.dma_start(loaded[:, e, cols - F0:].rearrange("p (c d) -> p c d", c=FC),
                      c.ins["L2_ffn_w2" if second else "L0_ffn_w_down"][e].rearrange("(c p) d -> p c d", p=128)
                      ).then_inc(sem, 16)


X_UP, W_UP, H_UP = 16.0, 256.0, 4.0


def experts(c, n, second):
    nc = c.nc
    LOGITS = E if second else 2 * E
    X = c.inner if second else c.X
    with ExitStack() as ctx:
        def sb(name, shape, dt=F32):
            return ctx.enter_context(nc.sbuf_tensor(f"{n}_{name}", shape, dt))

        take = PartSemaphores(nc, ctx)

        def sem(name):
            return take(f"{n}_{name}")

        cols, loaded, W = split_layout(c, second)
        W_flat = c.arena[:, 0:E * cols].bitcast(F16)
        XT = sb("XT", [D, 2, B * S], F16)
        xn = sb("xn", [S, 2, QUAD, D])
        xs = sb("xs", [D, 2, TOK])
        logits = sb("logits", [S, B, LOGITS])
        weight = sb("weight", [S, B, E])
        tmp, tmp2, tmp3 = sb("tmp", [S, B, LOGITS]), sb("tmp2", [S, B, E]), sb("tmp3", [S, B, E])
        best = sb("best", [S, B, 4])
        left = sb("left", [S, B, E])
        wT = sb("wT", [E, 2, TOK]) if second else None
        shifted, rooted = sem("shifted"), sem("rooted")
        normed = Tally(sem("normed"), QUAD)
        turned = Tally(sem("turned"), 1, 2)
        xs_made = Tally(sem("xs_made"), 1)
        x_high = Tally(sem("x_high"), 1)
        x_low = Tally(sem("x_low"), 1, 2)
        w_high = Tally(sem("w_high"), 1)
        w_low = Tally(sem("w_low"), 1, 1)
        routed = Tally(sem("routed"), 1, 2)
        logits_made = Tally(sem("logits_made"), 1, 2)
        powers, weighed = sem("powers"), sem("weighed")
        w_turned, wT_made = sem("w_turned"), sem("wT_made")
        b2_done, b2_added = sem("b2_done"), sem("b2_added")
        chain_sem = sem("dve_chain")
        with nc.Block() as block:
            if not second:
                @block.gpsimd
                def _(pool):
                    masks_for_layer1_end(c, pool, sem("masks_end"))

            @block.scalar
            def _(act):
                rstd_on_scalar(c, act, shifted, rooted)
                act.wait_ge(c.arena2_in if second else c.arena_in, 16 * ((1 if second else 2) + E))
                with act.Fori(0, TURNS // 2) as i:
                    for k in range(2):
                        turn = i * 2 + k
                        wait_apart(act, w_low.sem, w_low.at(turn, -1), c.apart)
                        nc.scalar.activation(W_flat[:, bass.ds(turn * (2 * cols), cols)], loaded[:, bass.ds(turn * cols, cols)],
                                             ACT.Copy, scale=W_UP).then_inc(w_high.sem, 1)
                        act.wait_ge(turned.sem, turned.at(turn, 0))
                        act.wait_ge(routed.sem, routed.at(turn, -2))
                        act.wait_ge(x_low.sem, x_low.at(turn, -2))
                        if second:
                            nc.scalar.activation(xs[:, k, :], c.bank[k][:, :], ACT.Identity, scale=c.w("ln2_w"),
                                                 bias=c.w("ln2_b")).then_inc(xs_made.sem, 1)
                        else:
                            nc.scalar.activation(xs[:, k, :], c.bank[k][:, :], ACT.Copy).then_inc(xs_made.sem, 1)
                        wait_apart(act, xs_made.sem, xs_made.at(turn, 0), c.apart)
                        nc.scalar.activation(XT[:, 0, bass.ds(turn * TOK, TOK)], xs[:, k, :], ACT.Copy, scale=X_UP
                                             ).then_inc(x_high.sem, 1)
                act.wait_ge(powers, 1)
                nc.scalar.activation(tmp[:, :, 0:E], logits[:, :, 0:E], ACT.Exp).then_inc(powers, 1)
                if not second:
                    nc.scalar.activation(tmp[:, :, E:], logits[:, :, E:], ACT.Exp, scale=1 / 0.1).then_inc(powers, 1)
                else:
                    for q in range(TURNS):
                        act.wait_ge(w_turned, q + 1)
                        if q >= 2:
                            act.wait_ge(b2_done, q - 1)
                        nc.scalar.activation(wT[:, q % 2, :], c.bank[4 + q % 2][0:E, :], ACT.Copy).then_inc(wT_made, 1)

            @block.vector
            def _(dve):
                rstd_on_vector(c, dve, shifted, rooted)
                for t in (x_low, w_low, logits_made):
                    dve.sem_inc(t.sem, t.credit)
                with dve.Fori(0, TURNS // 2) as i:
                    for k in range(2):
                        turn = i * 2 + k
                        dve.wait_ge(turned.sem, turned.at(turn, -2))
                        for b in range(QUAD):
                            at = turn * QUAD + b
                            nc.vector.tensor_scalar(xn[:, k, b, :], X[:, bass.ds(at, 1), :], c.stat[:, bass.ds(at, 1), 0],
                                                    c.rstd[:, bass.ds(at, 1)], ALU.subtract, ALU.mult).then_inc(normed.sem, 1)
                        dve.wait_ge(w_high.sem, w_high.at(turn, 0))
                        nc.vector.scalar_tensor_tensor(out=W_flat[:, bass.ds(turn * (2 * cols) + cols, cols)],
                                                       in0=loaded[:, bass.ds(turn * cols, cols)], scalar=W_UP,
                                                       in1=W_flat[:, bass.ds(turn * (2 * cols), cols)],
                                                       op0=ALU.mult, op1=ALU.subtract).then_inc(w_low.sem, 1)
                        dve.wait_ge(x_high.sem, x_high.at(turn, 0))
                        nc.vector.scalar_tensor_tensor(out=XT[:, 1, bass.ds(turn * TOK, TOK)], in0=xs[:, k, :], scalar=X_UP,
                                                       in1=XT[:, 0, bass.ds(turn * TOK, TOK)],
                                                       op0=ALU.mult, op1=ALU.subtract).then_inc(x_low.sem, 1)
                        dve.wait_ge(routed.sem, routed.at(turn, 0))
                        nc.vector.tensor_copy(logits[:, bass.ds(turn * QUAD, QUAD), :],
                                              c.bank[2 + k][:, 0:QUAD * LOGITS].rearrange("p (b l) -> p b l", b=QUAD)
                                              ).then_inc(logits_made.sem, 1)
                dve.wait_ge(logits_made.sem, logits_made.at(TURNS - 1, 0))
                chain = Chain(dve, chain_sem)
                link = chain.link
                by8 = lambda ap: ap[:, :, :].rearrange("p b (s e) -> p (b s) e", e=E)
                R = B * LOGITS // E
                wide = lambda ap: ap.unsqueeze(2).broadcast_to([S, ap.shape[1], E])
                one = best[:, :, :].rearrange("p b k -> p (b k)")[:, 0:R]
                link(nc.vector.reduce_max(one, by8(logits), AX.X))
                nc.vector.tensor_tensor(by8(logits), by8(logits), wide(one), ALU.subtract).then_inc(powers, 1)
                dve.wait_ge(powers, 2 if second else 3)
                link(nc.vector.reduce_sum(one, by8(tmp), AX.X))
                link(nc.vector.reciprocal(one, one))
                link(nc.vector.tensor_tensor(by8(tmp), by8(tmp), wide(one), ALU.mult))
                total = best[:, :, 0]
                if second:
                    p, rank = tmp[:, :, :], c.w("expert_rank").unsqueeze(1).broadcast_to([S, B, E])
                    for found, among in ((tmp2, p), (tmp3, left[:, :, :])):
                        found = found[:, :, :]
                        link(nc.vector.reduce_max(total, among, AX.X))
                        link(nc.vector.tensor_tensor(found, among, wide(total), ALU.is_equal))
                        link(nc.vector.tensor_tensor(found, found, rank, ALU.mult))
                        link(nc.vector.reduce_max(total, found, AX.X))
                        link(nc.vector.tensor_tensor(found, found, wide(total), ALU.is_equal))
                        link(nc.vector.scalar_tensor_tensor(out=left[:, :, :], in0=found, scalar=-2.0, in1=p,
                                                            op0=ALU.mult, op1=ALU.add))
                    link(nc.vector.tensor_tensor(tmp2[:, :, :], tmp2[:, :, :], tmp3[:, :, :], ALU.add))
                    link(nc.vector.tensor_tensor(weight[:, :, :], tmp2[:, :, :], p, ALU.mult))
                    link(nc.vector.reduce_sum(total, weight[:, :, :], AX.X))
                else:
                    link(nc.vector.tensor_tensor(weight[:, :, :], tmp[:, :, 0:E], tmp[:, :, E:], ALU.mult))
                    link(nc.vector.reduce_sum(total, weight[:, :, :], AX.X))
                    link(nc.vector.tensor_scalar(total, total, 1e-9, None, ALU.add))
                link(nc.vector.reciprocal(total, total))
                nc.vector.tensor_tensor(weight[:, :, :], weight[:, :, :], wide(total), ALU.mult).then_inc(weighed, 1)
                dve.wait_ge(weighed, 1)
                if second:
                    for q in range(TURNS):
                        dve.wait_ge(b2_done, q + 1)
                        Xt = c.X[:, q * QUAD:(q + 1) * QUAD, :]
                        nc.vector.tensor_tensor(Xt, Xt, c.bank[6 + q % 2][:, :].rearrange("p (b d) -> p b d", b=QUAD), ALU.add
                                                ).then_inc(b2_added, 1)
                link(nc.vector.tensor_scalar(tmp2[:, :, :], weight[:, :, :], 1 / (W_UP * H_UP), None, ALU.mult))

            @block.tensor
            def _(pe):
                pe.sem_inc(turned.sem, turned.credit)
                pe.sem_inc(routed.sem, routed.credit)
                with pe.Fori(0, TURNS // 2) as i:
                    for k in range(2):
                        turn = i * 2 + k
                        for b in range(QUAD):
                            pe.wait_ge(normed.sem, normed.at(turn, b))
                            last = nc.tensor.transpose(c.bank[k][:, b * S:(b + 1) * S], xn[:, k, b, :], c.w("ident"))
                        last.then_inc(turned.sem, 1)
                        pe.wait_ge(xs_made.sem, xs_made.at(turn, 0))
                        pe.wait_ge(logits_made.sem, logits_made.at(turn, -2))
                        for b in range(QUAD):
                            last = nc.tensor.matmul(c.bank[2 + k][:, b * LOGITS:(b + 1) * LOGITS], xs[:, k, b * S:(b + 1) * S],
                                                    c.w("gate2" if second else "router"), start=True, stop=True)
                        last.then_inc(routed.sem, 1)
                if second:
                    pe.wait_ge(weighed, 1)
                    for t in range(TURNS + 1):
                        if t < TURNS:
                            for b in range(QUAD):
                                last = nc.tensor.transpose(c.bank[4 + t % 2][0:E, b * S:(b + 1) * S], weight[:, t * QUAD + b, :],
                                                           c.w("ident"))
                            last.then_inc(w_turned, 1)
                        if t >= 1:
                            q = t - 1
                            pe.wait_ge(wT_made, q + 1)
                            if q >= 2:
                                pe.wait_ge(b2_added, q - 1)
                            for b in range(QUAD):
                                last = nc.tensor.matmul(c.bank[6 + q % 2][:, b * D:(b + 1) * D], wT[:, q % 2, b * S:(b + 1) * S],
                                                        c.w("b2", E), start=True, stop=True)
                            last.then_inc(b2_done, 1)

        UNITS = E * FC
        factor = tmp2
        act_out = sb("act_out", [128, 2, TOK])
        h = act_out if second else sb("h", [128, 2, TOK])
        H = sb("H", [128, 2, 2, TOK], F16)
        gated = Tally(sem("gated"), UNITS)
        upped = Tally(sem("upped"), UNITS)
        acted = Tally(sem("acted"), UNITS, 2)
        h_made = Tally(sem("h_made"), UNITS, 2)
        h_high = Tally(sem("h_high"), UNITS, 2)
        h_low = Tally(sem("h_low"), UNITS, 2)
        downed = Tally(sem("downed"), UNITS, 2)
        added = Tally(sem("added"), E, 2)
        G_COLS, U_COLS, D_COLS = 0, cols - 2 * F0, cols - F0
        with nc.Block() as block:
            @block.scalar
            def _(act):
                act.sem_inc(acted.sem, acted.credit)
                act.sem_inc(h_high.sem, h_high.credit)
                with act.Fori(0, TURNS) as i:
                    for t in range(UNITS + 1):
                        if t < UNITS:
                            act.wait_ge(gated.sem, gated.at(i, t))
                            read = h_low if second else h_made
                            act.wait_ge(read.sem, read.at(i, t - 2))
                            if second:
                                nc.scalar.activation(act_out[:, t % 2, :], c.bank[t % 2][:, :], ACT.Gelu_apprx_tanh,
                                                     bias=c.w("b1")[:, t:t + 1], scale=1 / (X_UP * W_UP)).then_inc(acted.sem, 1)
                            else:
                                nc.scalar.activation(act_out[:, t % 2, :], c.bank[t % 2][:, :], ACT.Silu,
                                                     scale=1 / (X_UP * W_UP)).then_inc(acted.sem, 1)
                        if t >= 1:
                            u = t - 1
                            made = acted if second else h_made
                            act.wait_ge(made.sem, made.at(i, u))
                            act.wait_ge(downed.sem, downed.at(i, u - 2))
                            nc.scalar.activation(H[:, u % 2, 0, :], h[:, u % 2, :], ACT.Copy, scale=H_UP).then_inc(h_high.sem, 1)

            @block.vector
            def _(dve):
                dve.sem_inc(h_low.sem, h_low.credit)
                dve.sem_inc(added.sem, added.credit)
                if not second:
                    dve.sem_inc(h_made.sem, h_made.credit)
                with dve.Fori(0, TURNS) as i:
                    for t in range(UNITS + 4):
                        if t < UNITS and not second:
                            dve.wait_ge(acted.sem, acted.at(i, t))
                            dve.wait_ge(upped.sem, upped.at(i, t))
                            dve.wait_ge(h_high.sem, h_high.at(i, t - 2))
                            dve.wait_ge(h_low.sem, h_low.at(i, t - 2))
                            nc.vector.scalar_tensor_tensor(out=h[:, t % 2, :], in0=c.bank[2 + t % 2][:, :],
                                                           scalar=1 / (X_UP * W_UP), in1=act_out[:, t % 2, :],
                                                           op0=ALU.mult, op1=ALU.mult).then_inc(h_made.sem, 1)
                        u = t - 1
                        if 0 <= u < UNITS:
                            dve.wait_ge(h_high.sem, h_high.at(i, u))
                            nc.vector.scalar_tensor_tensor(out=H[:, u % 2, 1, :], in0=h[:, u % 2, :], scalar=H_UP,
                                                           in1=H[:, u % 2, 0, :], op0=ALU.mult, op1=ALU.subtract
                                                           ).then_inc(h_low.sem, 1)
                        if t >= FC + 2 and (t - FC - 2) % FC == 1:
                            e = (t - FC - 2) // FC
                            dve.wait_ge(downed.sem, downed.at(i, e * FC + FC - 1))
                            wait_apart(dve, added.sem, added.at(i, e - 1), c.apart)
                            for b in range(QUAD):
                                at = i * QUAD + b
                                Xb = c.X[:, bass.ds(at, 1), :].rearrange("p b d -> p (b d)")
                                last = nc.vector.scalar_tensor_tensor(
                                    out=Xb, in0=c.bank[6 + e % 2][:, b * D:(b + 1) * D],
                                    scalar=factor[:, bass.ds(at, 1), e], in1=Xb, op0=ALU.mult, op1=ALU.add)
                            last.then_inc(added.sem, 1)
                    wait_apart(dve, added.sem, added.at(i, E - 1), c.apart)
                    for b in range(QUAD):
                        nc.vector.bn_stats(c.stats6[:, bass.ds(i * QUAD + b, 1), :], c.X[:, bass.ds(i * QUAD + b, 1), :])

            @block.tensor
            def _(pe):
                pe.sem_inc(downed.sem, downed.credit)
                with pe.Fori(0, TURNS) as i:
                    x = [XT[:, part, bass.ds(i * TOK, TOK)] for part in range(2)]

                    def three_passes(bank, e, at):
                        for k, (w_part, x_part) in enumerate(((0, 0), (0, 1), (1, 0))):
                            last = nc.tensor.matmul(bank[:, :], W[:, e, w_part, at:at + 128], x[x_part],
                                                    start=(k == 0), stop=(k == 2))
                        return last

                    for t in range(UNITS + 2):
                        if t < UNITS:
                            e, f = t // FC, t % FC
                            pe.wait_ge(acted.sem, acted.at(i, t - 2))
                            three_passes(c.bank[t % 2], e, G_COLS + f * 128).then_inc(gated.sem, 1)
                            if not second:
                                pe.wait_ge(h_made.sem, h_made.at(i, t - 2))
                                three_passes(c.bank[2 + t % 2], e, U_COLS + f * 128).then_inc(upped.sem, 1)
                        if t >= 2:
                            u = t - 2
                            e, f = u // FC, u % FC
                            pe.wait_ge(h_low.sem, h_low.at(i, u))
                            if f == 0:
                                pe.wait_ge(added.sem, added.at(i, e - 2))
                            for b in range(QUAD):
                                for k, (h_part, w_part) in enumerate(((0, 0), (0, 1), (1, 0))):
                                    last = nc.tensor.matmul(
                                        c.bank[6 + e % 2][:, b * D:(b + 1) * D], H[:, u % 2, h_part, b * S:(b + 1) * S],
                                        W[:, e, w_part, D_COLS + f * 128:D_COLS + (f + 1) * 128],
                                        start=(f == 0 and b == 0 and k == 0), stop=(f == FC - 1 and k == 2),
                                        skip_group_check=True)
                            last.then_inc(downed.sem, 1)


def ffn1(c):
    nc = c.nc
    RMAX = bass.bass_isa.ReduceOp.max
    CH = F1 // 128
    QMAX = 32767.0
    with ExitStack() as ctx:
        def sb(name, shape, dt=F32):
            return ctx.enter_context(nc.sbuf_tensor(f"G1_{name}", shape, dt))

        take = PartSemaphores(nc, ctx)

        def sem(name):
            return take(f"G1_{name}")

        XT = sb("XT", [D, B * S])
        xn = sb("xn", [S, QUAD, D])
        up = c.arena[:, 0:CH * B * S].rearrange("p (c t) -> p c t", c=CH)
        gate = c.wide[:, :].rearrange("p (c t) -> p c t", c=CH)
        W = c.w1_in[:, :, :]
        WQ = sb("WQ", [128, 3 * CH * 128])
        WT = sb("WT", [128, 3, CH, 128])
        block_max, block_inv = sb("block_max", [128, 36]), sb("block_inv", [128, 36])
        sig = sb("sig", [128, 2, CH, TOK])
        yT = sb("yT", [D, TOK])
        tops = sb("tops", [128, 5, 2 * CH * TURNS])
        top, tops_all = sb("top", [128, 8]), sb("tops_all", [128, 8])
        scale, inv = sb("scale", [128, 8]), sb("inv", [128, 8])
        shifted, rooted = sem("shifted"), sem("rooted")
        w_quantised, w_turned, wt_made = sem("w_quantised"), sem("w_turned"), sem("wt_made")
        normed, turned = Tally(sem("normed"), QUAD), Tally(sem("turned"), 1, 2)
        xt_made = Tally(sem("xt_made"), 1, 2)
        x_topped = Tally(sem("x_topped"), 1, 2)
        top_ready, top_spread = sem("top_ready"), sem("top_spread")
        x_rounded = sem("x_rounded")
        multiplied = Tally(sem("multiplied"), 2 * CH)
        stored = Tally(sem("stored"), 2 * CH, 2 * CH)
        topped = Tally(sem("topped"), 2 * CH, 2 * CH)
        gate_rounded = Tally(sem("gate_rounded"), 1)
        sig_made = Tally(sem("sig_made"), 1)
        sig_used = Tally(sem("sig_used"), 1, 2)
        o_rounded = sem("o_rounded")
        down_done, yT_made = Tally(sem("down_done"), 1), Tally(sem("yT_made"), 1, 1)
        y_turned, added = Tally(sem("y_turned"), 1, 1), Tally(sem("added"), 1, 1)
        chain_sem, scales_ready = sem("dve_chain"), sem("scales_ready")
        carried = sb("carried", [128, 4])
        block = ctx.enter_context(nc.Block())
        X0, UP, GATE, GS, O = range(5)

        @block.gpsimd
        def _(pool):
            for k in range(4):
                pool.wait_ge(top_ready, k + 1)
                at, width = ((X0, 1), (UP, 2), (GS, 1), (O, 1))[k]
                nc.gpsimd.partition_all_reduce(tops_all[:, at:at + width], top[:, at:at + width], 128, RMAX
                                               ).then_inc(top_spread, 1)

        @block.scalar
        def _(act):
            rstd_on_scalar(c, act, shifted, rooted)
            for k in range(3):
                act.wait_ge(w_turned, k + 1)
                nc.scalar.activation(WT[:, k, :, :], c.bank[2 + k][:, 0:CH * 128].rearrange("p (c o) -> p c o", c=CH), ACT.Copy
                                     ).then_inc(wt_made, 1)
            act.sem_inc(xt_made.sem, xt_made.credit)
            act.sem_inc(stored.sem, stored.credit)
            act.sem_inc(yT_made.sem, yT_made.credit)
            with act.Fori(0, TURNS // 2) as j:
                for r in range(2):
                    act.wait_ge(turned.sem, 2 * j + r + 1 + turned.credit)
                    nc.scalar.activation(XT[:, bass.ds((2 * j + r) * TOK, TOK)], c.bank[r][:, :], ACT.Copy).then_inc(xt_made.sem, 1)
            with act.Fori(0, TURNS) as i:
                for k in range(2 * CH):
                    act.wait_ge(multiplied.sem, multiplied.at(i, k))
                    dst = (up, gate)[k // CH][:, k % CH, bass.ds(i * TOK, TOK)]
                    nc.scalar.activation(dst, c.bank[2 + k][:, :], ACT.Copy).then_inc(stored.sem, 1)
            with act.Fori(0, TURNS // 2) as j:
                for r in range(2):
                    act.wait_ge(gate_rounded.sem, 2 * j + r + 1)
                    act.wait_ge(sig_used.sem, 2 * j + r + 1)
                    nc.scalar.activation(sig[:, r, :, :], gate[:, :, bass.ds((2 * j + r) * TOK, TOK)], ACT.Sigmoid,
                                         scale=scale[:, GATE:GATE + 1]).then_inc(sig_made.sem, 1)
            with act.Fori(0, TURNS) as i:
                act.wait_ge(down_done.sem, down_done.at(i, 0))
                act.wait_ge(y_turned.sem, y_turned.at(i, -1))
                nc.scalar.activation(yT[:, :], c.bank[0][:, :], ACT.Copy, scale=scale[:, O:O + 1]).then_inc(yT_made.sem, 1)

        @block.vector
        def _(dve):
            chain = Chain(dve, chain_sem)
            link = chain.link
            rstd_on_vector(c, dve, shifted, rooted)
            for t in (x_topped, topped, sig_used, added):
                dve.sem_inc(t.sem, t.credit)
            dve.wait_ge(c.w1_sem, 48)
            w3 = WQ[:, :].rearrange("p (b w) -> p b w", w=32)
            spread = lambda ap: ap[:, :].unsqueeze(2).broadcast_to([128, 36, 32])
            link(nc.vector.tensor_reduce(block_max[:, :], W, AX.X, ALU.max, apply_absolute_value=True))
            link(nc.vector.tensor_scalar(block_max[:, :], block_max[:, :], 1 / 7.0, 1e-12, ALU.mult, ALU.max))
            link(nc.vector.reciprocal(block_inv[:, :], block_max[:, :]))
            link(nc.vector.tensor_tensor(w3, W, spread(block_inv), ALU.mult))
            link(nc.vector.tensor_scalar(w3, w3, ROUND, ROUND + 7.0, ALU.add, ALU.min))
            link(nc.vector.tensor_scalar(w3, w3, ROUND - 8.0, ROUND, ALU.max, ALU.subtract))
            nc.vector.tensor_tensor(w3, w3, spread(block_max), ALU.mult).then_inc(w_quantised, 1)

            with dve.Fori(0, TURNS // 2) as j:
                for r in range(2):
                    turn = 2 * j + r
                    dve.wait_ge(turned.sem, turn + turned.credit)
                    for b in range(QUAD):
                        at = turn * QUAD + b
                        nc.vector.tensor_scalar(xn[:, b, :], c.X[:, bass.ds(at, 1), :], c.stat[:, bass.ds(at, 1), 0],
                                                c.rstd[:, bass.ds(at, 1)], ALU.subtract, ALU.mult).then_inc(normed.sem, 1)
                    dve.wait_ge(xt_made.sem, turn + 1 + xt_made.credit)
                    nc.vector.tensor_reduce(tops[:, X0, bass.ds(turn, 1)], XT[:, bass.ds(turn * TOK, TOK)], AX.X, ALU.max,
                                            apply_absolute_value=True).then_inc(x_topped.sem, 1)

            def find_scales(first, last, count, carried, k):
                nc.vector.reduce_max(top[:, first:last], tops[:, first:last, 0:count], AX.X).then_inc(top_ready, 1)
                dve.wait_ge(top_spread, k + 1)
                s = scale[:, first:last]
                link(nc.vector.tensor_tensor(s, tops_all[:, first:last], carried, ALU.mult))
                link(nc.vector.tensor_scalar(s, s, 1 / QMAX, 1e-12, ALU.mult, ALU.max))
                link(nc.vector.reciprocal(inv[:, first:last], s))
                link(nc.vector.tensor_tensor(inv[:, first:last], inv[:, first:last], carried, ALU.mult))

            def rounded(dst, who):
                return nc.vector.tensor_scalar(dst, dst, inv[:, who:who + 1], ROUND, ALU.mult, ALU.add)

            def settled(dst):
                return nc.vector.tensor_scalar(dst, dst, ROUND + QMAX, ROUND, ALU.min, ALU.subtract)

            link(nc.vector.memset(carried[:, :], 1.0))
            dve.wait_ge(x_topped.sem, TURNS + x_topped.credit)
            find_scales(X0, X0 + 1, TURNS, carried[:, 0:1], 0)
            dve.wait_ge(xt_made.sem, TURNS + xt_made.credit)
            for i in range(TURNS):
                cols = XT[:, i * TOK:(i + 1) * TOK]
                link(rounded(cols, X0))
                settled(cols).then_inc(x_rounded, 1)
            with dve.Fori(0, TURNS) as i:
                for k in range(2 * CH):
                    dve.wait_ge(stored.sem, stored.at(i, k))
                    src = (up, gate)[k // CH][:, k % CH, bass.ds(i * TOK, TOK)]
                    nc.vector.tensor_reduce(tops[:, UP + k // CH, bass.ds(i * CH + k % CH, 1)], src, AX.X, ALU.max,
                                            apply_absolute_value=True).then_inc(topped.sem, 1)
            dve.wait_ge(topped.sem, (TURNS + 1) * 2 * CH)
            dve.wait_ge(stored.sem, (TURNS + 1) * 2 * CH)
            link(nc.vector.tensor_copy(carried[:, 0:2], scale[:, X0:X0 + 1].broadcast_to([128, 2])))
            find_scales(UP, UP + 2, TURNS * CH, carried[:, 0:2], 1)
            nc.vector.tensor_scalar(carried[:, 2:3], scale[:, GATE:GATE + 1], 1 / 65536.0, None, ALU.mult
                                    ).then_inc(scales_ready, 1)

            steps = Chain(dve, sem("sigmoid_steps"), 12)
            with dve.Fori(0, TURNS // 2) as j:
                steps.start(j)
                for r in range(2):
                    turn = 2 * j + r
                    g, u = gate[:, :, bass.ds(turn * TOK, TOK)], up[:, :, bass.ds(turn * TOK, TOK)]
                    sg = sig[:, r, :, :]
                    steps.link(rounded(g, GATE))
                    settled(g).then_inc(gate_rounded.sem, 1)
                    steps.link(rounded(u, UP))
                    steps.link(settled(u))
                    dve.wait_ge(sig_made.sem, turn + 1)
                    steps.link(nc.vector.tensor_scalar(sg, sg, 65536.0, ROUND, ALU.mult, ALU.add))
                    steps.link(nc.vector.tensor_scalar(sg, sg, ROUND + 65535.0, ROUND, ALU.min, ALU.subtract))
                    nc.vector.tensor_tensor(g, g, sg, ALU.mult).then_inc(sig_used.sem, 1)
                    dve.wait_ge(sig_used.sem, turn + 1 + sig_used.credit)
                    steps.link(nc.vector.tensor_reduce(tops[:, GS, bass.ds(turn, 1)], g, AX.XY, ALU.max,
                                                       apply_absolute_value=True))
            assert steps.n == steps.per
            find_scales(GS, GS + 1, TURNS, carried[:, 2:3], 2)

            steps = Chain(dve, sem("product_steps"), 4)
            with dve.Fori(0, TURNS) as i:
                steps.start(i)
                g, u = gate[:, :, bass.ds(i * TOK, TOK)], up[:, :, bass.ds(i * TOK, TOK)]
                steps.link(rounded(g, GS))
                steps.link(settled(g))
                steps.link(nc.vector.tensor_tensor(g, g, u, ALU.mult))
                steps.link(nc.vector.tensor_reduce(tops[:, O, bass.ds(i, 1)], g, AX.XY, ALU.max, apply_absolute_value=True))
            assert steps.n == steps.per
            link(nc.vector.tensor_tensor(carried[:, 3:4], scale[:, GS:GS + 1], scale[:, UP:UP + 1], ALU.mult))
            find_scales(O, O + 1, TURNS, carried[:, 3:4], 3)

            steps = Chain(dve, sem("o_steps"), 1)
            with dve.Fori(0, TURNS) as i:
                steps.start(i)
                g = gate[:, :, bass.ds(i * TOK, TOK)]
                steps.link(rounded(g, O))
                settled(g).then_inc(o_rounded, 1)
            with dve.Fori(0, TURNS) as i:
                dve.wait_ge(y_turned.sem, y_turned.at(i, 0))
                Xt = c.X[:, bass.ds(i * QUAD, QUAD), :]
                nc.vector.tensor_tensor(Xt, Xt, c.bank[1][:, :].rearrange("p (b d) -> p b d", b=QUAD), ALU.add
                                        ).then_inc(added.sem, 1)
                wait_apart(dve, added.sem, added.at(i, 0), c.apart)
                for b in range(QUAD):
                    nc.vector.bn_stats(c.stats6[:, bass.ds(i * QUAD + b, 1), :], c.X[:, bass.ds(i * QUAD + b, 1), :])

        @block.tensor
        def _(pe):
            for t in (turned, y_turned):
                pe.sem_inc(t.sem, t.credit)
            pe.wait_ge(w_quantised, 1)
            for k in range(3):
                for q in range(CH):
                    at = (k * CH + q) * 128
                    last = nc.tensor.transpose(c.bank[2 + k][:, q * 128:(q + 1) * 128], WQ[:, at:at + 128], c.w("ident"))
                last.then_inc(w_turned, 1)
            pe.wait_ge(wt_made, 3)
            with pe.Fori(0, TURNS // 2) as j:
                for r in range(2):
                    turn = 2 * j + r
                    pe.wait_ge(xt_made.sem, turn + 1)
                    for b in range(QUAD):
                        pe.wait_ge(normed.sem, turn * QUAD + b + 1)
                        last = nc.tensor.transpose(c.bank[r][:, b * S:(b + 1) * S], xn[:, b, :], c.w("ident"))
                    last.then_inc(turned.sem, 1)
            pe.wait_ge(x_rounded, TURNS)
            with pe.Fori(0, TURNS) as i:
                for k in range(2 * CH):
                    pe.wait_ge(stored.sem, stored.at(i, k - 2 * CH))
                    nc.tensor.matmul(c.bank[2 + k][:, :], WT[:, k // CH, k % CH, :], XT[:, bass.ds(i * TOK, TOK)],
                                     start=True, stop=True).then_inc(multiplied.sem, 1)
            with pe.Fori(0, TURNS) as i:
                pe.wait_ge(o_rounded, i + 1)
                pe.wait_ge(yT_made.sem, yT_made.at(i, -1))
                for q in range(CH):
                    last = nc.tensor.matmul(c.bank[0][:, :], WT[:, 2, q, :], gate[:, q, bass.ds(i * TOK, TOK)],
                                            start=(q == 0), stop=(q == CH - 1))
                last.then_inc(down_done.sem, 1)
                pe.wait_ge(yT_made.sem, yT_made.at(i, 0))
                pe.wait_ge(added.sem, added.at(i, -1))
                for b in range(QUAD):
                    last = nc.tensor.transpose(c.bank[1][:, b * S:(b + 1) * S], yT[:, b * S:(b + 1) * S], c.w("ident"))
                last.then_inc(y_turned.sem, 1)


def many_heads(c, n, own, mask):
    nc = c.nc
    NK = S if own else KEYS
    UNITS = QUAD * GROUPS
    scale = 1.0 if mask == "pairs" else DH ** -0.5
    with ExitStack() as ctx:
        def sb(name, shape, dt=F32):
            return ctx.enter_context(nc.sbuf_tensor(f"{n}_{name}", shape, dt))

        take = PartSemaphores(nc, ctx)

        def sem(name):
            return take(f"{n}_{name}")

        xn, xnT = sb("xn", [S, QUAD, D]), sb("xnT", [D, TOK])
        normed_once = sb("normed_once", [S, 2, QUAD, D]) if own else None
        rstd_twice = sb("rstd_twice", [S, B]) if own else c.rstd
        keysT = xnT if own else sb("ctxT", [D, QUAD * KEYS])
        halves = sb("halves", [D, 2, TOK], F16)
        QS, KS = sb("QS", [128, 2, GROUPS, TOK], F16), sb("KS", [128, 2, GROUPS, QUAD * NK], F16)
        V = sb("V", [NK, 2, QUAD, HEADS, 32])
        neg_max = sb("neg_max", [S, 4, PER], BF16)
        P, PT = sb("P", [S, 2, PER * NK]), sb("PT", [NK, 2, PER * S])
        OT = sb("OT", [128, 2, GROUPS * S])
        rcp = sb("rcp", [S, 2, HEADS])
        out, outT = sb("out", [S, 2, HEADS, DH]), sb("outT", [D, 2, S])
        spread = c.w("spread").bitcast(F16).rearrange("d (w g p) -> d w g p", w=4, g=GROUPS)
        if mask:
            shut = c.wide[:, B * (D + KEYS):B * (D + KEYS) + B * KEYS // 2].bitcast(BF16)
            words = B * KEYS // (4 if mask == "pairs" else 1)
            raw_words = c.wide[:, B * D:B * D + words].bitcast(I32)
            raw = c.wide[:, B * D:B * D + words].bitcast(U8 if mask == "pairs" else I32)
        shifted, rooted = sem("shifted"), sem("rooted")
        rooted_twice = sem("rooted_twice")
        mask_in, mask_made, v_ready = sem("mask_in"), sem("mask_made"), sem("v_ready")
        X_T, QUERIES, Q_GROUP, KEYS_, K_GROUP, VALUES = 0, 1, 2, 2 + GROUPS, 3 + GROUPS, 3 + 2 * GROUPS
        ITEMS = VALUES + 1
        ctx_in = Tally(sem("ctx_in"), 16)
        normed = Tally(sem("normed"), QUAD)
        projected = Tally(sem("projected"), ITEMS, 1)
        xnT_made = Tally(sem("xnT_made"), 1)
        high_made = Tally(sem("high_made"), 2)
        low_made = Tally(sem("low_made"), 2)
        qk_made = Tally(sem("qk_made"), 2 * GROUPS)
        v_made = Tally(sem("v_made"), 1, 1)
        scored = Tally(sem("scored"), UNITS)
        maxed = Tally(sem("maxed"), UNITS)
        lessened = Tally(sem("lessened"), UNITS)
        exped = Tally(sem("exped"), UNITS, 4)
        p_turned = Tally(sem("p_turned"), UNITS, 2)
        pT_made = Tally(sem("pT_made"), UNITS, 1)
        pv_done = Tally(sem("pv_done"), UNITS, 2)
        oT_made = Tally(sem("oT_made"), QUAD, 1)
        o_turned = Tally(sem("o_turned"), QUAD, 2)
        inverted = Tally(sem("inverted"), QUAD)
        out_made = Tally(sem("out_made"), QUAD)
        out_turned = Tally(sem("out_turned"), QUAD, 2)
        outT_made = Tally(sem("outT_made"), QUAD)
        o_done = Tally(sem("o_done"), QUAD, 2)
        added = Tally(sem("added"), QUAD, 1)
        block = ctx.enter_context(nc.Block())
        S_BANK, PT_BANK, OT_BANK, TAIL, PROJ = c.bank[0:4], c.bank[4], c.bank[5], c.bank[6], c.bank[7]
        STEP = {1: X_T, 3: QUERIES, 9: KEYS_, 14: VALUES}
        STEP.update({4 + g: Q_GROUP + g for g in range(GROUPS)})
        STEP.update({10 + g: K_GROUP + g for g in range(GROUPS)})

        class Slot:

            def __init__(self, s, parity, project, attend, finish):
                self.s, self.parity, self.project, self.attend, self.finish = s, parity, project, attend, finish
                self.turn = s - 1
                self.steps = UNITS if project or attend else 6

            def runs(self, k):
                return self.attend if k >= 0 else self.finish

            def at(self, tally, k):
                if k + 1 + tally.credit > 0:
                    return tally.at(self.turn, k)
                return tally.at(self.turn - 1, k + tally.per)

            def place(self, k):
                return 1 - self.parity if k >= 0 else self.parity

            def sequence(self, t, behind):
                b, rest = (t - behind) // GROUPS, (t - behind) % GROUPS
                return b if rest == 0 and self.runs(b) else None

        def slots(eng, run):
            run(Slot(0, 0, True, False, False))
            run(Slot(1, 1, True, True, False))
            with eng.Fori(0, (TURNS - 2) // 2) as j:
                run(Slot(j * 2 + 2, 0, True, True, True))
                run(Slot(j * 2 + 3, 1, True, True, True))
            run(Slot(TURNS, 0, False, True, True))
            run(Slot(TURNS + 1, 1, False, False, True))

        @block.sync
        def _(sp):
            if mask:
                sp.wait_ge(c.wide_in, 32)
                if mask == "pairs":
                    sp.dma_start(raw_words, c.ins["mask3"]).then_inc(mask_in, 16)
                else:
                    sp.dma_start(raw_words, c.ins["mask2"].partition_broadcast(S)).then_inc(mask_in, 16)
            if not own:
                with sp.Fori(0, TURNS) as i:
                    sp.wait_ge(projected.sem, projected.at(i, -1))
                    sp.dma_start(keysT[:, :], c.ins["ctxT"][:, bass.ds(i * (QUAD * KEYS), QUAD * KEYS)]
                                 ).then_inc(ctx_in.sem, 16)
            if mask == "keys":
                sp.wait_ge(c.arena_in, 16 * (2 + E))
                load_experts(c, sp, True, c.arena2_in)

        @block.gpsimd
        def _(pool):
            nc.gpsimd.memset(V[:, :, :, :, :], 0.0).then_inc(v_ready, 1)
            pool.wait_ge(v_ready, 1)
            nc.gpsimd.memset(V[:, :, :, :, DH:DH + 1], 1.0).then_inc(v_ready, 1)

        @block.scalar
        def _(act):
            rstd_on_scalar(c, act, shifted, rooted)
            if own:
                act.wait_ge(rooted_twice, 1)
                nc.scalar.activation(rstd_twice[:, :], rstd_twice[:, :], ACT.Sqrt).then_inc(rooted_twice, 1)
            for t in (exped, pT_made, oT_made):
                act.sem_inc(t.sem, t.credit)

            def item_read(slot, item):
                if item == X_T:
                    act.wait_ge(projected.sem, projected.at(slot.s, X_T))
                    if own:
                        nc.scalar.activation(xnT[:, :], PROJ[:, :], ACT.Identity, scale=c.w("ln1_w"), bias=c.w("ln1_b")
                                             ).then_inc(xnT_made.sem, 1)
                    else:
                        nc.scalar.activation(xnT[:, :], PROJ[:, :], ACT.Copy).then_inc(xnT_made.sem, 1)
                if item in (QUERIES, KEYS_):
                    bias, width = ("_bq", TOK) if item == QUERIES else ("_bk", QUAD * NK)
                    act.wait_ge(projected.sem, projected.at(slot.s, item))
                    nc.scalar.activation(halves[:, 0, 0:width], PROJ[:, 0:width], ACT.Identity, bias=c.w(n + bias)
                                         ).then_inc(high_made.sem, 1)

            def run(slot):
                for t in range(slot.steps):
                    if slot.project and t - 1 in STEP:
                        item_read(slot, STEP[t - 1])
                    u = t - 1
                    if slot.runs(u):
                        act.wait_ge(lessened.sem, slot.at(lessened, u))
                        act.wait_ge(p_turned.sem, slot.at(p_turned, u - 2))
                        nc.scalar.activation(P[:, u % 2, :], S_BANK[u % 4][:, 0:PER * NK], ACT.Exp, scale=scale
                                             ).then_inc(exped.sem, 1)
                    b = slot.sequence(t, 8)
                    if b is not None:
                        act.wait_ge(out_turned.sem, slot.at(out_turned, b))
                        act.wait_ge(o_done.sem, slot.at(o_done, b - 2))
                        nc.scalar.activation(outT[:, b % 2, :], TAIL[:, 0:S], ACT.Copy).then_inc(outT_made.sem, 1)
                    u = t - 2
                    if slot.runs(u):
                        act.wait_ge(p_turned.sem, slot.at(p_turned, u))
                        act.wait_ge(pv_done.sem, slot.at(pv_done, u - 2))
                        nc.scalar.activation(PT[:, u % 2, :], PT_BANK[0:NK, :], ACT.Copy).then_inc(pT_made.sem, 1)
                    b = slot.sequence(t, 6)
                    if b is not None:
                        act.wait_ge(pv_done.sem, slot.at(pv_done, 4 * b + 3))
                        act.wait_ge(o_turned.sem, slot.at(o_turned, b - 2))
                        nc.scalar.activation(OT[:, b % 2, :], OT_BANK[:, :], ACT.Copy).then_inc(oT_made.sem, 1)

            slots(act, run)

        @block.vector
        def _(dve):
            rstd_on_vector(c, dve, shifted, rooted)
            setup = Chain(dve, sem("setup_chain"))
            if own:
                setup.link(nc.vector.tensor_tensor(rstd_twice[:, :], c.rstd[:, :], c.rstd[:, :], ALU.mult))
                setup.link(nc.vector.tensor_tensor(rstd_twice[:, :], rstd_twice[:, :], c.stat[:, :, 1], ALU.mult))
                nc.vector.tensor_scalar(rstd_twice[:, :], rstd_twice[:, :], EPS, None, ALU.add).then_inc(rooted_twice, 1)
                dve.wait_ge(rooted_twice, 2)
                setup.link(nc.vector.reciprocal(rstd_twice[:, :], rstd_twice[:, :]))
                setup.link(nc.vector.tensor_tensor(rstd_twice[:, :], rstd_twice[:, :], c.rstd[:, :], ALU.mult))
            for t in (added, v_made):
                dve.sem_inc(t.sem, t.credit)

            def norm(slot):
                for b in range(QUAD):
                    at = slot.s * QUAD + b
                    nc.vector.tensor_scalar(xn[:, b, :], c.X[:, bass.ds(at, 1), :], c.stat[:, bass.ds(at, 1), 0],
                                            rstd_twice[:, bass.ds(at, 1)], ALU.subtract, ALU.mult).then_inc(normed.sem, 1)

            def norm_once(slot):
                if slot.finish:
                    dve.wait_ge(added.sem, added.at(slot.turn, -1))
                for b in range(QUAD):
                    at = slot.s * QUAD + b
                    nc.vector.tensor_scalar(normed_once[:, slot.parity, b, :], c.X[:, bass.ds(at, 1), :],
                                            c.stat[:, bass.ds(at, 1), 0], c.rstd[:, bass.ds(at, 1)], ALU.subtract, ALU.mult)

            def item_read(slot, item):
                dve.wait_ge(projected.sem, projected.at(slot.s, item))
                if item in (QUERIES, KEYS_):
                    k, bias, width = (0, "_bq", TOK) if item == QUERIES else (1, "_bk", QUAD * NK)
                    dve.wait_ge(high_made.sem, high_made.at(slot.s, k))
                    nc.vector.scalar_tensor_tensor(out=halves[:, 1, 0:width], in0=PROJ[:, 0:width], scalar=c.w(n + bias),
                                                   in1=halves[:, 0, 0:width], op0=ALU.add, op1=ALU.subtract
                                                   ).then_inc(low_made.sem, 1)
                elif item == VALUES:
                    if not slot.attend:
                        dve.wait_ge(v_ready, 2)
                    for b in range(QUAD):
                        last = nc.vector.tensor_tensor(
                            V[:, slot.parity, b, :, 0:DH], PROJ[0:NK, b * D:(b + 1) * D].rearrange("k (h d) -> k h d", h=HEADS),
                            c.w(n + "_bv", NK).rearrange("k (h d) -> k h d", h=HEADS), ALU.add)
                    last.then_inc(v_made.sem, 1)
                elif item != X_T:
                    dst, g, width = (QS, item - Q_GROUP, TOK) if item < KEYS_ else (KS, item - K_GROUP, QUAD * NK)
                    nc.vector.tensor_copy(dst[:, slot.parity, g, :], PROJ[:, 0:width]).then_inc(qk_made.sem, 1)

            def run(slot):
                for t in range(slot.steps):
                    if slot.project and t - 1 in STEP and STEP[t - 1] != X_T:
                        item_read(slot, STEP[t - 1])
                    if slot.runs(t):
                        dve.wait_ge(scored.sem, slot.at(scored, t))
                        nc.vector.tensor_reduce(neg_max[:, t % 4, :],
                                                S_BANK[t % 4][:, 0:PER * NK].rearrange("q (j k) -> q j k", j=PER),
                                                AX.X, ALU.max, negate=True).then_inc(maxed.sem, 1)
                    if slot.project and t == 0:
                        norm(slot)
                    if slot.project and own and t == 6:
                        norm_once(slot)
                    b = slot.sequence(t, 7)
                    if b is not None:
                        dve.wait_ge(o_turned.sem, slot.at(o_turned, b))
                        dve.wait_ge(out_turned.sem, slot.at(out_turned, b - 2))
                        by_head = TAIL[:, :].rearrange("q (h w) -> q h w", h=HEADS)
                        nc.vector.reciprocal(rcp[:, b % 2, :], by_head[:, :, DH]).then_inc(inverted.sem, 1)
                        dve.wait_ge(inverted.sem, slot.at(inverted, b))
                        nc.vector.tensor_tensor(out[:, b % 2, :, :], by_head[:, :, 0:DH],
                                                rcp[:, b % 2, :].unsqueeze(2).broadcast_to([S, HEADS, DH]), ALU.mult
                                                ).then_inc(out_made.sem, 1)
                    b = slot.sequence(t, 9)
                    if b is not None:
                        at = (slot.turn if b >= 0 else slot.turn - 1) * QUAD + b % QUAD
                        X, result = c.X[:, bass.ds(at, 1), :], TAIL[:, S:2 * S]
                        dve.wait_ge(o_done.sem, slot.at(o_done, b))
                        if own:
                            h = c.inner[:, bass.ds(at, 1), :]
                            nc.vector.tensor_tensor(h, normed_once[:, slot.place(b), b % QUAD, :], result, ALU.add
                                                    ).then_inc(added.sem, 1)
                            wait_apart(dve, added.sem, slot.at(added, b), c.apart)
                            nc.vector.bn_stats(c.stats6[:, bass.ds(at, 1), :], h)
                            nc.vector.tensor_tensor(X, X, h, ALU.add)
                        else:
                            nc.vector.tensor_tensor(X, X, result, ALU.add).then_inc(added.sem, 1)
                            wait_apart(dve, added.sem, slot.at(added, b), c.apart)
                            nc.vector.bn_stats(c.stats6[:, bass.ds(at, 1), :], X)

            if mask:
                dve.wait_ge(mask_in, 16)
            if mask == "keys":
                nc.vector.tensor_scalar(shut[:, :], raw, 0.0, SHUT, ALU.is_equal, ALU.mult).then_inc(mask_made, 1)
            if mask == "pairs":
                nc.vector.tensor_scalar(shut[:, :], raw, SHUT, None, ALU.mult).then_inc(mask_made, 1)
            slots(dve, run)

        @block.tensor
        def _(pe):
            for t in (projected, p_turned, pv_done, o_turned, out_turned, o_done):
                pe.sem_inc(t.sem, t.credit)

            def item_made(slot, item):
                s = slot.s
                if item == X_T:
                    pe.wait_ge(v_made.sem, v_made.at(s, -1))
                    for b in range(QUAD):
                        pe.wait_ge(normed.sem, normed.at(s, b))
                        last = nc.tensor.transpose(PROJ[:, b * S:(b + 1) * S], xn[:, b, :], c.w("ident"))
                elif item in (QUERIES, KEYS_):
                    if item == QUERIES:
                        pe.wait_ge(xnT_made.sem, xnT_made.at(s, 0))
                    else:
                        pe.wait_ge(qk_made.sem, qk_made.at(s, GROUPS - 1))
                        if not own:
                            pe.wait_ge(ctx_in.sem, ctx_in.at(s, 15))
                    w, src, width = ("_wq", xnT, TOK) if item == QUERIES else ("_wk", keysT, QUAD * NK)
                    last = nc.tensor.matmul(PROJ[:, 0:width], c.w(n + w), src[:, :], start=True, stop=True)
                elif item == VALUES:
                    pe.wait_ge(qk_made.sem, qk_made.at(s, 2 * GROUPS - 1))
                    for b in range(QUAD):
                        last = nc.tensor.matmul(PROJ[0:NK, b * D:(b + 1) * D], keysT[:, b * NK:(b + 1) * NK],
                                                c.w(n + "_wv"), start=True, stop=True)
                else:
                    k, g, width = (0, item - Q_GROUP, TOK) if item < KEYS_ else (1, item - K_GROUP, QUAD * NK)
                    if g == 0:
                        pe.wait_ge(low_made.sem, low_made.at(s, k))
                    else:
                        pe.wait_ge(qk_made.sem, qk_made.at(s, k * GROUPS + g - 1))
                    for half in range(2):
                        last = nc.tensor.matmul(PROJ[:, 0:width], spread[:, 2 * k + half, g, :], halves[:, half, 0:width],
                                                start=(half == 0), stop=(half == 1))
                last.then_inc(projected.sem, 1)

            def run(slot):
                here, before = slot.place(0), slot.place(-1)
                for t in range(slot.steps):
                    if slot.runs(t):
                        b, j = t // PER, t % PER
                        rows = slice(32 * j, 32 * j + 32)
                        if t == 0:
                            pe.wait_ge(qk_made.sem, qk_made.at(slot.turn, 2 * GROUPS - 1))
                            if mask and not slot.finish:
                                pe.wait_ge(mask_made, 1)
                        pe.wait_ge(exped.sem, slot.at(exped, t - 4))
                        for g in range(GROUPS):
                            last = nc.tensor.matmul(S_BANK[t % 4][:, g * NK:(g + 1) * NK], QS[rows, here, g, b * S:(b + 1) * S],
                                                    KS[rows, here, g, b * NK:(b + 1) * NK], start=(g == 0), stop=False,
                                                    skip_group_check=True)
                        if mask:
                            at = (slot.turn * QUAD + b) * NK
                            last = nc.tensor.matmul(S_BANK[t % 4][:, 0:PER * NK].rearrange("q (j k) -> q j k", j=PER), c.ident16[:, :],
                                                    shut[:, bass.ds(at, NK)].unsqueeze(1).broadcast_to([S, PER, NK]),
                                                    start=False, stop=True, skip_group_check=True)
                        last.then_inc(scored.sem, 1)
                    u = t - 1
                    if slot.runs(u):
                        pe.wait_ge(maxed.sem, slot.at(maxed, u))
                        nc.tensor.matmul(S_BANK[u % 4][:, 0:PER * NK].rearrange("q (j k) -> q j k", j=PER), c.ident16[:, :],
                                         neg_max[:, u % 4, :].unsqueeze(2).broadcast_to([S, PER, NK]),
                                         start=False, stop=True, skip_group_check=True).then_inc(lessened.sem, 1)
                    b = slot.sequence(t, 7)
                    if b is not None:
                        pe.wait_ge(oT_made.sem, slot.at(oT_made, b))
                        pe.wait_ge(added.sem, slot.at(added, b - 1))
                        for g in range(GROUPS):
                            last = nc.tensor.transpose(TAIL[:, g * S:(g + 1) * S], OT[:, b % 2, g * S:(g + 1) * S], c.w("ident"))
                        last.then_inc(o_turned.sem, 1)
                    b = slot.sequence(t, 8)
                    if b is not None:
                        pe.wait_ge(out_made.sem, slot.at(out_made, b))
                        nc.tensor.transpose(TAIL[:, 0:S], out[:, b % 2, :, :].rearrange("q h d -> q (h d)"), c.w("ident")
                                            ).then_inc(out_turned.sem, 1)
                    b = slot.sequence(t, 9)
                    if b is not None:
                        pe.wait_ge(outT_made.sem, slot.at(outT_made, b))
                        nc.tensor.matmul(TAIL[:, S:2 * S], outT[:, b % 2, :], c.w(n + "_wo"), start=True, stop=False)
                        nc.tensor.matmul(TAIL[:, S:2 * S], c.ones_row[:, 0:S], c.w(n + "_bo", 1), start=False, stop=True
                                         ).then_inc(o_done.sem, 1)
                    u = t - 2
                    if slot.runs(u):
                        pe.wait_ge(exped.sem, slot.at(exped, u))
                        pe.wait_ge(pT_made.sem, slot.at(pT_made, u - 1))
                        for j in range(PER):
                            last = nc.tensor.transpose(PT_BANK[0:NK, j * S:(j + 1) * S], P[:, u % 2, j * NK:(j + 1) * NK],
                                                       c.w("ident"))
                        last.then_inc(p_turned.sem, 1)
                    u = t - 3
                    if slot.runs(u):
                        b, j = u // PER, u % PER
                        pe.wait_ge(pT_made.sem, slot.at(pT_made, u))
                        if u == 0:
                            pe.wait_ge(v_made.sem, v_made.at(slot.turn, 0))
                        if j == 0:
                            pe.wait_ge(oT_made.sem, slot.at(oT_made, b - 1))
                        for g in range(GROUPS):
                            last = nc.tensor.matmul(OT_BANK[32 * g:32 * g + 32, j * S:(j + 1) * S],
                                                    V[:, slot.place(u), b % QUAD, GROUPS * j + g, :],
                                                    PT[:, u % 2, g * S:(g + 1) * S], start=True, stop=True)
                        last.then_inc(pv_done.sem, 1)
                    if slot.project and t in STEP:
                        item_made(slot, STEP[t])

            slots(pe, run)


def ffn3(c):
    nc = c.nc
    RADD = bass.bass_isa.ReduceOp.add
    BATCH = 8
    LOOPS = B // BATCH
    with ExitStack() as ctx:
        def sb(name, shape, dt=F32):
            return ctx.enter_context(nc.sbuf_tensor(f"G3_{name}", shape, dt))

        take = PartSemaphores(nc, ctx)

        def sem(name):
            return take(f"G3_{name}")

        W = c.w3_in
        W2 = sb("W2", [128, 3, F0])
        WQ = sb("WQ", [128, 3, F0], BF16)
        WT = sb("WT", [128, 3, F0], BF16)
        sums, sums_all, mean, mean_inv = sb("sums", [128, 3]), sb("sums_all", [128, 3]), sb("mean", [128, 3]), sb("mean_inv", [128, 3])
        xn, xq, xqT = sb("xn", [S, 2, D]), sb("xq", [S, 2, D], BF16), sb("xqT", [D, 2, S], BF16)
        xcol, hcol = sb("xcol", [S, 4, 8]), sb("hcol", [S, 4, 8])
        gate = sb("gate", [S, 2, F0])
        h, hq, hqT = sb("h", [S, 2, F0]), sb("hq", [S, 2, F0], BF16), sb("hqT", [128, 2, F0], BF16)
        shifted, rooted = sem("shifted"), sem("rooted")
        summed, summed_all, w_made, w_turned, wt_made = (sem(x) for x in ("summed", "summed_all", "w_made", "w_turned", "wt_made"))
        xq_made = Tally(sem("xq_made"), BATCH)
        x_turned = Tally(sem("x_turned"), BATCH, 2)
        xqT_made = Tally(sem("xqT_made"), BATCH, 1)
        gated = Tally(sem("gated"), BATCH, 2)
        upped = Tally(sem("upped"), BATCH, 2)
        silued = Tally(sem("silued"), BATCH, 2)
        h_made = Tally(sem("h_made"), BATCH, 2)
        h_scaled = Tally(sem("h_scaled"), BATCH)
        h_rounded = Tally(sem("h_rounded"), BATCH)
        hq_made = Tally(sem("hq_made"), BATCH, 2)
        h_turned = Tally(sem("h_turned"), BATCH, 2)
        hqT_made = Tally(sem("hqT_made"), BATCH, 1)
        down_done = Tally(sem("down_done"), BATCH, 2)
        added = Tally(sem("added"), BATCH, 4)
        written = sem("written")
        chain_sem = sem("dve_chain")
        block = ctx.enter_context(nc.Block())

        @block.sync
        def _(sp):
            with sp.Fori(0, LOOPS) as i:
                sp.wait_ge(added.sem, added.at(i, BATCH - 1))
                sp.dma_start(c.outs[0][:, bass.ds(i * BATCH, BATCH), :], c.X[:, bass.ds(i * BATCH, BATCH), :]).then_inc(written, 16)
            sp.wait_ge(written, 16 * LOOPS)

        @block.gpsimd
        def _(pool):
            pool.wait_ge(summed, 1)
            nc.gpsimd.partition_all_reduce(sums_all[:, :], sums[:, :], 128, RADD).then_inc(summed_all, 1)

        @block.scalar
        def _(act):
            rstd_on_scalar(c, act, shifted, rooted)
            for k in range(3):
                act.wait_ge(w_turned, k + 1)
                nc.scalar.activation(WT[:, k, :], c.bank[k][:, :], ACT.Copy).then_inc(wt_made, 1)
            for t in (xqT_made, silued, hqT_made):
                act.sem_inc(t.sem, t.credit)
            with act.Fori(0, LOOPS) as i:
                for t in range(BATCH + 4):
                    b = t - 1
                    if 0 <= b < BATCH:
                        act.wait_ge(x_turned.sem, x_turned.at(i, b))
                        act.wait_ge(upped.sem, upped.at(i, b - 2))
                        nc.scalar.activation(xqT[:, b % 2, :], c.bank[0][:, 0:S], ACT.Copy).then_inc(xqT_made.sem, 1)
                    b = t - 3
                    if 0 <= b < BATCH:
                        act.wait_ge(hq_made.sem, hq_made.at(i, b - 2))
                        act.wait_ge(h_scaled.sem, h_scaled.at(i, b))
                        nc.scalar.activation(h[:, b % 2, :], h[:, b % 2, :], ACT.Copy, scale=hcol[:, b % 4, 2:3], bias=ROUND
                                             ).then_inc(h_rounded.sem, 1)
                    b = t - 2
                    if 0 <= b < BATCH:
                        act.wait_ge(gated.sem, gated.at(i, b))
                        act.wait_ge(h_made.sem, h_made.at(i, b - 2))
                        nc.scalar.activation(gate[:, b % 2, :], c.bank[1 + b % 2][:, :], ACT.Silu, scale=xcol[:, b % 4, 3:4]
                                             ).then_inc(silued.sem, 1)
                    b = t - 4
                    if 0 <= b < BATCH:
                        act.wait_ge(h_turned.sem, h_turned.at(i, b))
                        act.wait_ge(down_done.sem, down_done.at(i, b - 2))
                        nc.scalar.activation(hqT[:, b % 2, :], c.bank[5][:, :], ACT.Copy).then_inc(hqT_made.sem, 1)

        @block.vector
        def _(dve):
            rstd_on_vector(c, dve, shifted, rooted)
            setup = Chain(dve, sem("setup_chain"))
            link = setup.link
            dve.wait_ge(c.w3_sem, 48)
            nc.vector.tensor_reduce(sums[:, :], W[:, :, :], AX.X, ALU.add, apply_absolute_value=True).then_inc(summed, 1)
            dve.wait_ge(summed_all, 1)
            link(nc.vector.tensor_scalar(mean[:, :], sums_all[:, :], 1.0 / (D * F0), 1e-5, ALU.mult, ALU.max))
            link(nc.vector.reciprocal(mean_inv[:, :], mean[:, :]))
            for k in range(3):
                link(nc.vector.tensor_scalar(W2[:, k, :], W[:, k, :], mean_inv[:, k:k + 1], ROUND, ALU.mult, ALU.add))
            link(nc.vector.tensor_scalar(W2[:, :, :], W2[:, :, :], ROUND - 1.0, ROUND + 1.0, ALU.max, ALU.min))
            nc.vector.tensor_scalar(WQ[:, :, :], W2[:, :, :], ROUND, None, ALU.subtract).then_inc(w_made, 1)
            for t in (h_made, hq_made, added):
                dve.sem_inc(t.sem, t.credit)
            chain = Chain(dve, chain_sem, BATCH * 8)
            with dve.Fori(0, LOOPS) as i:
                chain.start(i)
                link = chain.link
                for t in range(BATCH + 5):
                    b = t
                    if b < BATCH:
                        at, r, q = i * BATCH + b, b % 2, b % 4
                        col = xcol[:, q, :]
                        dve.wait_ge(x_turned.sem, x_turned.at(i, b - 2))
                        link(nc.vector.tensor_scalar(xn[:, r, :], c.X[:, bass.ds(at, 1), :], c.stat[:, bass.ds(at, 1), 0],
                                                     c.rstd[:, bass.ds(at, 1)], ALU.subtract, ALU.mult))
                        link(nc.vector.tensor_reduce(col[:, 0:1], xn[:, r, :], AX.X, ALU.max, apply_absolute_value=True))
                        link(nc.vector.tensor_scalar(col[:, 1:2], col[:, 0:1], 1e-5, 1 / 127.0, ALU.max, ALU.mult))
                        link(nc.vector.reciprocal(col[:, 2:3], col[:, 1:2]))
                        nc.vector.tensor_scalar(col[:, 3:5], mean[:, 0:2], col[:, 1:2], None, ALU.mult)
                        link(nc.vector.tensor_scalar(xn[:, r, :], xn[:, r, :], col[:, 2:3], ROUND, ALU.mult, ALU.add))
                        nc.vector.tensor_scalar(xq[:, r, :], xn[:, r, :], ROUND + 127.0, ROUND, ALU.min, ALU.subtract
                                                ).then_inc(xq_made.sem, 1)
                    b = t - 2
                    if 0 <= b < BATCH:
                        r, q = b % 2, b % 4
                        col = hcol[:, q, :]
                        dve.wait_ge(silued.sem, silued.at(i, b))
                        dve.wait_ge(upped.sem, upped.at(i, b))
                        dve.wait_ge(added.sem, added.at(i, b - 4))
                        nc.vector.scalar_tensor_tensor(out=h[:, r, :], in0=c.bank[3 + r][:, :], scalar=xcol[:, q, 4:5],
                                                       in1=gate[:, r, :], op0=ALU.mult, op1=ALU.mult).then_inc(h_made.sem, 1)
                        dve.wait_ge(h_made.sem, h_made.at(i, b))
                        link(nc.vector.tensor_reduce(col[:, 0:1], h[:, r, :], AX.X, ALU.max, apply_absolute_value=True))
                        link(nc.vector.tensor_scalar(col[:, 1:2], col[:, 0:1], 1e-5, 1 / 127.0, ALU.max, ALU.mult))
                        nc.vector.reciprocal(col[:, 2:3], col[:, 1:2]).then_inc(h_scaled.sem, 1)
                        link(nc.vector.tensor_scalar(col[:, 3:4], mean[:, 2:3], col[:, 1:2], None, ALU.mult))
                    b = t - 3
                    if 0 <= b < BATCH:
                        r = b % 2
                        dve.wait_ge(h_rounded.sem, h_rounded.at(i, b))
                        dve.wait_ge(h_turned.sem, h_turned.at(i, b - 2))
                        nc.vector.tensor_scalar(hq[:, r, :], h[:, r, :], ROUND + 127.0, ROUND, ALU.min, ALU.subtract
                                                ).then_inc(hq_made.sem, 1)
                    b = t - 5
                    if 0 <= b < BATCH:
                        X = c.X[:, bass.ds(i * BATCH + b, 1), :]
                        dve.wait_ge(down_done.sem, down_done.at(i, b))
                        nc.vector.scalar_tensor_tensor(out=X, in0=c.bank[6 + b % 2][:, 0:D], scalar=hcol[:, b % 4, 3:4], in1=X,
                                                       op0=ALU.mult, op1=ALU.add).then_inc(added.sem, 1)
            assert chain.n == chain.per, (chain.n, chain.per)

        @block.tensor
        def _(pe):
            pe.wait_ge(w_made, 1)
            for k in range(3):
                for q in range(FC):
                    last = nc.tensor.matmul(c.bank[k][:, q * 128:(q + 1) * 128], WQ[:, k, q * 128:(q + 1) * 128], c.ident16[:, :],
                                            start=True, stop=True)
                last.then_inc(w_turned, 1)
            for t in (x_turned, gated, upped, h_turned, down_done):
                pe.sem_inc(t.sem, t.credit)
            pe.wait_ge(wt_made, 3)
            with pe.Fori(0, LOOPS) as i:
                for t in range(BATCH + 5):
                    b = t - 1
                    if 0 <= b < BATCH:
                        pe.wait_ge(xq_made.sem, xq_made.at(i, b))
                        pe.wait_ge(xqT_made.sem, xqT_made.at(i, b - 1))
                        nc.tensor.matmul(c.bank[0][:, 0:S], xq[:, b % 2, :], c.ident16[:, :], start=True, stop=True
                                         ).then_inc(x_turned.sem, 1)
                    b = t - 2
                    if 0 <= b < BATCH:
                        pe.wait_ge(xqT_made.sem, xqT_made.at(i, b))
                        pe.wait_ge(silued.sem, silued.at(i, b - 2))
                        nc.tensor.matmul(c.bank[1 + b % 2][:, :], xqT[:, b % 2, :], WT[:, 0, :], start=True, stop=True
                                         ).then_inc(gated.sem, 1)
                        pe.wait_ge(h_made.sem, h_made.at(i, b - 2))
                        nc.tensor.matmul(c.bank[3 + b % 2][:, :], xqT[:, b % 2, :], WT[:, 1, :], start=True, stop=True
                                         ).then_inc(upped.sem, 1)
                    b = t - 4
                    if 0 <= b < BATCH:
                        pe.wait_ge(hq_made.sem, hq_made.at(i, b))
                        pe.wait_ge(hqT_made.sem, hqT_made.at(i, b - 1))
                        for q in range(FC):
                            last = nc.tensor.matmul(c.bank[5][:, q * S:(q + 1) * S], hq[:, b % 2, q * 128:(q + 1) * 128],
                                                    c.ident16[:, :], start=True, stop=True)
                        last.then_inc(h_turned.sem, 1)
                    b = t - 5
                    if 0 <= b < BATCH:
                        pe.wait_ge(hqT_made.sem, hqT_made.at(i, b))
                        pe.wait_ge(added.sem, added.at(i, b - 2))
                        for q in range(FC):
                            last = nc.tensor.matmul(c.bank[6 + b % 2][:, 0:D], hqT[:, b % 2, q * S:(q + 1) * S],
                                                    WT[:, 2, q * 128:(q + 1) * 128], start=(q == 0), stop=(q == FC - 1))
                        last.then_inc(down_done.sem, 1)


def closing(c):
    nc = c.nc
    with ExitStack() as ctx:
        stored = PartSemaphores(nc, ctx)("stored")
        with nc.Block() as block:
            @block.sync
            def _(sp):
                sp.dma_start(c.outs[0], c.X[:, :, :]).then_inc(stored, 16)
                sp.wait_ge(stored, 16)
                for loaded, count in ((c.w1_sem, 3), (c.w3_sem, 3), (c.wide_in, 2), (c.arena_in, 2 + E)):
                    sp.wait_ge(loaded, 16 * count)


PARTS = {
    "a0": lambda c: one_head(c, "L0", False, D ** -0.5),
    "e0": lambda c: experts(c, "E0", False),
    "a1": lambda c: one_head(c, "L1", True, 1.0),
    "g1": ffn1,
    "x2": lambda c: many_heads(c, "X2", False, "keys"),
    "f2": lambda c: many_heads(c, "F2", True, None),
    "e2": lambda c: experts(c, "E2", True),
    "x3": lambda c: many_heads(c, "X3", False, "pairs"),
    "g3": ffn3,
}


def program(nc, ins, outs, parts=tuple(PARTS)):
    with ExitStack() as ctx:
        c = Core(nc, ctx, ins, outs)
        opening(c)
        for part in parts:
            PARTS[part](c)
        if parts[-1] != "g3":
            closing(c)


def laid_out(inputs):
    a = {k: np.asarray(v) for k, v in inputs.items()}
    small = np.zeros((128, SMALL_WIDTH), np.float32)

    def put(name, rows, value):
        at, width = SMALL[name]
        small[0:rows, at:at + width] = np.broadcast_to(value, (rows, width))

    put("ident", 128, np.eye(128, dtype=np.float32))
    p = np.arange(128)
    product = p % 32 // DH
    spread = np.zeros((128, 4, GROUPS, 128), np.float16)
    for which, stands in enumerate((product < 2, product >= 2, product % 2 == 0, product % 2 == 1)):
        for g in range(GROUPS):
            spread[(p // 32 * GROUPS + g) * DH + p % DH, which, g, p] = stands
    put("spread", 128, spread.reshape(128, -1).view(np.float32))
    put("expert_rank", 128, np.arange(E, 0, -1, dtype=np.float32)[None, :])
    for x in ("q", "k", "v", "o"):
        put(f"L0_w{x}", 128, a[f"L0_xattn_W{x}"].T)
    put("L0_bo", 128, a["L0_xattn_bo"][None, :])
    put("L0_bv", 128, a["L0_xattn_bv"][None, :])
    put("L0_bq", 128, a["L0_xattn_bq"][:, None])
    put("L1_wk", 128, a["L1_xattn_W_k"].T)
    put("L1_wo", 128, a["L1_xattn_W_o"].T)
    put("L1_bo", 128, a["L1_xattn_b_o"][None, :])
    put("L1_bk", 128, a["L1_xattn_b_k"][:, None])
    wqkv, bqkv = a["L2_ffn_w_qkv"], a["L2_ffn_b_qkv"]
    for l, wq, wk, wv, wo, bq, bk, bv, bo in (
        ("X2", a["L2_xattn_Wq"].T, a["L2_xattn_Wk"].T, a["L2_xattn_Wv"].T, a["L2_xattn_Wo"].T,
         a["L2_xattn_bq"], a["L2_xattn_bk"], a["L2_xattn_bv"], a["L2_xattn_bo"]),
        ("F2", wqkv[:, 0:128], wqkv[:, 128:256], wqkv[:, 256:384], a["L2_ffn_w_o"],
         bqkv[0:128], bqkv[128:256], bqkv[256:384], a["L2_ffn_b_o"]),
        ("X3", a["L3_xattn_wq_w"].T, a["L3_xattn_wk_w"].T, a["L3_xattn_wv_w"].T, a["L3_xattn_wo_w"].T,
         a["L3_xattn_wq_b"], a["L3_xattn_wk_b"], a["L3_xattn_wv_b"], a["L3_xattn_wo_b"]),
    ):
        put(l + "_wq", 128, wq)
        put(l + "_wk", 128, wk)
        put(l + "_wv", 128, wv)
        put(l + "_wo", 128, wo)
        put(l + "_bv", 128, bv[None, :])
        put(l + "_bo", 128, bo[None, :])
        put(l + "_bq", 128, bq[:, None])
        put(l + "_bk", 128, bk[:, None])
    put("router", 128, np.concatenate([a["L0_ffn_w_router"], a["L0_ffn_w_gating"]], axis=1))
    put("gate2", 128, a["L2_ffn_w_gate"])
    for x in ("ln1_w", "ln1_b", "ln2_w", "ln2_b"):
        put(x, 128, a["L2_ffn_" + x][:, None])
    put("b1", 128, a["L2_ffn_b1"].reshape(E * FC, 128).T)
    put("b2", E, a["L2_ffn_b2"])
    out = {
        "x": a["x"].transpose(1, 0, 2),
        "small": small,
        "ctxT": a["ctx_1024"].transpose(2, 0, 1).reshape(D, B * KEYS),
        "ctx": a["ctx_1024"].transpose(1, 0, 2),
        "cell_mask": a["mask_BxSxS2_ff1"].transpose(1, 0, 2).reshape(S, B * KEYS),
        "seq_mask": a["mask_BxS2_ff1"].reshape(1, B * KEYS),
        "mask2": a["mask_BxS2_ik0"].reshape(1, B * KEYS),
        "mask3": a["mask_Bx1xSxS2_bk1"].reshape(B, S, KEYS).transpose(1, 0, 2).reshape(S, B * KEYS),
    }
    for x in ("L0_ffn_w_gate", "L0_ffn_w_up", "L0_ffn_w_down", "L1_ffn_w_gate", "L1_ffn_w_up", "L1_ffn_w_down",
              "L2_ffn_w1", "L2_ffn_w2", "L3_ffn_w_gate", "L3_ffn_w_up", "L3_ffn_w_down"):
        out[x] = a[x]
    out = {k: np.ascontiguousarray(v) for k, v in out.items()}
    out["mask3"] = out["mask3"].view(np.int32)
    return out


def kernel(**inputs):
    import concourse.bacc as bacc
    from concourse.bass_utils import run_bass_kernel_spmd

    nc = bacc.Bacc("TRN2", target_bir_lowering=False, num_devices=1)
    arrays = laid_out(inputs)
    ins = {k: nc.dram_tensor(f"in_{k}", v.shape, mybir.dt.from_np(v.dtype), kind="ExternalInput").ap()
           for k, v in arrays.items()}
    out = nc.dram_tensor("out_0", (S, B, D), F32, kind="ExternalOutput").ap()
    program(nc, ins, [out])
    r = run_bass_kernel_spmd(nc, [{f"in_{k}": v for k, v in arrays.items()}], core_ids=[0])
    return np.ascontiguousarray(r.results[0]["out_0"].transpose(1, 0, 2))
```

```python
import numpy as np
import concourse.bass as bass
from concourse import mybir
from contextlib import ExitStack

F32, BF16, F16, I32, U8 = (mybir.dt.float32, mybir.dt.bfloat16, mybir.dt.float16, mybir.dt.int32, mybir.dt.uint8)
ALU, ACT, AX = mybir.AluOpType, mybir.ActivationFunctionType, mybir.AxisListType

B, S, D, KEYS = 32, 128, 128, 120
QUAD = 4
TURNS = B // QUAD
TOK = QUAD * S
HEADS, DH = 16, 8
PER = 4
GROUPS = HEADS // PER
EPS = 1e-5
E, F0, F1 = 8, 512, 384
FC = F0 // 128
SHUT = -float(2 ** 44)
ROUND = 1.5 * 2 ** 23

SMALL = {}


def _column(name, width):
    SMALL[name] = (sum(w for _, w in SMALL.values()), width)


for _name, _width in (
    [("ident", 128)] + [(f"L0_{x}", 128) for x in ("wq", "wk", "wv", "wo", "bo", "bv")] + [("L0_bq", 1)]
    + [("spread", 4 * HEADS * 32 // 2), ("expert_rank", 8)]
    + [(f"L1_{x}", 128) for x in ("wk", "wo", "bo")] + [("L1_bk", 1)]
    + [(f"{l}_{x}", w) for l in ("X2", "F2", "X3")
       for x, w in (("wq", 128), ("wk", 128), ("wv", 128), ("wo", 128), ("bo", 128), ("bv", 128), ("bq", 1), ("bk", 1))]
    + [("router", 16), ("gate2", 8), ("ln1_w", 1), ("ln1_b", 1), ("ln2_w", 1), ("ln2_b", 1), ("b1", E * FC), ("b2", 128)]
):
    _column(_name, _width)
SMALL_WIDTH = sum(w for _, w in SMALL.values())
FIRST_WIDTH = SMALL["spread"][0]


class Tally:

    def __init__(self, sem, per, credit=0):
        self.sem, self.per, self.credit = sem, per, credit

    def at(self, turn, n):
        assert n + 1 + self.credit > 0
        return turn * self.per + (n + 1 + self.credit)


class Chain:

    def __init__(self, eng, sem, per=0):
        self.eng, self.sem, self.per, self.n, self.turn = eng, sem, per, 0, 0

    def link(self, instruction):
        self.n += 1
        instruction.then_inc(self.sem, 1)
        self.eng.wait_ge(self.sem, self.turn * self.per + self.n)

    def start(self, turn):
        self.turn, self.n = turn, 0


class Core:

    def __init__(self, nc, ctx, ins, outs):
        self.nc, self.ins, self.outs = nc, ins, outs

        def sb(name, shape, dt=F32):
            return ctx.enter_context(nc.sbuf_tensor(name, shape, dt))

        self.X = sb("X", [S, B, D])
        self.stat = sb("stat", [S, B, 2])
        self.stats6 = sb("stats6", [S, B, 6])
        self.norm_work = sb("norm_work", [S, 2, B])
        self.rstd = sb("rstd", [S, B])
        self.small = sb("small", [128, SMALL_WIDTH])
        self.arena = sb("arena", [128, 3 * F0 * (E + 1)])
        self.ident16 = sb("ident16", [128, 128], BF16)
        self.ones_row = sb("ones_row", [1, S])
        self.wide = sb("wide", [128, 12288])
        self.bank = [ctx.enter_context(nc.psum_tensor(f"bank{i}", [128, 512], F32)) for i in range(8)]
        self.rest_in = ctx.enter_context(nc.semaphore("rest_in"))
        self.apart = ctx.enter_context(nc.semaphore("apart"))
        self.arena_in = ctx.enter_context(nc.semaphore("arena_in"))
        self.wide_in = ctx.enter_context(nc.semaphore("wide_in"))
        self.w1_in = sb("w1_in", [128, 36, 32])
        self.w1_sem = ctx.enter_context(nc.semaphore("w1_in_sem"))
        self.arena2_in = ctx.enter_context(nc.semaphore("arena2_in"))
        self.inner = self.wide[:, 0:B * D].rearrange("p (b d) -> p b d", b=B)
        self.w3_in = sb("w3_in", [128, 3, F0])
        self.w3_sem = ctx.enter_context(nc.semaphore("w3_in_sem"))
        self.masks_made = ctx.enter_context(nc.semaphore("masks_made"))
        self.masks_logged = ctx.enter_context(nc.semaphore("masks_logged"))

    def w(self, name, rows=128):
        at, width = SMALL[name]
        return self.small[0:rows, at:at + width]


class PartSemaphores:

    def __init__(self, nc, ctx):
        self.nc, self.taken = nc, []
        ctx.callback(self.give_back)

    def __call__(self, name):
        self.taken.append(self.nc.alloc_semaphore(name=name))
        return self.taken[-1]

    def give_back(self):
        self.nc.clear_and_free_semaphores(self.taken)
        self.nc.all_engine_barrier()


def opening(c):
    nc = c.nc
    with ExitStack() as ctx:
        sem = PartSemaphores(nc, ctx)
        x_in = [sem(f"x_in{h}") for h in range(4)]
        small_in, made = sem("small_in"), sem("made")
        with nc.Block() as block:
            @block.sync
            def _(sp):
                for h in range(4):
                    sp.dma_start(c.X[:, 8 * h:8 * h + 8, :], c.ins["x"][:, 8 * h:8 * h + 8, :]).then_inc(x_in[h], 16)
                sp.dma_start(c.small[:, 0:FIRST_WIDTH], c.ins["small"][:, 0:FIRST_WIDTH]).then_inc(small_in, 16)
                sp.dma_start(c.small[:, FIRST_WIDTH:], c.ins["small"][:, FIRST_WIDTH:]).then_inc(c.rest_in, 16)
                sp.wait_ge(small_in, 16)

            @block.scalar
            def _(act):
                act.wait_ge(small_in, 16)
                nc.scalar.activation(c.ident16[:, :], c.w("ident"), ACT.Copy).then_inc(made, 1)

            @block.vector
            def _(dve):
                nc.vector.memset(c.ones_row[:, :], 1.0).then_inc(made, 1)
                for b in range(B):
                    if b % 8 == 0:
                        dve.wait_ge(x_in[b // 8], 16)
                    nc.vector.bn_stats(c.stats6[:, b, :], c.X[:, b, :])


NORM_STEPS = 5


def rstd_on_scalar(c, act, steps, rooted):
    act.wait_ge(steps, NORM_STEPS)
    c.nc.scalar.activation(c.rstd[:, :], c.rstd[:, :], ACT.Sqrt).then_inc(rooted, 1)


def rstd_on_vector(c, dve, steps, rooted):
    nc, v = c.nc, c.nc.vector
    even_mean, even_sq, odd_mean, odd_sq = (c.stats6[:, :, k] for k in (1, 2, 4, 5))
    mean, var, work, diff = c.stat[:, :, 0], c.stat[:, :, 1], c.norm_work[:, 0, :], c.norm_work[:, 1, :]
    v.tensor_tensor(work, even_mean, odd_mean, ALU.add)
    v.tensor_tensor(diff, even_mean, odd_mean, ALU.subtract)
    v.tensor_tensor(var, even_sq, odd_sq, ALU.add).then_inc(steps, 1)
    dve.wait_ge(steps, 1)
    v.tensor_scalar(mean, work, 0.5, None, ALU.mult)
    v.tensor_tensor(diff, diff, diff, ALU.mult).then_inc(steps, 1)
    dve.wait_ge(steps, 2)
    v.scalar_tensor_tensor(out=var, in0=diff, scalar=D / 4, in1=var, op0=ALU.mult, op1=ALU.add).then_inc(steps, 1)
    dve.wait_ge(steps, 3)
    v.tensor_scalar(var, var, 1 / D, None, ALU.mult).then_inc(steps, 1)
    dve.wait_ge(steps, 4)
    v.tensor_scalar(c.rstd[:, :], var, EPS, None, ALU.add).then_inc(steps, 1)
    dve.wait_ge(rooted, 1)
    v.reciprocal(c.rstd[:, :], c.rstd[:, :]).then_inc(rooted, 1)
    dve.wait_ge(rooted, 2)


def overlapping_turns(eng, run):
    run(0, 0, True, False)
    with eng.Fori(0, (TURNS - 2) // 2) as j:
        run(j * 2 + 1, 1, True, True)
        run(j * 2 + 2, 0, True, True)
    run(TURNS - 1, 1, True, True)
    run(TURNS, 0, False, True)


class Turn:

    def __init__(self, i, own, before, steps):
        self.i, self.own, self.before, self.steps = i, own, before, steps

    def runs(self, k):
        return self.own if k >= 0 else self.before

    def at(self, tally, k):
        if k + 1 + tally.credit > 0:
            return tally.at(self.i, k)
        return tally.at(self.i - 1, k + tally.per)


def linked_turns(eng, run, count, steps, left):
    run(Turn(0, True, False, steps))
    with eng.Fori(1, count) as i:
        run(Turn(i, True, True, steps))
    run(Turn(count, False, True, left))


def wait_apart(eng, sem, value, apart):
    eng.wait_ge(sem, value)
    eng.sem_inc(apart, 1)


def mask_loads(c, eng):
    eng.dma_start(c.wide[:, 3840:7680], c.ins["cell_mask"]).then_inc(c.wide_in, 16)
    eng.dma_start(c.wide[:, 7680:11520], c.ins["seq_mask"].partition_broadcast(S)).then_inc(c.wide_in, 16)


def later_loads(c, eng):
    w1 = c.w1_in[:, :, :].rearrange("p b w -> p (b w)")
    for k, x in enumerate(("up", "gate")):
        eng.dma_start(w1[:, k * F1:(k + 1) * F1].rearrange("p (c i) -> p c i", c=F1 // 128),
                      c.ins[f"L1_ffn_w_{x}"].rearrange("(c p) i -> p c i", p=128)).then_inc(c.w1_sem, 16)
    eng.dma_start(w1[:, 2 * F1:], c.ins["L1_ffn_w_down"]).then_inc(c.w1_sem, 16)
    for k, x in enumerate(("gate", "up")):
        eng.dma_start(c.w3_in[:, k, :].rearrange("p (c i) -> p c i", c=FC),
                      c.ins[f"L3_ffn_w_{x}"].rearrange("(c p) i -> p c i", p=128)).then_inc(c.w3_sem, 16)
    eng.dma_start(c.w3_in[:, 2, :], c.ins["L3_ffn_w_down"]).then_inc(c.w3_sem, 16)


def one_head(c, n, masked, scale):
    nc = c.nc
    WK = QUAD * KEYS
    with ExitStack() as ctx:
        def sb(name, shape, dt=F32):
            return ctx.enter_context(nc.sbuf_tensor(f"{n}_{name}", shape, dt))

        take = PartSemaphores(nc, ctx)

        def sem(name):
            return take(f"{n}_{name}")

        xn, xnT = sb("xn", [S, QUAD, D]), sb("xnT", [D, TOK])
        ctxT = sb("ctxT", [D, 2, WK])
        qT = xnT if masked else sb("qT", [D, TOK])
        kT = sb("kT", [D, WK])
        V = sb("V", [KEYS, 2, QUAD, D])
        P, Pn = sb("P", [S, QUAD, KEYS]), sb("Pn", [S, QUAD, KEYS])
        scored = sb("scored", [S, WK]) if masked else None
        PT, OT = sb("PT", [KEYS, TOK]), sb("OT", [D, TOK])
        greatest, neg_max = sb("greatest", [S, QUAD]), sb("neg_max", [S, QUAD])
        sums, rcp = sb("sums", [S, QUAD]), sb("rcp", [S, QUAD])
        log_mask = c.wide[:, 0:B * KEYS]
        seq_shut = None if masked else sb("seq_shut", [S, B * KEYS])
        shifted, rooted = sem("shifted"), sem("rooted")
        ctx_in = [Tally(sem(f"ctx_in{k}"), 16) for k in range(2)]
        val_in = [Tally(sem(f"val_in{k}"), 16) for k in range(2)]
        normed = Tally(sem("normed"), QUAD)
        turned = Tally(sem("turned"), 1, 1)
        xnT_made = Tally(sem("xnT_made"), 1, 1)
        q_done, q_made = Tally(sem("q_done"), 1, 1), Tally(sem("q_made"), 1, 1)
        k_done, k_made = Tally(sem("k_done"), 1, 2), Tally(sem("k_made"), 1, 1)
        v_done, v_made = Tally(sem("v_done"), 1, 2), Tally(sem("v_made"), 1, 1)
        s_done = Tally(sem("s_done"), 1, 1)
        s_read = Tally(sem("s_read"), 1, 1)
        maxed = Tally(sem("maxed"), 1)
        exped = Tally(sem("exped"), 1, 1)
        scaled = Tally(sem("scaled"), 1, 1)
        p_turned = Tally(sem("p_turned"), 1, 1)
        pT_made = Tally(sem("pT_made"), 1, 1)
        pv_done = Tally(sem("pv_done"), 1, 2)
        oT_made = Tally(sem("oT_made"), 1, 1)
        o_done = Tally(sem("o_done"), 1, 1)
        added = Tally(sem("added"), 1, 1)
        summed = Tally(sem("summed"), 1)
        topped = Tally(sem("topped"), 1)
        block = ctx.enter_context(nc.Block())
        bank = c.bank

        def slots(eng, slot, first=None):
            if first:
                first(0)
            slot(0, 0, True, True, False)
            with eng.Fori(0, (TURNS - 2) // 2) as j:
                slot(j * 2 + 1, 1, True, True, True)
                slot(j * 2 + 2, 0, True, True, True)
            slot(TURNS - 1, 1, False, True, True)
            slot(TURNS, 0, False, False, True)

        @block.sync
        def _(sp):
            with sp.Fori(0, TURNS // 2) as j:
                for k in range(2):
                    turn = j * 2 + k
                    read = k_done if masked else v_done
                    sp.wait_ge(read.sem, read.at(turn, -2))
                    sp.dma_start(ctxT[:, k, :], c.ins["ctxT"][:, bass.ds(turn * WK, WK)]).then_inc(ctx_in[k].sem, 16)
                    if masked:
                        sp.wait_ge(pv_done.sem, pv_done.at(turn, -2))
                        sp.dma_start(V[:, k, :, :], c.ins["ctx"][:, bass.ds(turn * QUAD, QUAD), :]).then_inc(val_in[k].sem, 16)
                    else:
                        load_expert(c, sp, turn)
            if not masked:
                sp.wait_ge(c.rest_in, 16)

        @block.gpsimd
        def _(pool):
            if not masked:
                masks_for_layer1(c, pool, seq_shut)

        @block.scalar
        def _(act):
            rstd_on_scalar(c, act, shifted, rooted)
            if not masked:
                act.wait_ge(ctx_in[0].sem, 16)
                mask_loads(c, act)
            for t in (xnT_made, exped, pT_made, oT_made) + (() if masked else (q_made,)):
                act.sem_inc(t.sem, t.credit)

            def slot(s, parity, norms, scores, output):
                last = s - 1
                if output:
                    act.wait_ge(maxed.sem, maxed.at(last, 0))
                    act.wait_ge(scaled.sem, scaled.at(last, -1))
                    for b in range(QUAD):
                        src = scored if masked else bank[2]
                        done = nc.scalar.activation(P[:, b, :], src[:, b * KEYS:(b + 1) * KEYS], ACT.Exp, scale=scale,
                                                    bias=neg_max[:, b:b + 1], accum_out=sums[:, b:b + 1])
                    done.then_inc(exped.sem, 1)
                if scores:
                    act.wait_ge(turned.sem, turned.at(s, 0))
                    read = s_done if masked else q_done
                    act.wait_ge(read.sem, read.at(s, -1))
                    nc.scalar.activation(xnT[:, :], bank[0][:, :], ACT.Copy).then_inc(xnT_made.sem, 1)
                if output:
                    act.wait_ge(p_turned.sem, p_turned.at(last, 0))
                    act.wait_ge(pv_done.sem, pv_done.at(last, -1))
                    nc.scalar.activation(PT[:, :], bank[4][0:KEYS, :], ACT.Copy).then_inc(pT_made.sem, 1)
                if scores and not masked:
                    act.wait_ge(q_done.sem, q_done.at(s, 0))
                    act.wait_ge(s_done.sem, s_done.at(s, -1))
                    nc.scalar.activation(qT[:, :], bank[1][:, :], ACT.Identity, bias=c.w("L0_bq")).then_inc(q_made.sem, 1)
                if output:
                    act.wait_ge(pv_done.sem, pv_done.at(last, 0))
                    act.wait_ge(o_done.sem, o_done.at(last, -1))
                    nc.scalar.activation(OT[:, :], bank[5][:, :], ACT.Copy).then_inc(oT_made.sem, 1)

            slots(act, slot)

        @block.vector
        def _(dve):
            rstd_on_vector(c, dve, shifted, rooted)
            for t in (scaled, added, k_made) + ((s_read,) if masked else (v_made,)):
                dve.sem_inc(t.sem, t.credit)

            def norm(turn):
                dve.wait_ge(turned.sem, turned.at(turn, -1))
                for b in range(QUAD):
                    at = turn * QUAD + b
                    nc.vector.tensor_scalar(xn[:, b, :], c.X[:, bass.ds(at, 1), :], c.stat[:, bass.ds(at, 1), 0],
                                            c.rstd[:, bass.ds(at, 1)], ALU.subtract, ALU.mult).then_inc(normed.sem, 1)

            def slot(s, parity, norms, scores, output):
                last = s - 1
                if output:
                    dve.wait_ge(exped.sem, exped.at(last, 0))
                    dve.wait_ge(p_turned.sem, p_turned.at(last, -1))
                    nc.vector.reciprocal(rcp[:, :], sums[:, :]).then_inc(summed.sem, 1)
                    dve.wait_ge(summed.sem, summed.at(last, 0))
                    nc.vector.tensor_tensor(Pn[:, :, :], P[:, :, :], rcp[:, :].unsqueeze(2).broadcast_to([S, QUAD, KEYS]),
                                            ALU.mult).then_inc(scaled.sem, 1)
                if scores:
                    dve.wait_ge(k_done.sem, k_done.at(s, 0))
                    dve.wait_ge(s_done.sem, s_done.at(s, -1))
                    if masked:
                        nc.vector.tensor_scalar(kT[:, :], bank[6][:, 0:WK], c.w("L1_bk"), None, ALU.add
                                                ).then_inc(k_made.sem, 1)
                    else:
                        nc.vector.tensor_copy(kT[:, :], bank[6][:, 0:WK]).then_inc(k_made.sem, 1)
                        dve.wait_ge(v_done.sem, v_done.at(s, 0))
                        dve.wait_ge(pv_done.sem, pv_done.at(s, -2))
                        nc.vector.tensor_tensor(V[:, parity, :, :], bank[7][0:KEYS, :].rearrange("k (b d) -> k b d", b=QUAD),
                                                c.w("L0_bv", KEYS).unsqueeze(1).broadcast_to([KEYS, QUAD, D]), ALU.add
                                                ).then_inc(v_made.sem, 1)
                if norms:
                    norm(s + 1)
                if scores:
                    dve.wait_ge(s_done.sem, s_done.at(s, 0))
                    dve.wait_ge(exped.sem, exped.at(s, -1))
                    src = bank[2][:, 0:WK]
                    if masked:
                        nc.vector.tensor_tensor(scored[:, :], src, log_mask[:, bass.ds(s * WK, WK)], ALU.add
                                                ).then_inc(s_read.sem, 1)
                        dve.wait_ge(s_read.sem, s_read.at(s, 0))
                        src = scored[:, :]
                    nc.vector.reduce_max(greatest[:, :], src.rearrange("q (b k) -> q b k", b=QUAD), AX.X).then_inc(topped.sem, 1)
                    dve.wait_ge(topped.sem, topped.at(s, 0))
                    nc.vector.tensor_scalar(neg_max[:, :], greatest[:, :], -scale, None, ALU.mult).then_inc(maxed.sem, 1)
                if output:
                    X = c.X[:, bass.ds(last * QUAD, QUAD), :]
                    dve.wait_ge(o_done.sem, o_done.at(last, 0))
                    nc.vector.tensor_tensor(X, X, bank[3][:, :].rearrange("p (b d) -> p b d", b=QUAD), ALU.add
                                            ).then_inc(added.sem, 1)
                    wait_apart(dve, added.sem, added.at(last, 0), c.apart)
                    for b in range(QUAD):
                        at = last * QUAD + b
                        nc.vector.bn_stats(c.stats6[:, bass.ds(at, 1), :], c.X[:, bass.ds(at, 1), :])

            slots(dve, slot, norm)

        @block.tensor
        def _(pe):
            for t in (turned, k_done, p_turned, pv_done, o_done, s_done) + (() if masked else (v_done, q_done)):
                pe.sem_inc(t.sem, t.credit)

            def slot(s, parity, norms, scores, output):
                last, other = s - 1, 1 - parity
                arrived = lambda turn, odd: (turn - odd) * 8 + 16

                def turn_probabilities():
                    pe.wait_ge(scaled.sem, scaled.at(last, 0))
                    pe.wait_ge(pT_made.sem, pT_made.at(last, -1))
                    for b in range(QUAD):
                        done = nc.tensor.transpose(bank[4][0:KEYS, b * S:(b + 1) * S], Pn[:, b, :], c.w("ident"))
                    done.then_inc(p_turned.sem, 1)

                def queries():
                    pe.wait_ge(xnT_made.sem, xnT_made.at(s, 0))
                    pe.wait_ge(q_made.sem, q_made.at(s, -1))
                    nc.tensor.matmul(bank[1][:, :], c.w("L0_wq"), xnT[:, :], start=True, stop=True).then_inc(q_done.sem, 1)

                def probabilities_times_values():
                    pe.wait_ge(pT_made.sem, pT_made.at(last, 0))
                    if masked:
                        pe.wait_ge(val_in[other].sem, arrived(last, other))
                    else:
                        pe.wait_ge(v_made.sem, v_made.at(last, 0))
                    pe.wait_ge(oT_made.sem, oT_made.at(last, -1))
                    for b in range(QUAD):
                        done = nc.tensor.matmul(bank[5][:, b * S:(b + 1) * S], V[:, other, b, :], PT[:, b * S:(b + 1) * S],
                                                start=True, stop=True)
                    done.then_inc(pv_done.sem, 1)

                def scores_of_turn():
                    made = xnT_made if masked else q_made
                    pe.wait_ge(made.sem, made.at(s, 0))
                    pe.wait_ge(k_made.sem, k_made.at(s, 0))
                    read = s_read if masked else exped
                    pe.wait_ge(read.sem, read.at(s, -1))
                    for b in range(QUAD):
                        done = nc.tensor.matmul(bank[2][:, b * KEYS:(b + 1) * KEYS], qT[:, b * S:(b + 1) * S],
                                                kT[:, b * KEYS:(b + 1) * KEYS], start=True, stop=True)
                    done.then_inc(s_done.sem, 1)

                if scores:
                    for b in range(QUAD):
                        if b == 0:
                            pe.wait_ge(xnT_made.sem, xnT_made.at(s, -1))
                        pe.wait_ge(normed.sem, normed.at(s, b))
                        done = nc.tensor.transpose(bank[0][:, b * S:(b + 1) * S], xn[:, b, :], c.w("ident"))
                    done.then_inc(turned.sem, 1)
                    pe.wait_ge(ctx_in[parity].sem, arrived(s, parity))
                    pe.wait_ge(k_made.sem, k_made.at(s, -1))
                    nc.tensor.matmul(bank[6][:, 0:WK], c.w(n + "_wk"), ctxT[:, parity, :], start=True, stop=True
                                     ).then_inc(k_done.sem, 1)
                    if not masked:
                        pe.wait_ge(v_made.sem, v_made.at(s, -1))
                        for b in range(QUAD):
                            done = nc.tensor.matmul(bank[7][0:KEYS, b * D:(b + 1) * D], ctxT[:, parity, b * KEYS:(b + 1) * KEYS],
                                                    c.w("L0_wv"), start=True, stop=True)
                        done.then_inc(v_done.sem, 1)
                if masked and scores:
                    scores_of_turn()
                if output:
                    turn_probabilities()
                if scores and not masked:
                    queries()
                if output:
                    probabilities_times_values()
                if scores and not masked:
                    scores_of_turn()
                if output:
                    pe.wait_ge(added.sem, added.at(last, -1))
                    nc.tensor.matmul(bank[3][:, :].rearrange("p (b d) -> p b d", b=QUAD), c.ones_row[:, :],
                                     c.w(n + "_bo", 1).unsqueeze(1).broadcast_to([1, QUAD, D]), start=True, stop=False,
                                     skip_group_check=True)
                    pe.wait_ge(oT_made.sem, oT_made.at(last, 0))
                    for b in range(QUAD):
                        done = nc.tensor.matmul(bank[3][:, b * D:(b + 1) * D], OT[:, b * S:(b + 1) * S], c.w(n + "_wo"),
                                                start=False, stop=True, skip_group_check=True)
                    done.then_inc(o_done.sem, 1)

            slots(pe, slot)


def masks_for_layer1(c, pool, seq_shut):
    nc = c.nc
    least = 2.0 ** -63
    shut, cell, seq = c.wide[:, 0:3840], c.wide[:, 3840:7680], c.wide[:, 7680:11520]
    pool.wait_ge(c.wide_in, 32)
    nc.gpsimd.tensor_scalar(shut, cell, 0.0, -1e30, ALU.is_le, ALU.mult).then_inc(c.masks_made, 1)
    nc.gpsimd.tensor_scalar(seq_shut[:, :], seq, 0.0, -1e30, ALU.is_le, ALU.mult).then_inc(c.masks_made, 1)
    pool.wait_ge(c.masks_made, 2)
    nc.gpsimd.tensor_tensor(shut, shut, seq_shut[:, :], ALU.add).then_inc(c.masks_made, 1)
    nc.gpsimd.tensor_scalar(cell, cell, least, None, ALU.max).then_inc(c.masks_made, 1)
    nc.gpsimd.tensor_scalar(seq, seq, least, None, ALU.max).then_inc(c.masks_made, 1)


def masks_for_layer1_end(c, pool, sem):
    nc = c.nc
    shut, cell, seq = c.wide[:, 0:3840], c.wide[:, 3840:7680], c.wide[:, 7680:11520]
    pool.wait_ge(c.masks_logged, 2)
    nc.gpsimd.tensor_tensor(cell, cell, seq, ALU.add).then_inc(sem, 1)
    pool.wait_ge(sem, 1)
    nc.gpsimd.tensor_tensor(shut, shut, cell, ALU.add).then_inc(sem, 1)


def split_layout(c, second):
    cols = (2 if second else 3) * F0
    loaded = c.arena[:, cols:(E + 1) * cols]
    return cols, loaded, c.arena[:, 0:E * cols].bitcast(F16).rearrange("p (e part q) -> p e part q", e=E, part=2)


def load_expert(c, eng, e):
    cols, loaded, _ = split_layout(c, False)
    place = loaded[:, bass.ds(e * cols, cols)]
    for k, name in enumerate(("gate", "up")):
        eng.dma_start(place[:, k * F0:(k + 1) * F0], c.ins[f"L0_ffn_w_{name}"][bass.ds(e, 1)].rearrange("e d f -> d (e f)")
                      ).then_inc(c.arena_in, 16)
    eng.dma_start(place[:, 2 * F0:].rearrange("p (c d) -> p c d", c=FC),
                  c.ins["L0_ffn_w_down"][bass.ds(e, 1)].rearrange("e (c p) d -> p (e c) d", p=128)).then_inc(c.arena_in, 16)


def load_experts_of_layer2(c, eng):
    cols, loaded, _ = split_layout(c, True)
    loaded = loaded.rearrange("p (e q) -> p e q", e=E)
    eng.dma_start(loaded[:, :, 0:F0], c.ins["L2_ffn_w1"].rearrange("e d f -> d e f")).then_inc(c.arena2_in, 16)
    for e in range(E):
        eng.dma_start(loaded[:, e, F0:].rearrange("p (c d) -> p c d", c=FC),
                      c.ins["L2_ffn_w2"][e].rearrange("(c p) d -> p c d", p=128)).then_inc(c.arena2_in, 16)


X_UP, W_UP, H_UP = 16.0, 256.0, 4.0


def experts(c, n, second):
    nc = c.nc
    LOGITS = E if second else 2 * E
    X = c.inner if second else c.X
    with ExitStack() as ctx:
        def sb(name, shape, dt=F32):
            return ctx.enter_context(nc.sbuf_tensor(f"{n}_{name}", shape, dt))

        take = PartSemaphores(nc, ctx)

        def sem(name):
            return take(f"{n}_{name}")

        cols, loaded, W = split_layout(c, second)
        W_flat = c.arena[:, 0:E * cols].bitcast(F16)
        XT = sb("XT", [D, 2, B * S], F16)
        xn = sb("xn", [S, 2, QUAD, D])
        xs = sb("xs", [D, 2, TOK])
        logits = sb("logits", [S, B, LOGITS])
        weight = sb("weight", [S, B, E])
        tmp, tmp2, tmp3 = sb("tmp", [S, B, LOGITS]), sb("tmp2", [S, B, E]), sb("tmp3", [S, B, E])
        best = sb("best", [S, B, 4])
        left = sb("left", [S, B, E])
        wT = sb("wT", [E, 2, TOK]) if second else None
        shifted, rooted = sem("shifted"), sem("rooted")
        normed = Tally(sem("normed"), QUAD)
        turned = Tally(sem("turned"), 1, 2)
        xs_made = Tally(sem("xs_made"), 1)
        x_high = Tally(sem("x_high"), 1)
        x_low = Tally(sem("x_low"), 1, 2)
        w_high = Tally(sem("w_high"), 1)
        w_low = Tally(sem("w_low"), 1, 1)
        routed = Tally(sem("routed"), 1, 2)
        logits_made = Tally(sem("logits_made"), 1, 2)
        powers, weighed = sem("powers"), sem("weighed")
        w_turned, wT_made = sem("w_turned"), sem("wT_made")
        b2_done, b2_added = sem("b2_done"), sem("b2_added")
        chain_sem = sem("dve_chain")
        with nc.Block() as block:
            if not second:
                @block.sync
                def _(sp):
                    later_loads(c, sp)

            @block.scalar
            def _(act):
                rstd_on_scalar(c, act, shifted, rooted)
                act.wait_ge(c.arena2_in if second else c.arena_in, 16 * (1 + E if second else 3 * E))
                with act.Fori(0, TURNS // 2) as i:
                    for k in range(2):
                        turn = i * 2 + k
                        wait_apart(act, w_low.sem, w_low.at(turn, -1), c.apart)
                        nc.scalar.activation(W_flat[:, bass.ds(turn * (2 * cols), cols)], loaded[:, bass.ds(turn * cols, cols)],
                                             ACT.Copy, scale=W_UP).then_inc(w_high.sem, 1)
                        act.wait_ge(turned.sem, turned.at(turn, 0))
                        act.wait_ge(routed.sem, routed.at(turn, -2))
                        act.wait_ge(x_low.sem, x_low.at(turn, -2))
                        if second:
                            nc.scalar.activation(xs[:, k, :], c.bank[k][:, :], ACT.Identity, scale=c.w("ln2_w"),
                                                 bias=c.w("ln2_b")).then_inc(xs_made.sem, 1)
                        else:
                            nc.scalar.activation(xs[:, k, :], c.bank[k][:, :], ACT.Copy).then_inc(xs_made.sem, 1)
                        wait_apart(act, xs_made.sem, xs_made.at(turn, 0), c.apart)
                        nc.scalar.activation(XT[:, 0, bass.ds(turn * TOK, TOK)], xs[:, k, :], ACT.Copy, scale=X_UP
                                             ).then_inc(x_high.sem, 1)
                act.wait_ge(powers, 1)
                nc.scalar.activation(tmp[:, :, 0:E], logits[:, :, 0:E], ACT.Exp).then_inc(powers, 1)
                if not second:
                    nc.scalar.activation(tmp[:, :, E:], logits[:, :, E:], ACT.Exp, scale=1 / 0.1).then_inc(powers, 1)
                    act.wait_ge(c.masks_made, 5)
                    nc.scalar.activation(c.wide[:, 3840:7680], c.wide[:, 3840:7680], ACT.Ln).then_inc(c.masks_logged, 1)
                    nc.scalar.activation(c.wide[:, 7680:11520], c.wide[:, 7680:11520], ACT.Ln).then_inc(c.masks_logged, 1)
                else:
                    for q in range(TURNS):
                        act.wait_ge(w_turned, q + 1)
                        if q >= 2:
                            act.wait_ge(b2_done, q - 1)
                        nc.scalar.activation(wT[:, q % 2, :], c.bank[4 + q % 2][0:E, :], ACT.Copy).then_inc(wT_made, 1)

            @block.vector
            def _(dve):
                rstd_on_vector(c, dve, shifted, rooted)
                for t in (x_low, w_low, logits_made):
                    dve.sem_inc(t.sem, t.credit)

                def run(s, parity, first, second_half):
                    if first:
                        dve.wait_ge(turned.sem, turned.at(s, -2))
                        for b in range(QUAD):
                            at = s * QUAD + b
                            nc.vector.tensor_scalar(xn[:, parity, b, :], X[:, bass.ds(at, 1), :], c.stat[:, bass.ds(at, 1), 0],
                                                    c.rstd[:, bass.ds(at, 1)], ALU.subtract, ALU.mult).then_inc(normed.sem, 1)
                    if second_half:
                        turn, k = s - 1, 1 - parity
                        dve.wait_ge(w_high.sem, w_high.at(turn, 0))
                        nc.vector.scalar_tensor_tensor(out=W_flat[:, bass.ds(turn * (2 * cols) + cols, cols)],
                                                       in0=loaded[:, bass.ds(turn * cols, cols)], scalar=W_UP,
                                                       in1=W_flat[:, bass.ds(turn * (2 * cols), cols)],
                                                       op0=ALU.mult, op1=ALU.subtract).then_inc(w_low.sem, 1)
                        dve.wait_ge(x_high.sem, x_high.at(turn, 0))
                        nc.vector.scalar_tensor_tensor(out=XT[:, 1, bass.ds(turn * TOK, TOK)], in0=xs[:, k, :], scalar=X_UP,
                                                       in1=XT[:, 0, bass.ds(turn * TOK, TOK)],
                                                       op0=ALU.mult, op1=ALU.subtract).then_inc(x_low.sem, 1)
                        dve.wait_ge(routed.sem, routed.at(turn, 0))
                        nc.vector.tensor_copy(logits[:, bass.ds(turn * QUAD, QUAD), :],
                                              c.bank[2 + k][:, 0:QUAD * LOGITS].rearrange("p (b l) -> p b l", b=QUAD)
                                              ).then_inc(logits_made.sem, 1)

                overlapping_turns(dve, run)
                dve.wait_ge(logits_made.sem, logits_made.at(TURNS - 1, 0))
                chain = Chain(dve, chain_sem)
                link = chain.link
                by8 = lambda ap: ap[:, :, :].rearrange("p b (s e) -> p (b s) e", e=E)
                R = B * LOGITS // E
                wide = lambda ap: ap.unsqueeze(2).broadcast_to([S, ap.shape[1], E])
                one = best[:, :, :].rearrange("p b k -> p (b k)")[:, 0:R]
                link(nc.vector.reduce_max(one, by8(logits), AX.X))
                nc.vector.tensor_tensor(by8(logits), by8(logits), wide(one), ALU.subtract).then_inc(powers, 1)
                dve.wait_ge(powers, 2 if second else 3)
                link(nc.vector.reduce_sum(one, by8(tmp), AX.X))
                link(nc.vector.reciprocal(one, one))
                link(nc.vector.tensor_tensor(by8(tmp), by8(tmp), wide(one), ALU.mult))
                total = best[:, :, 0]
                if second:
                    p, rank = tmp[:, :, :], c.w("expert_rank").unsqueeze(1).broadcast_to([S, B, E])
                    for found, among in ((tmp2, p), (tmp3, left[:, :, :])):
                        found = found[:, :, :]
                        link(nc.vector.reduce_max(total, among, AX.X))
                        link(nc.vector.tensor_tensor(found, among, wide(total), ALU.is_equal))
                        link(nc.vector.tensor_tensor(found, found, rank, ALU.mult))
                        link(nc.vector.reduce_max(total, found, AX.X))
                        link(nc.vector.tensor_tensor(found, found, wide(total), ALU.is_equal))
                        link(nc.vector.scalar_tensor_tensor(out=left[:, :, :], in0=found, scalar=-2.0, in1=p,
                                                            op0=ALU.mult, op1=ALU.add))
                    link(nc.vector.tensor_tensor(tmp2[:, :, :], tmp2[:, :, :], tmp3[:, :, :], ALU.add))
                    link(nc.vector.tensor_tensor(weight[:, :, :], tmp2[:, :, :], p, ALU.mult))
                    link(nc.vector.reduce_sum(total, weight[:, :, :], AX.X))
                else:
                    link(nc.vector.tensor_tensor(weight[:, :, :], tmp[:, :, 0:E], tmp[:, :, E:], ALU.mult))
                    link(nc.vector.reduce_sum(total, weight[:, :, :], AX.X))
                    link(nc.vector.tensor_scalar(total, total, 1e-9, None, ALU.add))
                link(nc.vector.reciprocal(total, total))
                nc.vector.tensor_tensor(weight[:, :, :], weight[:, :, :], wide(total), ALU.mult).then_inc(weighed, 1)
                dve.wait_ge(weighed, 1)
                if second:
                    for q in range(TURNS):
                        dve.wait_ge(b2_done, q + 1)
                        Xt = c.X[:, q * QUAD:(q + 1) * QUAD, :]
                        nc.vector.tensor_tensor(Xt, Xt, c.bank[6 + q % 2][:, :].rearrange("p (b d) -> p b d", b=QUAD), ALU.add
                                                ).then_inc(b2_added, 1)
                link(nc.vector.tensor_scalar(tmp2[:, :, :], weight[:, :, :], 1 / (W_UP * H_UP), None, ALU.mult))

            @block.tensor
            def _(pe):
                pe.sem_inc(turned.sem, turned.credit)
                pe.sem_inc(routed.sem, routed.credit)
                with pe.Fori(0, TURNS // 2) as i:
                    for k in range(2):
                        turn = i * 2 + k
                        for b in range(QUAD):
                            pe.wait_ge(normed.sem, normed.at(turn, b))
                            last = nc.tensor.transpose(c.bank[k][:, b * S:(b + 1) * S], xn[:, k, b, :], c.w("ident"))
                        last.then_inc(turned.sem, 1)
                        pe.wait_ge(xs_made.sem, xs_made.at(turn, 0))
                        pe.wait_ge(logits_made.sem, logits_made.at(turn, -2))
                        for b in range(QUAD):
                            last = nc.tensor.matmul(c.bank[2 + k][:, b * LOGITS:(b + 1) * LOGITS], xs[:, k, b * S:(b + 1) * S],
                                                    c.w("gate2" if second else "router"), start=True, stop=True)
                        last.then_inc(routed.sem, 1)
                if second:
                    pe.wait_ge(weighed, 1)
                    for t in range(TURNS + 1):
                        if t < TURNS:
                            for b in range(QUAD):
                                last = nc.tensor.transpose(c.bank[4 + t % 2][0:E, b * S:(b + 1) * S], weight[:, t * QUAD + b, :],
                                                           c.w("ident"))
                            last.then_inc(w_turned, 1)
                        if t >= 1:
                            q = t - 1
                            pe.wait_ge(wT_made, q + 1)
                            if q >= 2:
                                pe.wait_ge(b2_added, q - 1)
                            for b in range(QUAD):
                                last = nc.tensor.matmul(c.bank[6 + q % 2][:, b * D:(b + 1) * D], wT[:, q % 2, b * S:(b + 1) * S],
                                                        c.w("b2", E), start=True, stop=True)
                            last.then_inc(b2_done, 1)

        UNITS = E * FC
        factor = tmp2
        act_out = sb("act_out", [128, 2, TOK])
        h = act_out if second else sb("h", [128, 2, TOK])
        H = sb("H", [128, 2, 2, TOK], F16)
        gated = Tally(sem("gated"), UNITS)
        upped = Tally(sem("upped"), UNITS)
        acted = Tally(sem("acted"), UNITS, 2)
        h_made = Tally(sem("h_made"), UNITS, 2)
        h_high = Tally(sem("h_high"), UNITS, 2)
        h_low = Tally(sem("h_low"), UNITS, 2)
        downed = Tally(sem("downed"), UNITS, 2)
        added = Tally(sem("added"), E, 2)
        G_COLS, U_COLS, D_COLS = 0, cols - 2 * F0, cols - F0
        LEFT = 4

        turns = lambda eng, run: linked_turns(eng, run, TURNS, UNITS, LEFT)

        with nc.Block() as block:
            if not second:
                @block.gpsimd
                def _(pool):
                    masks_for_layer1_end(c, pool, sem("masks_end"))

            @block.scalar
            def _(act):
                act.sem_inc(acted.sem, acted.credit)
                act.sem_inc(h_high.sem, h_high.credit)

                def run(turn):
                    for t in range(turn.steps):
                        u = t - 1
                        if turn.runs(u):
                            made = acted if second else h_made
                            act.wait_ge(made.sem, turn.at(made, u))
                            act.wait_ge(downed.sem, turn.at(downed, u - 2))
                            nc.scalar.activation(H[:, u % 2, 0, :], h[:, u % 2, :], ACT.Copy, scale=H_UP).then_inc(h_high.sem, 1)
                        if turn.runs(t):
                            act.wait_ge(gated.sem, turn.at(gated, t))
                            read = h_low if second else h_made
                            act.wait_ge(read.sem, turn.at(read, t - 2))
                            if second:
                                nc.scalar.activation(act_out[:, t % 2, :], c.bank[t % 2][:, :], ACT.Gelu_apprx_tanh,
                                                     bias=c.w("b1")[:, t:t + 1], scale=1 / (X_UP * W_UP)).then_inc(acted.sem, 1)
                            else:
                                nc.scalar.activation(act_out[:, t % 2, :], c.bank[t % 2][:, :], ACT.Silu,
                                                     scale=1 / (X_UP * W_UP)).then_inc(acted.sem, 1)

                turns(act, run)

            @block.vector
            def _(dve):
                dve.sem_inc(h_low.sem, h_low.credit)
                dve.sem_inc(added.sem, added.credit)
                if not second:
                    dve.sem_inc(h_made.sem, h_made.credit)

                def run(turn):
                    for t in range(turn.steps):
                        u = t - 1
                        if turn.runs(u):
                            dve.wait_ge(h_high.sem, turn.at(h_high, u))
                            nc.vector.scalar_tensor_tensor(out=H[:, u % 2, 1, :], in0=h[:, u % 2, :], scalar=H_UP,
                                                           in1=H[:, u % 2, 0, :], op0=ALU.mult, op1=ALU.subtract
                                                           ).then_inc(h_low.sem, 1)
                        if turn.runs(t) and not second:
                            dve.wait_ge(acted.sem, turn.at(acted, t))
                            dve.wait_ge(upped.sem, turn.at(upped, t))
                            dve.wait_ge(h_high.sem, turn.at(h_high, t - 2))
                            dve.wait_ge(h_low.sem, turn.at(h_low, t - 2))
                            nc.vector.scalar_tensor_tensor(out=h[:, t % 2, :], in0=c.bank[2 + t % 2][:, :],
                                                           scalar=1 / (X_UP * W_UP), in1=act_out[:, t % 2, :],
                                                           op0=ALU.mult, op1=ALU.mult).then_inc(h_made.sem, 1)
                        e = (t - FC - 3) // FC
                        if (t - FC - 3) % FC == 0 and turn.runs(e):
                            dve.wait_ge(downed.sem, turn.at(downed, e * FC + FC - 1))
                            wait_apart(dve, added.sem, turn.at(added, e - 1), c.apart)
                            first = (turn.i if e >= 0 else turn.i - 1) * QUAD
                            for b in range(QUAD):
                                Xb = c.X[:, bass.ds(first + b, 1), :].rearrange("p b d -> p (b d)")
                                last = nc.vector.scalar_tensor_tensor(
                                    out=Xb, in0=c.bank[6 + e % 2][:, b * D:(b + 1) * D],
                                    scalar=factor[:, bass.ds(first + b, 1), e % E], in1=Xb, op0=ALU.mult, op1=ALU.add)
                            last.then_inc(added.sem, 1)
                            if e < 0:
                                wait_apart(dve, added.sem, turn.at(added, e), c.apart)
                                for b in range(QUAD):
                                    nc.vector.bn_stats(c.stats6[:, bass.ds(first + b, 1), :], c.X[:, bass.ds(first + b, 1), :])

                turns(dve, run)

            @block.tensor
            def _(pe):
                pe.sem_inc(downed.sem, downed.credit)

                def run(turn):
                    def three_passes(bank, e, at):
                        for k, (w_part, x_part) in enumerate(((0, 0), (0, 1), (1, 0))):
                            last = nc.tensor.matmul(bank[:, :], W[:, e, w_part, at:at + 128],
                                                    XT[:, x_part, bass.ds(turn.i * TOK, TOK)], start=(k == 0), stop=(k == 2))
                        return last

                    for t in range(turn.steps):
                        if turn.runs(t):
                            e, f = t // FC, t % FC
                            pe.wait_ge(acted.sem, turn.at(acted, t - 2))
                            three_passes(c.bank[t % 2], e, G_COLS + f * 128).then_inc(gated.sem, 1)
                            if not second:
                                pe.wait_ge(h_made.sem, turn.at(h_made, t - 2))
                                three_passes(c.bank[2 + t % 2], e, U_COLS + f * 128).then_inc(upped.sem, 1)
                        u = t - 2
                        if turn.runs(u):
                            e, f = u // FC, u % FC
                            pe.wait_ge(h_low.sem, turn.at(h_low, u))
                            if f == 0:
                                pe.wait_ge(added.sem, turn.at(added, e - 2))
                            for b in range(QUAD):
                                for k, (h_part, w_part) in enumerate(((0, 0), (0, 1), (1, 0))):
                                    last = nc.tensor.matmul(
                                        c.bank[6 + e % 2][:, b * D:(b + 1) * D], H[:, u % 2, h_part, b * S:(b + 1) * S],
                                        W[:, e % E, w_part, D_COLS + f * 128:D_COLS + (f + 1) * 128],
                                        start=(f == 0 and b == 0 and k == 0), stop=(f == FC - 1 and k == 2),
                                        skip_group_check=True)
                            last.then_inc(downed.sem, 1)

                turns(pe, run)


def ffn1(c):
    nc = c.nc
    RMAX = bass.bass_isa.ReduceOp.max
    CH = F1 // 128
    QMAX = 32767.0
    with ExitStack() as ctx:
        def sb(name, shape, dt=F32):
            return ctx.enter_context(nc.sbuf_tensor(f"G1_{name}", shape, dt))

        take = PartSemaphores(nc, ctx)

        def sem(name):
            return take(f"G1_{name}")

        XT = sb("XT", [D, B * S])
        xn = sb("xn", [S, QUAD, D])
        up = c.arena[:, 0:CH * B * S].rearrange("p (c t) -> p c t", c=CH)
        gate = c.wide[:, :].rearrange("p (c t) -> p c t", c=CH)
        W = c.w1_in[:, :, :]
        WQ = sb("WQ", [128, 3 * CH * 128])
        WT = sb("WT", [128, 3, CH, 128])
        block_max, block_inv = sb("block_max", [128, 36]), sb("block_inv", [128, 36])
        sig = sb("sig", [128, 2, CH, TOK])
        yT = sb("yT", [D, 2, TOK])
        tops = sb("tops", [128, 5, 2 * CH * TURNS])
        top, tops_all = sb("top", [128, 8]), sb("tops_all", [128, 8])
        scale, inv = sb("scale", [128, 8]), sb("inv", [128, 8])
        shifted, rooted = sem("shifted"), sem("rooted")
        w_quantised, w_turned, wt_made = sem("w_quantised"), sem("w_turned"), sem("wt_made")
        normed, turned = Tally(sem("normed"), QUAD), Tally(sem("turned"), 1, 2)
        xt_made = Tally(sem("xt_made"), 1, 2)
        x_topped = Tally(sem("x_topped"), 1, 2)
        top_ready, top_spread = sem("top_ready"), sem("top_spread")
        x_rounded = sem("x_rounded")
        multiplied = Tally(sem("multiplied"), 2 * CH)
        stored = Tally(sem("stored"), 2 * CH, 2 * CH)
        topped = Tally(sem("topped"), 2 * CH, 2 * CH)
        g_lifted, u_lifted = Tally(sem("g_lifted"), 1), Tally(sem("u_lifted"), 1)
        sig_lifted = Tally(sem("sig_lifted"), 1)
        product_lifted, o_lifted = sem("product_lifted"), sem("o_lifted")
        gate_rounded = Tally(sem("gate_rounded"), 1)
        up_rounded, sig_rounded = Tally(sem("up_rounded"), 1), Tally(sem("sig_rounded"), 1)
        gs_topped = Tally(sem("gs_topped"), 1)
        sig_made = Tally(sem("sig_made"), 1)
        sig_used = Tally(sem("sig_used"), 1, 2)
        o_rounded = sem("o_rounded")
        down_done, yT_made = Tally(sem("down_done"), 1), Tally(sem("yT_made"), 1, 2)
        y_turned, added = Tally(sem("y_turned"), 1, 2), Tally(sem("added"), 1, 2)
        chain_sem, scales_ready = sem("dve_chain"), sem("scales_ready")
        carried = sb("carried", [128, 4])
        block = ctx.enter_context(nc.Block())
        X0, UP, GATE, GS, O = range(5)

        @block.gpsimd
        def _(pool):
            for k in range(4):
                pool.wait_ge(top_ready, k + 1)
                at, width = ((X0, 1), (UP, 2), (GS, 1), (O, 1))[k]
                nc.gpsimd.partition_all_reduce(tops_all[:, at:at + width], top[:, at:at + width], 128, RMAX
                                               ).then_inc(top_spread, 1)

        @block.scalar
        def _(act):
            rstd_on_scalar(c, act, shifted, rooted)
            act.sem_inc(xt_made.sem, xt_made.credit)
            act.sem_inc(stored.sem, stored.credit)
            act.sem_inc(yT_made.sem, yT_made.credit)
            with act.Fori(0, TURNS // 2) as j:
                for r in range(2):
                    act.wait_ge(turned.sem, 2 * j + r + 1 + turned.credit)
                    nc.scalar.activation(XT[:, bass.ds((2 * j + r) * TOK, TOK)], c.bank[r][:, :], ACT.Copy).then_inc(xt_made.sem, 1)
            for k in range(3):
                act.wait_ge(w_turned, k + 1)
                nc.scalar.activation(WT[:, k, :, :], c.bank[2 + k][:, 0:CH * 128].rearrange("p (c o) -> p c o", c=CH), ACT.Copy
                                     ).then_inc(wt_made, 1)
            with act.Fori(0, TURNS) as i:
                for k in range(2 * CH):
                    act.wait_ge(multiplied.sem, multiplied.at(i, k))
                    dst = (up, gate)[k // CH][:, k % CH, bass.ds(i * TOK, TOK)]
                    nc.scalar.activation(dst, c.bank[2 + k][:, :], ACT.Copy).then_inc(stored.sem, 1)

            def rounding(dst, factor):
                return nc.scalar.activation(dst, dst, ACT.Copy, scale=factor, bias=ROUND)

            act.wait_ge(scales_ready, 1)

            def sigmoids(s, parity, first, second):
                if first:
                    g, u = gate[:, :, bass.ds(s * TOK, TOK)], up[:, :, bass.ds(s * TOK, TOK)]
                    rounding(g, inv[:, GATE:GATE + 1]).then_inc(g_lifted.sem, 1)
                    rounding(u, inv[:, UP:UP + 1]).then_inc(u_lifted.sem, 1)
                if second:
                    turn, sg = s - 1, sig[:, 1 - parity, :, :]
                    wait_apart(act, gate_rounded.sem, gate_rounded.at(turn, 0), c.apart)
                    wait_apart(act, sig_used.sem, sig_used.at(turn, -2), c.apart)
                    nc.scalar.activation(sg, gate[:, :, bass.ds(turn * TOK, TOK)], ACT.Sigmoid, scale=scale[:, GATE:GATE + 1]
                                         ).then_inc(sig_made.sem, 1)
                    act.wait_ge(sig_made.sem, sig_made.at(turn, 0))
                    rounding(sg, 65536.0).then_inc(sig_lifted.sem, 1)

            overlapping_turns(act, sigmoids)
            for who, ready, lifted in ((GS, 2, product_lifted), (O, 3, o_lifted)):
                act.wait_ge(scales_ready, ready)
                with act.Fori(0, TURNS) as i:
                    rounding(gate[:, :, bass.ds(i * TOK, TOK)], inv[:, who:who + 1]).then_inc(lifted, 1)
            with act.Fori(0, TURNS // 2) as j:
                for r in range(2):
                    turn = j * 2 + r
                    act.wait_ge(down_done.sem, down_done.at(turn, 0))
                    act.wait_ge(y_turned.sem, y_turned.at(turn, -2))
                    nc.scalar.activation(yT[:, r, :], c.bank[r][:, :], ACT.Copy, scale=scale[:, O:O + 1]
                                         ).then_inc(yT_made.sem, 1)

        @block.vector
        def _(dve):
            chain = Chain(dve, chain_sem)
            link = chain.link
            rstd_on_vector(c, dve, shifted, rooted)
            for t in (x_topped, topped, sig_used, added):
                dve.sem_inc(t.sem, t.credit)
            with dve.Fori(0, TURNS // 2) as j:
                for r in range(2):
                    turn = 2 * j + r
                    dve.wait_ge(turned.sem, turn + turned.credit)
                    for b in range(QUAD):
                        at = turn * QUAD + b
                        nc.vector.tensor_scalar(xn[:, b, :], c.X[:, bass.ds(at, 1), :], c.stat[:, bass.ds(at, 1), 0],
                                                c.rstd[:, bass.ds(at, 1)], ALU.subtract, ALU.mult).then_inc(normed.sem, 1)
                    dve.wait_ge(xt_made.sem, turn + 1 + xt_made.credit)
                    nc.vector.tensor_reduce(tops[:, X0, bass.ds(turn, 1)], XT[:, bass.ds(turn * TOK, TOK)], AX.X, ALU.max,
                                            apply_absolute_value=True).then_inc(x_topped.sem, 1)

            def quantise_weights():
                dve.wait_ge(c.w1_sem, 48)
                w3 = WQ[:, :].rearrange("p (b w) -> p b w", w=32)
                spread = lambda ap: ap[:, :].unsqueeze(2).broadcast_to([128, 36, 32])
                link(nc.vector.tensor_reduce(block_max[:, :], W, AX.X, ALU.max, apply_absolute_value=True))
                link(nc.vector.tensor_scalar(block_max[:, :], block_max[:, :], 1 / 7.0, 1e-12, ALU.mult, ALU.max))
                link(nc.vector.reciprocal(block_inv[:, :], block_max[:, :]))
                link(nc.vector.tensor_tensor(w3, W, spread(block_inv), ALU.mult))
                link(nc.vector.tensor_scalar(w3, w3, ROUND, ROUND + 7.0, ALU.add, ALU.min))
                link(nc.vector.tensor_scalar(w3, w3, ROUND - 8.0, ROUND, ALU.max, ALU.subtract))
                nc.vector.tensor_tensor(w3, w3, spread(block_max), ALU.mult).then_inc(w_quantised, 1)

            def find_scales(first, last, count, carried, k, meanwhile=lambda: None):
                nc.vector.reduce_max(top[:, first:last], tops[:, first:last, 0:count], AX.X).then_inc(top_ready, 1)
                meanwhile()
                dve.wait_ge(top_spread, k + 1)
                s = scale[:, first:last]
                link(nc.vector.tensor_tensor(s, tops_all[:, first:last], carried, ALU.mult))
                link(nc.vector.tensor_scalar(s, s, 1 / QMAX, 1e-12, ALU.mult, ALU.max))
                link(nc.vector.reciprocal(inv[:, first:last], s))
                link(nc.vector.tensor_tensor(inv[:, first:last], inv[:, first:last], carried, ALU.mult))

            def rounded(dst, who):
                return nc.vector.tensor_scalar(dst, dst, inv[:, who:who + 1], ROUND, ALU.mult, ALU.add)

            def settled(dst):
                return nc.vector.tensor_scalar(dst, dst, ROUND + QMAX, ROUND, ALU.min, ALU.subtract)

            link(nc.vector.memset(carried[:, :], 1.0))
            dve.wait_ge(x_topped.sem, TURNS + x_topped.credit)
            find_scales(X0, X0 + 1, TURNS, carried[:, 0:1], 0, quantise_weights)
            dve.wait_ge(xt_made.sem, TURNS + xt_made.credit)
            for i in range(TURNS):
                cols = XT[:, i * TOK:(i + 1) * TOK]
                link(rounded(cols, X0))
                settled(cols).then_inc(x_rounded, 1)
            with dve.Fori(0, TURNS) as i:
                for k in range(2 * CH):
                    dve.wait_ge(stored.sem, stored.at(i, k))
                    src = (up, gate)[k // CH][:, k % CH, bass.ds(i * TOK, TOK)]
                    nc.vector.tensor_reduce(tops[:, UP + k // CH, bass.ds(i * CH + k % CH, 1)], src, AX.X, ALU.max,
                                            apply_absolute_value=True).then_inc(topped.sem, 1)
            dve.wait_ge(topped.sem, (TURNS + 1) * 2 * CH)
            dve.wait_ge(stored.sem, (TURNS + 1) * 2 * CH)
            link(nc.vector.tensor_copy(carried[:, 0:2], scale[:, X0:X0 + 1].broadcast_to([128, 2])))
            find_scales(UP, UP + 2, TURNS * CH, carried[:, 0:2], 1)
            nc.vector.tensor_scalar(carried[:, 2:3], scale[:, GATE:GATE + 1], 1 / 65536.0, None, ALU.mult
                                    ).then_inc(scales_ready, 1)

            def sigmoids(s, parity, first, second):
                if first:
                    g, u = gate[:, :, bass.ds(s * TOK, TOK)], up[:, :, bass.ds(s * TOK, TOK)]
                    wait_apart(dve, g_lifted.sem, g_lifted.at(s, 0), c.apart)
                    settled(g).then_inc(gate_rounded.sem, 1)
                    wait_apart(dve, u_lifted.sem, u_lifted.at(s, 0), c.apart)
                    settled(u).then_inc(up_rounded.sem, 1)
                if second:
                    turn, sg = s - 1, sig[:, 1 - parity, :, :]
                    g = gate[:, :, bass.ds(turn * TOK, TOK)]
                    dve.wait_ge(sig_lifted.sem, sig_lifted.at(turn, 0))
                    nc.vector.tensor_scalar(sg, sg, ROUND + 65535.0, ROUND, ALU.min, ALU.subtract).then_inc(sig_rounded.sem, 1)
                    wait_apart(dve, sig_rounded.sem, sig_rounded.at(turn, 0), c.apart)
                    nc.vector.tensor_tensor(g, g, sg, ALU.mult).then_inc(sig_used.sem, 1)
                    wait_apart(dve, sig_used.sem, sig_used.at(turn, 0), c.apart)
                    nc.vector.tensor_reduce(tops[:, GS, bass.ds(turn, 1)], g, AX.XY, ALU.max, apply_absolute_value=True
                                            ).then_inc(gs_topped.sem, 1)

            overlapping_turns(dve, sigmoids)
            dve.wait_ge(gs_topped.sem, TURNS)
            find_scales(GS, GS + 1, TURNS, carried[:, 2:3], 2)
            nc.vector.tensor_tensor(carried[:, 3:4], scale[:, GS:GS + 1], scale[:, UP:UP + 1], ALU.mult).then_inc(scales_ready, 1)
            dve.wait_ge(scales_ready, 2)

            steps = Chain(dve, sem("product_steps"), 3)
            with dve.Fori(0, TURNS) as i:
                steps.start(i)
                g, u = gate[:, :, bass.ds(i * TOK, TOK)], up[:, :, bass.ds(i * TOK, TOK)]
                wait_apart(dve, product_lifted, i + 1, c.apart)
                steps.link(settled(g))
                steps.link(nc.vector.tensor_tensor(g, g, u, ALU.mult))
                steps.link(nc.vector.tensor_reduce(tops[:, O, bass.ds(i, 1)], g, AX.XY, ALU.max, apply_absolute_value=True))
            assert steps.n == steps.per
            find_scales(O, O + 1, TURNS, carried[:, 3:4], 3)
            dve.sem_inc(scales_ready, 1)
            with dve.Fori(0, TURNS) as i:
                wait_apart(dve, o_lifted, i + 1, c.apart)
                settled(gate[:, :, bass.ds(i * TOK, TOK)]).then_inc(o_rounded, 1)
            with dve.Fori(0, TURNS // 2) as j:
                for r in range(2):
                    turn = j * 2 + r
                    dve.wait_ge(y_turned.sem, y_turned.at(turn, 0))
                    Xt = c.X[:, bass.ds(turn * QUAD, QUAD), :]
                    nc.vector.tensor_tensor(Xt, Xt, c.bank[2 + r][:, :].rearrange("p (b d) -> p b d", b=QUAD), ALU.add
                                            ).then_inc(added.sem, 1)
                    wait_apart(dve, added.sem, added.at(turn, 0), c.apart)
                    for b in range(QUAD):
                        at = turn * QUAD + b
                        nc.vector.bn_stats(c.stats6[:, bass.ds(at, 1), :], c.X[:, bass.ds(at, 1), :])

        @block.tensor
        def _(pe):
            for t in (turned, y_turned):
                pe.sem_inc(t.sem, t.credit)
            with pe.Fori(0, TURNS // 2) as j:
                for r in range(2):
                    turn = 2 * j + r
                    pe.wait_ge(xt_made.sem, turn + 1)
                    for b in range(QUAD):
                        pe.wait_ge(normed.sem, turn * QUAD + b + 1)
                        last = nc.tensor.transpose(c.bank[r][:, b * S:(b + 1) * S], xn[:, b, :], c.w("ident"))
                    last.then_inc(turned.sem, 1)
            pe.wait_ge(w_quantised, 1)
            for k in range(3):
                for q in range(CH):
                    at = (k * CH + q) * 128
                    last = nc.tensor.transpose(c.bank[2 + k][:, q * 128:(q + 1) * 128], WQ[:, at:at + 128], c.w("ident"))
                last.then_inc(w_turned, 1)
            pe.wait_ge(wt_made, 3)
            pe.wait_ge(x_rounded, TURNS)
            with pe.Fori(0, TURNS) as i:
                for k in range(2 * CH):
                    pe.wait_ge(stored.sem, stored.at(i, k - 2 * CH))
                    nc.tensor.matmul(c.bank[2 + k][:, :], WT[:, k // CH, k % CH, :], XT[:, bass.ds(i * TOK, TOK)],
                                     start=True, stop=True).then_inc(multiplied.sem, 1)

            def down(s, parity, first, second):
                if first:
                    pe.wait_ge(o_rounded, s + 1)
                    pe.wait_ge(yT_made.sem, yT_made.at(s, -2))
                    for q in range(CH):
                        last = nc.tensor.matmul(c.bank[parity][:, :], WT[:, 2, q, :], gate[:, q, bass.ds(s * TOK, TOK)],
                                                start=(q == 0), stop=(q == CH - 1))
                    last.then_inc(down_done.sem, 1)
                if second:
                    turn, place = s - 1, 1 - parity
                    pe.wait_ge(yT_made.sem, yT_made.at(turn, 0))
                    pe.wait_ge(added.sem, added.at(turn, -2))
                    for b in range(QUAD):
                        last = nc.tensor.transpose(c.bank[2 + place][:, b * S:(b + 1) * S], yT[:, place, b * S:(b + 1) * S],
                                                   c.w("ident"))
                    last.then_inc(y_turned.sem, 1)

            overlapping_turns(pe, down)


def many_heads(c, n, own, mask):
    nc = c.nc
    NK = S if own else KEYS
    UNITS = QUAD * GROUPS
    scale = 1.0 if mask == "pairs" else DH ** -0.5
    with ExitStack() as ctx:
        def sb(name, shape, dt=F32):
            return ctx.enter_context(nc.sbuf_tensor(f"{n}_{name}", shape, dt))

        take = PartSemaphores(nc, ctx)

        def sem(name):
            return take(f"{n}_{name}")

        xn, xnT = sb("xn", [S, QUAD, D]), sb("xnT", [D, TOK])
        normed_once = sb("normed_once", [S, 2, QUAD, D]) if own else None
        rstd_twice = sb("rstd_twice", [S, B]) if own else c.rstd
        keysT = xnT if own else sb("ctxT", [D, QUAD * KEYS])
        halves = sb("halves", [D, 2, TOK], F16)
        QS, KS = sb("QS", [128, 2, GROUPS, TOK], F16), sb("KS", [128, 2, GROUPS, QUAD * NK], F16)
        V = sb("V", [NK, 2, QUAD, HEADS, 32])
        greatest, neg_max = sb("greatest", [S, 4, PER]), sb("neg_max", [S, 4, PER])
        P, PT = sb("P", [S, 2, PER * NK]), sb("PT", [NK, 2, PER * S])
        OT = sb("OT", [128, 2, GROUPS * S])
        rcp = sb("rcp", [S, 2, HEADS])
        out, outT = sb("out", [S, 2, HEADS, DH]), sb("outT", [D, 2, S])
        spread = c.w("spread").bitcast(F16).rearrange("d (w g p) -> d w g p", w=4, g=GROUPS)
        if mask:
            shut = c.wide[:, B * (D + KEYS):B * (D + KEYS) + B * KEYS // 2].bitcast(BF16)
            words = B * KEYS // (4 if mask == "pairs" else 1)
            raw_words = c.wide[:, B * D:B * D + words].bitcast(I32)
            raw = c.wide[:, B * D:B * D + words].bitcast(U8 if mask == "pairs" else I32)
        shifted, rooted = sem("shifted"), sem("rooted")
        rooted_twice = sem("rooted_twice")
        mask_in, mask_made, v_ready = sem("mask_in"), sem("mask_made"), sem("v_ready")
        X_T, QUERIES, Q_GROUP, KEYS_, K_GROUP, VALUES = 0, 1, 2, 2 + GROUPS, 3 + GROUPS, 3 + 2 * GROUPS
        ITEMS = VALUES + 1
        ctx_in = Tally(sem("ctx_in"), 16)
        normed = Tally(sem("normed"), QUAD)
        projected = Tally(sem("projected"), ITEMS, 1)
        xnT_made = Tally(sem("xnT_made"), 1)
        high_made = Tally(sem("high_made"), 2)
        low_made = Tally(sem("low_made"), 2)
        qk_made = Tally(sem("qk_made"), 2 * GROUPS)
        v_made = Tally(sem("v_made"), 1, 1)
        scored = Tally(sem("scored"), UNITS)
        maxed = Tally(sem("maxed"), UNITS)
        reduced = Tally(sem("reduced"), UNITS) if scale != 1.0 else None
        exped = Tally(sem("exped"), UNITS, 4)
        p_turned = Tally(sem("p_turned"), UNITS, 2)
        pT_made = Tally(sem("pT_made"), UNITS, 1)
        pv_done = Tally(sem("pv_done"), UNITS, 2)
        oT_made = Tally(sem("oT_made"), QUAD, 1)
        o_turned = Tally(sem("o_turned"), QUAD, 2)
        inverted = Tally(sem("inverted"), QUAD)
        out_made = Tally(sem("out_made"), QUAD)
        out_turned = Tally(sem("out_turned"), QUAD, 2)
        outT_made = Tally(sem("outT_made"), QUAD)
        o_done = Tally(sem("o_done"), QUAD, 2)
        added = Tally(sem("added"), QUAD, 1)
        block = ctx.enter_context(nc.Block())
        S_BANK, PT_BANK, OT_BANK, TAIL, PROJ = c.bank[0:4], c.bank[4], c.bank[5], c.bank[6], c.bank[7]
        STEP = {1: X_T, 3: QUERIES, 9: KEYS_, 14: VALUES}
        STEP.update({4 + g: Q_GROUP + g for g in range(GROUPS)})
        STEP.update({10 + g: K_GROUP + g for g in range(GROUPS)})

        class Slot:

            def __init__(self, s, parity, project, attend, finish):
                self.s, self.parity, self.project, self.attend, self.finish = s, parity, project, attend, finish
                self.turn = s - 1
                self.steps = UNITS if project or attend else 6

            def runs(self, k):
                return self.attend if k >= 0 else self.finish

            def at(self, tally, k):
                if k + 1 + tally.credit > 0:
                    return tally.at(self.turn, k)
                return tally.at(self.turn - 1, k + tally.per)

            def place(self, k):
                return 1 - self.parity if k >= 0 else self.parity

            def sequence(self, t, behind):
                b, rest = (t - behind) // GROUPS, (t - behind) % GROUPS
                return b if rest == 0 and self.runs(b) else None

        def slots(eng, run):
            run(Slot(0, 0, True, False, False))
            run(Slot(1, 1, True, True, False))
            with eng.Fori(0, (TURNS - 2) // 2) as j:
                run(Slot(j * 2 + 2, 0, True, True, True))
                run(Slot(j * 2 + 3, 1, True, True, True))
            run(Slot(TURNS, 0, False, True, True))
            run(Slot(TURNS + 1, 1, False, False, True))

        @block.sync
        def _(sp):
            if mask:
                sp.wait_ge(c.wide_in, 32)
                if mask == "pairs":
                    sp.dma_start(raw_words, c.ins["mask3"]).then_inc(mask_in, 16)
                else:
                    sp.dma_start(raw_words, c.ins["mask2"].partition_broadcast(S)).then_inc(mask_in, 16)
            if not own:
                with sp.Fori(0, TURNS) as i:
                    sp.wait_ge(projected.sem, projected.at(i, -1))
                    sp.dma_start(keysT[:, :], c.ins["ctxT"][:, bass.ds(i * (QUAD * KEYS), QUAD * KEYS)]
                                 ).then_inc(ctx_in.sem, 16)
            if mask == "keys":
                sp.wait_ge(c.arena_in, 16 * (3 * E))
                load_experts_of_layer2(c, sp)

        @block.gpsimd
        def _(pool):
            nc.gpsimd.memset(V[:, :, :, :, :], 0.0).then_inc(v_ready, 1)
            pool.wait_ge(v_ready, 1)
            nc.gpsimd.memset(V[:, :, :, :, DH:DH + 1], 1.0).then_inc(v_ready, 1)

        @block.scalar
        def _(act):
            rstd_on_scalar(c, act, shifted, rooted)
            if own:
                act.wait_ge(rooted_twice, 1)
                nc.scalar.activation(rstd_twice[:, :], rstd_twice[:, :], ACT.Sqrt).then_inc(rooted_twice, 1)
            for t in (exped, pT_made):
                act.sem_inc(t.sem, t.credit)

            def item_read(slot, item):
                if item == X_T:
                    act.wait_ge(projected.sem, projected.at(slot.s, X_T))
                    if own:
                        nc.scalar.activation(xnT[:, :], PROJ[:, :], ACT.Identity, scale=c.w("ln1_w"), bias=c.w("ln1_b")
                                             ).then_inc(xnT_made.sem, 1)
                    else:
                        nc.scalar.activation(xnT[:, :], PROJ[:, :], ACT.Copy).then_inc(xnT_made.sem, 1)
                if item in (QUERIES, KEYS_):
                    bias, width = ("_bq", TOK) if item == QUERIES else ("_bk", QUAD * NK)
                    act.wait_ge(projected.sem, projected.at(slot.s, item))
                    nc.scalar.activation(halves[:, 0, 0:width], PROJ[:, 0:width], ACT.Identity, bias=c.w(n + bias)
                                         ).then_inc(high_made.sem, 1)

            def run(slot):
                for t in range(slot.steps):
                    if slot.project and t - 1 in STEP:
                        item_read(slot, STEP[t - 1])
                    u = t - 1
                    if slot.runs(u):
                        act.wait_ge(maxed.sem, slot.at(maxed, u))
                        act.wait_ge(p_turned.sem, slot.at(p_turned, u - 2))
                        for g in range(GROUPS):
                            head = slice(g * NK, (g + 1) * NK)
                            last = nc.scalar.activation(P[:, u % 2, head], S_BANK[u % 4][:, head], ACT.Exp, scale=scale,
                                                        bias=neg_max[:, u % 4, g:g + 1])
                        last.then_inc(exped.sem, 1)
                    b = slot.sequence(t, 8)
                    if b is not None:
                        act.wait_ge(out_turned.sem, slot.at(out_turned, b))
                        act.wait_ge(o_done.sem, slot.at(o_done, b - 2))
                        nc.scalar.activation(outT[:, b % 2, :], TAIL[:, 0:S], ACT.Copy).then_inc(outT_made.sem, 1)
                    u = t - 2
                    if slot.runs(u):
                        act.wait_ge(p_turned.sem, slot.at(p_turned, u))
                        act.wait_ge(pv_done.sem, slot.at(pv_done, u - 2))
                        nc.scalar.activation(PT[:, u % 2, :], PT_BANK[0:NK, :], ACT.Copy).then_inc(pT_made.sem, 1)

            slots(act, run)

        @block.vector
        def _(dve):
            rstd_on_vector(c, dve, shifted, rooted)
            setup = Chain(dve, sem("setup_chain"))
            if own:
                setup.link(nc.vector.tensor_tensor(rstd_twice[:, :], c.rstd[:, :], c.rstd[:, :], ALU.mult))
                setup.link(nc.vector.tensor_tensor(rstd_twice[:, :], rstd_twice[:, :], c.stat[:, :, 1], ALU.mult))
                nc.vector.tensor_scalar(rstd_twice[:, :], rstd_twice[:, :], EPS, None, ALU.add).then_inc(rooted_twice, 1)
                dve.wait_ge(rooted_twice, 2)
                setup.link(nc.vector.reciprocal(rstd_twice[:, :], rstd_twice[:, :]))
                setup.link(nc.vector.tensor_tensor(rstd_twice[:, :], rstd_twice[:, :], c.rstd[:, :], ALU.mult))
            for t in (added, v_made, oT_made):
                dve.sem_inc(t.sem, t.credit)

            def norm(slot):
                for b in range(QUAD):
                    at = slot.s * QUAD + b
                    nc.vector.tensor_scalar(xn[:, b, :], c.X[:, bass.ds(at, 1), :], c.stat[:, bass.ds(at, 1), 0],
                                            rstd_twice[:, bass.ds(at, 1)], ALU.subtract, ALU.mult).then_inc(normed.sem, 1)

            def norm_once(slot):
                if slot.finish:
                    dve.wait_ge(added.sem, added.at(slot.turn, -1))
                for b in range(QUAD):
                    at = slot.s * QUAD + b
                    nc.vector.tensor_scalar(normed_once[:, slot.parity, b, :], c.X[:, bass.ds(at, 1), :],
                                            c.stat[:, bass.ds(at, 1), 0], c.rstd[:, bass.ds(at, 1)], ALU.subtract, ALU.mult)

            def item_read(slot, item):
                dve.wait_ge(projected.sem, projected.at(slot.s, item))
                if item in (QUERIES, KEYS_):
                    k, bias, width = (0, "_bq", TOK) if item == QUERIES else (1, "_bk", QUAD * NK)
                    dve.wait_ge(high_made.sem, high_made.at(slot.s, k))
                    nc.vector.scalar_tensor_tensor(out=halves[:, 1, 0:width], in0=PROJ[:, 0:width], scalar=c.w(n + bias),
                                                   in1=halves[:, 0, 0:width], op0=ALU.add, op1=ALU.subtract
                                                   ).then_inc(low_made.sem, 1)
                elif item == VALUES:
                    if not slot.attend:
                        dve.wait_ge(v_ready, 2)
                    for b in range(QUAD):
                        last = nc.vector.tensor_tensor(
                            V[:, slot.parity, b, :, 0:DH], PROJ[0:NK, b * D:(b + 1) * D].rearrange("k (h d) -> k h d", h=HEADS),
                            c.w(n + "_bv", NK).rearrange("k (h d) -> k h d", h=HEADS), ALU.add)
                    last.then_inc(v_made.sem, 1)
                elif item != X_T:
                    dst, g, width = (QS, item - Q_GROUP, TOK) if item < KEYS_ else (KS, item - K_GROUP, QUAD * NK)
                    nc.vector.tensor_copy(dst[:, slot.parity, g, :], PROJ[:, 0:width]).then_inc(qk_made.sem, 1)

            def run(slot):
                for t in range(slot.steps):
                    if slot.project and t - 1 in STEP and STEP[t - 1] != X_T:
                        item_read(slot, STEP[t - 1])
                    if slot.runs(t):
                        dve.wait_ge(scored.sem, slot.at(scored, t))
                        by_head = S_BANK[t % 4][:, 0:PER * NK].rearrange("q (j k) -> q j k", j=PER)
                        if reduced is None:
                            nc.vector.tensor_reduce(neg_max[:, t % 4, :], by_head, AX.X, ALU.max, negate=True).then_inc(maxed.sem, 1)
                        else:
                            nc.vector.tensor_reduce(greatest[:, t % 4, :], by_head, AX.X, ALU.max, negate=True
                                                    ).then_inc(reduced.sem, 1)
                            dve.wait_ge(reduced.sem, slot.at(reduced, t))
                            nc.vector.tensor_scalar(neg_max[:, t % 4, :], greatest[:, t % 4, :], scale, None, ALU.mult
                                                    ).then_inc(maxed.sem, 1)
                    if slot.project and t == 0:
                        norm(slot)
                    if slot.project and own and t == 6:
                        norm_once(slot)
                    b = slot.sequence(t, 6)
                    if b is not None:
                        dve.wait_ge(pv_done.sem, slot.at(pv_done, 4 * b + 3))
                        dve.wait_ge(o_turned.sem, slot.at(o_turned, b - 2))
                        nc.vector.tensor_copy(OT[:, b % 2, :], OT_BANK[:, :]).then_inc(oT_made.sem, 1)
                    b = slot.sequence(t, 7)
                    if b is not None:
                        dve.wait_ge(o_turned.sem, slot.at(o_turned, b))
                        dve.wait_ge(out_turned.sem, slot.at(out_turned, b - 2))
                        by_head = TAIL[:, :].rearrange("q (h w) -> q h w", h=HEADS)
                        nc.vector.reciprocal(rcp[:, b % 2, :], by_head[:, :, DH]).then_inc(inverted.sem, 1)
                        dve.wait_ge(inverted.sem, slot.at(inverted, b))
                        nc.vector.tensor_tensor(out[:, b % 2, :, :], by_head[:, :, 0:DH],
                                                rcp[:, b % 2, :].unsqueeze(2).broadcast_to([S, HEADS, DH]), ALU.mult
                                                ).then_inc(out_made.sem, 1)
                    b = slot.sequence(t, 9)
                    if b is not None:
                        at = (slot.turn if b >= 0 else slot.turn - 1) * QUAD + b % QUAD
                        X, result = c.X[:, bass.ds(at, 1), :], TAIL[:, S:2 * S]
                        dve.wait_ge(o_done.sem, slot.at(o_done, b))
                        if own:
                            h = c.inner[:, bass.ds(at, 1), :]
                            nc.vector.tensor_tensor(h, normed_once[:, slot.place(b), b % QUAD, :], result, ALU.add
                                                    ).then_inc(added.sem, 1)
                            wait_apart(dve, added.sem, slot.at(added, b), c.apart)
                            nc.vector.bn_stats(c.stats6[:, bass.ds(at, 1), :], h)
                            nc.vector.tensor_tensor(X, X, h, ALU.add)
                        else:
                            nc.vector.tensor_tensor(X, X, result, ALU.add).then_inc(added.sem, 1)
                            wait_apart(dve, added.sem, slot.at(added, b), c.apart)
                            nc.vector.bn_stats(c.stats6[:, bass.ds(at, 1), :], X)

            if mask:
                dve.wait_ge(mask_in, 16)
            if mask == "keys":
                nc.vector.tensor_scalar(shut[:, :], raw, 0.0, SHUT, ALU.is_equal, ALU.mult).then_inc(mask_made, 1)
            if mask == "pairs":
                nc.vector.tensor_scalar(shut[:, :], raw, SHUT, None, ALU.mult).then_inc(mask_made, 1)
            slots(dve, run)

        @block.tensor
        def _(pe):
            for t in (projected, p_turned, pv_done, o_turned, out_turned, o_done):
                pe.sem_inc(t.sem, t.credit)

            def item_made(slot, item):
                s = slot.s
                if item == X_T:
                    pe.wait_ge(v_made.sem, v_made.at(s, -1))
                    for b in range(QUAD):
                        pe.wait_ge(normed.sem, normed.at(s, b))
                        last = nc.tensor.transpose(PROJ[:, b * S:(b + 1) * S], xn[:, b, :], c.w("ident"))
                elif item in (QUERIES, KEYS_):
                    if item == QUERIES:
                        pe.wait_ge(xnT_made.sem, xnT_made.at(s, 0))
                    else:
                        pe.wait_ge(qk_made.sem, qk_made.at(s, GROUPS - 1))
                        if not own:
                            pe.wait_ge(ctx_in.sem, ctx_in.at(s, 15))
                    w, src, width = ("_wq", xnT, TOK) if item == QUERIES else ("_wk", keysT, QUAD * NK)
                    last = nc.tensor.matmul(PROJ[:, 0:width], c.w(n + w), src[:, :], start=True, stop=True)
                elif item == VALUES:
                    pe.wait_ge(qk_made.sem, qk_made.at(s, 2 * GROUPS - 1))
                    for b in range(QUAD):
                        last = nc.tensor.matmul(PROJ[0:NK, b * D:(b + 1) * D], keysT[:, b * NK:(b + 1) * NK],
                                                c.w(n + "_wv"), start=True, stop=True)
                else:
                    k, g, width = (0, item - Q_GROUP, TOK) if item < KEYS_ else (1, item - K_GROUP, QUAD * NK)
                    if g == 0:
                        pe.wait_ge(low_made.sem, low_made.at(s, k))
                    else:
                        pe.wait_ge(qk_made.sem, qk_made.at(s, k * GROUPS + g - 1))
                    for half in range(2):
                        last = nc.tensor.matmul(PROJ[:, 0:width], spread[:, 2 * k + half, g, :], halves[:, half, 0:width],
                                                start=(half == 0), stop=(half == 1))
                last.then_inc(projected.sem, 1)

            def run(slot):
                here, before = slot.place(0), slot.place(-1)
                for t in range(slot.steps):
                    if slot.runs(t):
                        b, j = t // PER, t % PER
                        rows = slice(32 * j, 32 * j + 32)
                        if t == 0:
                            pe.wait_ge(qk_made.sem, qk_made.at(slot.turn, 2 * GROUPS - 1))
                            if mask and not slot.finish:
                                pe.wait_ge(mask_made, 1)
                        pe.wait_ge(exped.sem, slot.at(exped, t - 4))
                        for g in range(GROUPS):
                            last = nc.tensor.matmul(S_BANK[t % 4][:, g * NK:(g + 1) * NK], QS[rows, here, g, b * S:(b + 1) * S],
                                                    KS[rows, here, g, b * NK:(b + 1) * NK], start=(g == 0),
                                                    stop=(not mask and g == GROUPS - 1), skip_group_check=True)
                        if mask:
                            at = (slot.turn * QUAD + b) * NK
                            last = nc.tensor.matmul(S_BANK[t % 4][:, 0:PER * NK].rearrange("q (j k) -> q j k", j=PER), c.ident16[:, :],
                                                    shut[:, bass.ds(at, NK)].unsqueeze(1).broadcast_to([S, PER, NK]),
                                                    start=False, stop=True, skip_group_check=True)
                        last.then_inc(scored.sem, 1)
                    b = slot.sequence(t, 7)
                    if b is not None:
                        pe.wait_ge(oT_made.sem, slot.at(oT_made, b))
                        pe.wait_ge(added.sem, slot.at(added, b - 1))
                        for g in range(GROUPS):
                            last = nc.tensor.transpose(TAIL[:, g * S:(g + 1) * S], OT[:, b % 2, g * S:(g + 1) * S], c.w("ident"))
                        last.then_inc(o_turned.sem, 1)
                    b = slot.sequence(t, 8)
                    if b is not None:
                        pe.wait_ge(out_made.sem, slot.at(out_made, b))
                        nc.tensor.transpose(TAIL[:, 0:S], out[:, b % 2, :, :].rearrange("q h d -> q (h d)"), c.w("ident")
                                            ).then_inc(out_turned.sem, 1)
                    b = slot.sequence(t, 9)
                    if b is not None:
                        pe.wait_ge(outT_made.sem, slot.at(outT_made, b))
                        nc.tensor.matmul(TAIL[:, S:2 * S], outT[:, b % 2, :], c.w(n + "_wo"), start=True, stop=False)
                        nc.tensor.matmul(TAIL[:, S:2 * S], c.ones_row[:, :], c.w(n + "_bo", 1), start=False, stop=True
                                         ).then_inc(o_done.sem, 1)
                    u = t - 2
                    if slot.runs(u):
                        pe.wait_ge(exped.sem, slot.at(exped, u))
                        pe.wait_ge(pT_made.sem, slot.at(pT_made, u - 1))
                        for j in range(PER):
                            last = nc.tensor.transpose(PT_BANK[0:NK, j * S:(j + 1) * S], P[:, u % 2, j * NK:(j + 1) * NK],
                                                       c.w("ident"))
                        last.then_inc(p_turned.sem, 1)
                    u = t - 3
                    if slot.runs(u):
                        b, j = u // PER, u % PER
                        pe.wait_ge(pT_made.sem, slot.at(pT_made, u))
                        if u == 0:
                            pe.wait_ge(v_made.sem, v_made.at(slot.turn, 0))
                        if j == 0:
                            pe.wait_ge(oT_made.sem, slot.at(oT_made, b - 1))
                        for g in range(GROUPS):
                            last = nc.tensor.matmul(OT_BANK[32 * g:32 * g + 32, j * S:(j + 1) * S],
                                                    V[:, slot.place(u), b % QUAD, GROUPS * j + g, :],
                                                    PT[:, u % 2, g * S:(g + 1) * S], start=True, stop=True)
                        last.then_inc(pv_done.sem, 1)
                    if slot.project and t in STEP:
                        item_made(slot, STEP[t])

            slots(pe, run)


def ffn3(c):
    nc = c.nc
    RADD = bass.bass_isa.ReduceOp.add
    BATCH = 8
    LOOPS = B // BATCH
    with ExitStack() as ctx:
        def sb(name, shape, dt=F32):
            return ctx.enter_context(nc.sbuf_tensor(f"G3_{name}", shape, dt))

        take = PartSemaphores(nc, ctx)

        def sem(name):
            return take(f"G3_{name}")

        W = c.w3_in
        W2 = c.arena[:, 0:3 * F0].rearrange("p (k f) -> p k f", k=3)
        WQ = sb("WQ", [128, 3, F0], BF16)
        WT = sb("WT", [128, 3, F0], BF16)
        sums, sums_all, mean, mean_inv = sb("sums", [128, 3]), sb("sums_all", [128, 3]), sb("mean", [128, 3]), sb("mean_inv", [128, 3])
        xn = c.wide[:, 0:B * D].rearrange("p (b d) -> p b d", b=B)
        xq, xqT = sb("xq", [S, B, D], BF16), sb("xqT", [D, B * S], BF16)
        xcol = sb("xcol", [S, 5, B])
        hcol = sb("hcol", [S, BATCH, 4])
        gate = sb("gate", [S, 2, F0])
        h, hq, hqT = sb("h", [S, 2, F0]), sb("hq", [S, 2, F0], BF16), sb("hqT", [128, 2, F0], BF16)
        shifted, rooted = sem("shifted"), sem("rooted")
        summed, summed_all, w_made, w_turned, wt_made = (sem(x) for x in ("summed", "summed_all", "w_made", "w_turned", "wt_made"))
        x_scaled, x_lifted, xq_made = sem("x_scaled"), sem("x_lifted"), sem("xq_made")
        x_turned, xqT_made = sem("x_turned"), sem("xqT_made")
        gated = Tally(sem("gated"), BATCH)
        upped = Tally(sem("upped"), BATCH)
        silued = Tally(sem("silued"), BATCH, 2)
        h_made = Tally(sem("h_made"), BATCH, 2)
        topped, sized = Tally(sem("topped"), BATCH), Tally(sem("sized"), BATCH)
        h_scaled = Tally(sem("h_scaled"), BATCH)
        down_scaled = Tally(sem("down_scaled"), BATCH)
        h_lifted = Tally(sem("h_lifted"), BATCH)
        hq_made = Tally(sem("hq_made"), BATCH, 2)
        h_turned = Tally(sem("h_turned"), BATCH, 2)
        hqT_made = Tally(sem("hqT_made"), BATCH, 2)
        down_done = Tally(sem("down_done"), BATCH, 2)
        added = Tally(sem("added"), BATCH, 8)
        written = sem("written")
        block = ctx.enter_context(nc.Block())
        TURN_BANK = (c.bank[0], c.bank[5])
        LEFT = 6

        turns = lambda eng, run: linked_turns(eng, run, LOOPS, BATCH, LEFT)

        def tile(turn, k):
            return (turn.i if k >= 0 else turn.i - 1) * BATCH + k % BATCH

        @block.sync
        def _(sp):
            with sp.Fori(0, LOOPS) as i:
                sp.wait_ge(added.sem, added.at(i, BATCH - 1))
                sp.dma_start(c.outs[0][:, bass.ds(i * BATCH, BATCH), :], c.X[:, bass.ds(i * BATCH, BATCH), :]).then_inc(written, 16)
            sp.wait_ge(written, 16 * LOOPS)

        @block.gpsimd
        def _(pool):
            pool.wait_ge(summed, 1)
            nc.gpsimd.partition_all_reduce(sums_all[:, :], sums[:, :], 128, RADD).then_inc(summed_all, 1)

        @block.scalar
        def _(act):
            rstd_on_scalar(c, act, shifted, rooted)
            for t in (silued, hqT_made):
                act.sem_inc(t.sem, t.credit)
            for q in range(LOOPS):
                act.wait_ge(x_scaled, q + 1)
                for b in range(q * BATCH, (q + 1) * BATCH):
                    last = nc.scalar.activation(xn[:, b, :], xn[:, b, :], ACT.Copy, scale=xcol[:, 2, b:b + 1], bias=ROUND)
                last.then_inc(x_lifted, 1)
                if q < 3:
                    act.wait_ge(w_turned, q + 1)
                    nc.scalar.activation(WT[:, q, :], c.bank[1 + q][:, :], ACT.Copy).then_inc(wt_made, 1)
            for q in range(B // QUAD):
                act.wait_ge(x_turned, q + 1)
                nc.scalar.activation(xqT[:, q * TOK:(q + 1) * TOK], TURN_BANK[q % 2][:, :], ACT.Copy).then_inc(xqT_made, 1)

            def run(turn):
                for t in range(turn.steps):
                    if turn.runs(t):
                        act.wait_ge(gated.sem, turn.at(gated, t))
                        wait_apart(act, h_made.sem, turn.at(h_made, t - 2), c.apart)
                        nc.scalar.activation(gate[:, t % 2, :], c.bank[1 + t % 2][:, :], ACT.Silu,
                                             scale=xcol[:, 3, bass.ds(tile(turn, t), 1)]).then_inc(silued.sem, 1)
                    b = t - 2
                    if turn.runs(b):
                        act.wait_ge(h_scaled.sem, turn.at(h_scaled, b))
                        nc.scalar.activation(h[:, b % 2, :], h[:, b % 2, :], ACT.Copy, scale=hcol[:, b % BATCH, 2:3], bias=ROUND
                                             ).then_inc(h_lifted.sem, 1)
                    b = t - 3
                    if turn.runs(b):
                        act.wait_ge(h_turned.sem, turn.at(h_turned, b))
                        act.wait_ge(down_done.sem, turn.at(down_done, b - 2))
                        nc.scalar.activation(hqT[:, b % 2, :], TURN_BANK[b % 2][:, :], ACT.Copy).then_inc(hqT_made.sem, 1)

            turns(act, run)

        @block.vector
        def _(dve):
            setup = Chain(dve, sem("setup_chain"))
            link = setup.link
            dve.wait_ge(c.w3_sem, 48)
            nc.vector.tensor_reduce(sums[:, :], W[:, :, :], AX.X, ALU.add, apply_absolute_value=True).then_inc(summed, 1)
            rstd_on_vector(c, dve, shifted, rooted)
            dve.wait_ge(summed_all, 1)
            link(nc.vector.tensor_scalar(mean[:, :], sums_all[:, :], 1.0 / (D * F0), 1e-5, ALU.mult, ALU.max))
            link(nc.vector.reciprocal(mean_inv[:, :], mean[:, :]))
            for k in range(3):
                last = nc.vector.tensor_scalar(W2[:, k, :], W[:, k, :], mean_inv[:, k:k + 1], ROUND, ALU.mult, ALU.add)
            link(last)
            link(nc.vector.tensor_scalar(W2[:, :, :], W2[:, :, :], ROUND - 1.0, ROUND + 1.0, ALU.max, ALU.min))
            nc.vector.tensor_scalar(WQ[:, :, :], W2[:, :, :], ROUND, None, ALU.subtract).then_inc(w_made, 1)
            for t in (h_made, hq_made, added):
                dve.sem_inc(t.sem, t.credit)
            for q in range(LOOPS + 1):
                if q < LOOPS:
                    batch = slice(q * BATCH, (q + 1) * BATCH)
                    top, size, inverse, by_gate, by_up = (xcol[:, k, batch] for k in range(5))
                    for b in range(q * BATCH, (q + 1) * BATCH):
                        last = nc.vector.tensor_scalar(xn[:, b, :], c.X[:, b, :], c.stat[:, b, 0:1], c.rstd[:, b:b + 1],
                                                       ALU.subtract, ALU.mult)
                    link(last)
                    link(nc.vector.tensor_reduce(top, xn[:, batch, :], AX.X, ALU.max, apply_absolute_value=True))
                    link(nc.vector.tensor_scalar(size, top, 1e-5, 1 / 127.0, ALU.max, ALU.mult))
                    nc.vector.reciprocal(inverse, size).then_inc(x_scaled, 1)
                    nc.vector.tensor_scalar(by_gate, size, mean[:, 0:1], None, ALU.mult)
                    link(nc.vector.tensor_scalar(by_up, size, mean[:, 1:2], None, ALU.mult))
                if q >= 1:
                    batch = slice((q - 1) * BATCH, q * BATCH)
                    dve.wait_ge(x_lifted, q)
                    nc.vector.tensor_scalar(xq[:, batch, :], xn[:, batch, :], ROUND + 127.0, ROUND, ALU.min, ALU.subtract
                                            ).then_inc(xq_made, 1)

            def run(turn):
                for t in range(turn.steps):
                    b = t - 1
                    if turn.runs(b):
                        r, col = b % 2, hcol[:, b % BATCH, :]
                        dve.wait_ge(silued.sem, turn.at(silued, b))
                        dve.wait_ge(hq_made.sem, turn.at(hq_made, b - 2))
                        wait_apart(dve, upped.sem, turn.at(upped, b), c.apart)
                        nc.vector.scalar_tensor_tensor(out=h[:, r, :], in0=c.bank[3 + r][:, :],
                                                       scalar=xcol[:, 4, bass.ds(tile(turn, b), 1)],
                                                       in1=gate[:, r, :], op0=ALU.mult, op1=ALU.mult).then_inc(h_made.sem, 1)
                        dve.wait_ge(h_made.sem, turn.at(h_made, b))
                        nc.vector.tensor_reduce(col[:, 0:1], h[:, r, :], AX.X, ALU.max, apply_absolute_value=True
                                                ).then_inc(topped.sem, 1)
                        dve.wait_ge(topped.sem, turn.at(topped, b))
                        nc.vector.tensor_scalar(col[:, 1:2], col[:, 0:1], 1e-5, 1 / 127.0, ALU.max, ALU.mult).then_inc(sized.sem, 1)
                        dve.wait_ge(sized.sem, turn.at(sized, b))
                        nc.vector.reciprocal(col[:, 2:3], col[:, 1:2]).then_inc(h_scaled.sem, 1)
                        nc.vector.tensor_scalar(col[:, 3:4], mean[:, 2:3], col[:, 1:2], None, ALU.mult).then_inc(down_scaled.sem, 1)
                    b = t - 2
                    if turn.runs(b):
                        dve.wait_ge(h_lifted.sem, turn.at(h_lifted, b))
                        dve.wait_ge(h_turned.sem, turn.at(h_turned, b - 2))
                        nc.vector.tensor_scalar(hq[:, b % 2, :], h[:, b % 2, :], ROUND + 127.0, ROUND, ALU.min, ALU.subtract
                                                ).then_inc(hq_made.sem, 1)
                    b = t - 5
                    if turn.runs(b):
                        X = c.X[:, bass.ds(tile(turn, b), 1), :]
                        dve.wait_ge(down_scaled.sem, turn.at(down_scaled, b))
                        wait_apart(dve, down_done.sem, turn.at(down_done, b), c.apart)
                        nc.vector.scalar_tensor_tensor(out=X, in0=c.bank[6 + b % 2][:, 0:D], scalar=hcol[:, b % BATCH, 3:4],
                                                       in1=X, op0=ALU.mult, op1=ALU.add).then_inc(added.sem, 1)

            turns(dve, run)

        @block.tensor
        def _(pe):
            for t in (h_turned, down_done):
                pe.sem_inc(t.sem, t.credit)
            pe.wait_ge(w_made, 1)
            for k in range(3):
                for q in range(FC):
                    last = nc.tensor.matmul(c.bank[1 + k][:, q * 128:(q + 1) * 128], WQ[:, k, q * 128:(q + 1) * 128],
                                            c.ident16[:, :], start=True, stop=True)
                last.then_inc(w_turned, 1)
            for q in range(B // QUAD):
                pe.wait_ge(xq_made, q // 2 + 1)
                if q >= 2:
                    pe.wait_ge(xqT_made, q - 1)
                for b in range(QUAD):
                    last = nc.tensor.matmul(TURN_BANK[q % 2][:, b * S:(b + 1) * S], xq[:, q * QUAD + b, :], c.ident16[:, :],
                                            start=True, stop=True)
                last.then_inc(x_turned, 1)
            pe.wait_ge(wt_made, 3)
            pe.wait_ge(xqT_made, B // QUAD)

            def run(turn):
                for t in range(turn.steps):
                    if turn.runs(t):
                        xT = xqT[:, bass.ds(tile(turn, t) * S, S)]
                        wait_apart(pe, silued.sem, turn.at(silued, t - 2), c.apart)
                        nc.tensor.matmul(c.bank[1 + t % 2][:, :], xT, WT[:, 0, :], start=True, stop=True).then_inc(gated.sem, 1)
                        wait_apart(pe, h_made.sem, turn.at(h_made, t - 2), c.apart)
                        nc.tensor.matmul(c.bank[3 + t % 2][:, :], xT, WT[:, 1, :], start=True, stop=True).then_inc(upped.sem, 1)
                    b = t - 3
                    if turn.runs(b):
                        pe.wait_ge(hq_made.sem, turn.at(hq_made, b))
                        pe.wait_ge(hqT_made.sem, turn.at(hqT_made, b - 2))
                        for q in range(FC):
                            last = nc.tensor.matmul(TURN_BANK[b % 2][:, q * S:(q + 1) * S], hq[:, b % 2, q * 128:(q + 1) * 128],
                                                    c.ident16[:, :], start=True, stop=True)
                        last.then_inc(h_turned.sem, 1)
                    b = t - 4
                    if turn.runs(b):
                        pe.wait_ge(hqT_made.sem, turn.at(hqT_made, b))
                        pe.wait_ge(added.sem, turn.at(added, b - 2))
                        for q in range(FC):
                            last = nc.tensor.matmul(c.bank[6 + b % 2][:, 0:D], hqT[:, b % 2, q * S:(q + 1) * S],
                                                    WT[:, 2, q * 128:(q + 1) * 128], start=(q == 0), stop=(q == FC - 1))
                        last.then_inc(down_done.sem, 1)

            turns(pe, run)


def program(nc, ins, outs):
    with ExitStack() as ctx:
        c = Core(nc, ctx, ins, outs)
        opening(c)
        one_head(c, "L0", False, D ** -0.5)
        experts(c, "E0", False)
        one_head(c, "L1", True, 1.0)
        ffn1(c)
        many_heads(c, "X2", False, "keys")
        many_heads(c, "F2", True, None)
        experts(c, "E2", True)
        many_heads(c, "X3", False, "pairs")
        ffn3(c)


def laid_out(inputs):
    a = {k: np.asarray(v) for k, v in inputs.items()}
    small = np.zeros((128, SMALL_WIDTH), np.float32)

    def put(name, rows, value):
        at, width = SMALL[name]
        small[0:rows, at:at + width] = np.broadcast_to(value, (rows, width))

    put("ident", 128, np.eye(128, dtype=np.float32))
    p = np.arange(128)
    product = p % 32 // DH
    spread = np.zeros((128, 4, GROUPS, 128), np.float16)
    for which, stands in enumerate((product < 2, product >= 2, product % 2 == 0, product % 2 == 1)):
        for g in range(GROUPS):
            spread[(p // 32 * GROUPS + g) * DH + p % DH, which, g, p] = stands
    put("spread", 128, spread.reshape(128, -1).view(np.float32))
    put("expert_rank", 128, np.arange(E, 0, -1, dtype=np.float32)[None, :])
    for x in ("q", "k", "v", "o"):
        put(f"L0_w{x}", 128, a[f"L0_xattn_W{x}"].T)
    put("L0_bo", 128, a["L0_xattn_bo"][None, :])
    put("L0_bv", 128, a["L0_xattn_bv"][None, :])
    put("L0_bq", 128, a["L0_xattn_bq"][:, None])
    put("L1_wk", 128, a["L1_xattn_W_k"].T)
    put("L1_wo", 128, a["L1_xattn_W_o"].T)
    put("L1_bo", 128, a["L1_xattn_b_o"][None, :])
    put("L1_bk", 128, a["L1_xattn_b_k"][:, None])
    wqkv, bqkv = a["L2_ffn_w_qkv"], a["L2_ffn_b_qkv"]
    for l, wq, wk, wv, wo, bq, bk, bv, bo in (
        ("X2", a["L2_xattn_Wq"].T, a["L2_xattn_Wk"].T, a["L2_xattn_Wv"].T, a["L2_xattn_Wo"].T,
         a["L2_xattn_bq"], a["L2_xattn_bk"], a["L2_xattn_bv"], a["L2_xattn_bo"]),
        ("F2", wqkv[:, 0:128], wqkv[:, 128:256], wqkv[:, 256:384], a["L2_ffn_w_o"],
         bqkv[0:128], bqkv[128:256], bqkv[256:384], a["L2_ffn_b_o"]),
        ("X3", a["L3_xattn_wq_w"].T, a["L3_xattn_wk_w"].T, a["L3_xattn_wv_w"].T, a["L3_xattn_wo_w"].T,
         a["L3_xattn_wq_b"], a["L3_xattn_wk_b"], a["L3_xattn_wv_b"], a["L3_xattn_wo_b"]),
    ):
        put(l + "_wq", 128, wq)
        put(l + "_wk", 128, wk)
        put(l + "_wv", 128, wv)
        put(l + "_wo", 128, wo)
        put(l + "_bv", 128, bv[None, :])
        put(l + "_bo", 128, bo[None, :])
        put(l + "_bq", 128, bq[:, None])
        put(l + "_bk", 128, bk[:, None])
    put("router", 128, np.concatenate([a["L0_ffn_w_router"], a["L0_ffn_w_gating"]], axis=1))
    put("gate2", 128, a["L2_ffn_w_gate"])
    for x in ("ln1_w", "ln1_b", "ln2_w", "ln2_b"):
        put(x, 128, a["L2_ffn_" + x][:, None])
    put("b1", 128, a["L2_ffn_b1"].reshape(E * FC, 128).T)
    put("b2", E, a["L2_ffn_b2"])
    out = {
        "x": a["x"].transpose(1, 0, 2),
        "small": small,
        "ctxT": a["ctx_1024"].transpose(2, 0, 1).reshape(D, B * KEYS),
        "ctx": a["ctx_1024"].transpose(1, 0, 2),
        "cell_mask": a["mask_BxSxS2_ff1"].transpose(1, 0, 2).reshape(S, B * KEYS),
        "seq_mask": a["mask_BxS2_ff1"].reshape(1, B * KEYS),
        "mask2": a["mask_BxS2_ik0"].reshape(1, B * KEYS),
        "mask3": a["mask_Bx1xSxS2_bk1"].reshape(B, S, KEYS).transpose(1, 0, 2).reshape(S, B * KEYS),
    }
    for x in ("L0_ffn_w_gate", "L0_ffn_w_up", "L0_ffn_w_down", "L1_ffn_w_gate", "L1_ffn_w_up", "L1_ffn_w_down",
              "L2_ffn_w1", "L2_ffn_w2", "L3_ffn_w_gate", "L3_ffn_w_up", "L3_ffn_w_down"):
        out[x] = a[x]
    out = {k: np.ascontiguousarray(v) for k, v in out.items()}
    out["mask3"] = out["mask3"].view(np.int32)
    return out


def kernel(**inputs):
    import concourse.bacc as bacc
    from concourse.bass_utils import run_bass_kernel_spmd

    nc = bacc.Bacc("TRN2", target_bir_lowering=False, num_devices=1)
    arrays = laid_out(inputs)
    ins = {k: nc.dram_tensor(f"in_{k}", v.shape, mybir.dt.from_np(v.dtype), kind="ExternalInput").ap()
           for k, v in arrays.items()}
    out = nc.dram_tensor("out_0", (S, B, D), F32, kind="ExternalOutput").ap()
    program(nc, ins, [out])
    r = run_bass_kernel_spmd(nc, [{f"in_{k}": v for k, v in arrays.items()}], core_ids=[0])
    return np.ascontiguousarray(r.results[0]["out_0"].transpose(1, 0, 2))
```
